# Optimizing a Trainium2 kernel written in Bass

```python
import numpy as np
import jax
import jax.numpy as jnp

def _softmax(x, axis=-1):
    return jax.nn.softmax(x, axis=axis)

def _gelu(x):
    return jax.nn.gelu(x, approximate=True)

def _silu(x):
    return jax.nn.silu(x)

def _sigmoid(x):
    return jax.nn.sigmoid(x)

def _layernorm(x, axis=-1, eps=1e-05):
    m = jnp.mean(x, axis=axis, keepdims=True)
    v = jnp.var(x, axis=axis, keepdims=True)
    return (x - m) / jnp.sqrt(v + eps)

def _scatter_add(tgt, idx, src, axis=0):
    return tgt.at[idx].add(src)

def _segment_sum(src, seg, n):
    return jax.ops.segment_sum(src, seg, n)
kernel_name = 'mk_recurrent_d1_jaxref_r4_50f541'

def setup_inputs(seed: int=0):
    np.random.seed(seed)
    _w = jnp.asarray

    def _L0_attn_setup():
        import jax, jax.numpy as jnp
        import numpy as np
        H = 1024
        D_IN = 2048
        N = 16
        K = 4
        R = 64
        EPS = 1e-06

        def rms_forward(x, eps=EPS):
            xf = x.astype(jnp.float32)
            var = jnp.mean(xf * xf, axis=-1, keepdims=True)
            return (xf * jax.lax.rsqrt(var + eps)).astype(x.dtype)
        key = jax.random.key(seed)
        ks = jax.random.split(key, 10)
        s = 0.02
        hidden_states = jax.random.normal(ks[0], (2, 256, H), dtype=jnp.float32)
        W_in = jax.random.normal(ks[1], (2 * D_IN, H), dtype=jnp.float32) * s
        conv_w = jax.random.normal(ks[2], (D_IN, K), dtype=jnp.float32) * 0.2
        conv_b = jax.random.normal(ks[3], (D_IN,), dtype=jnp.float32) * 0.02
        W_x = jax.random.normal(ks[4], (R + 2 * N, D_IN), dtype=jnp.float32) * s
        W_dt = jax.random.normal(ks[5], (D_IN, R), dtype=jnp.float32) * s
        b_dt = jax.random.normal(ks[6], (D_IN,), dtype=jnp.float32) * 0.02
        A_log = jnp.log(jnp.broadcast_to(jnp.arange(1, N + 1, dtype=jnp.float32)[None, :], (D_IN, N)))
        D = jnp.ones((D_IN,), dtype=jnp.float32)
        W_out = jax.random.normal(ks[7], (H, D_IN), dtype=jnp.float32) * s
        return {'hidden_states': hidden_states, 'W_in': W_in, 'conv_w': conv_w, 'conv_b': conv_b, 'W_x': W_x, 'W_dt': W_dt, 'b_dt': b_dt, 'A_log': A_log, 'D': D, 'W_out': W_out}
    _L0_attn_in = _L0_attn_setup()

    def _L0_ffn_setup():
        import jax, jax.numpy as jnp
        import numpy as np
        H = 1024
        I = 2752
        R = 32
        NLEV = 16
        Q_ZERO = 7.5
        Q_STEP = 0.005
        LR_SCALE = 0.02

        def _qlinear(x, q, scale, A, Bm):
            w = (q.astype(jnp.float32) - Q_ZERO) * (scale * Q_STEP)[:, None]
            y = jnp.einsum('bsh,oh->bso', x, w)
            return y + LR_SCALE * (x @ A @ Bm)
        key = jax.random.key(seed)
        ks = jax.random.split(key, 13)
        B, S = (2, 512)
        inp = {'x': jax.random.normal(ks[0], (B, S, H), jnp.float32), 'gate_q': jax.random.randint(ks[1], (I, H), 0, NLEV, jnp.int32), 'gate_scale': jax.random.uniform(ks[2], (I,), jnp.float32), 'gate_A': jax.random.normal(ks[3], (H, R), jnp.float32), 'gate_B': jax.random.normal(ks[4], (R, I), jnp.float32), 'up_q': jax.random.randint(ks[5], (I, H), 0, NLEV, jnp.int32), 'up_scale': jax.random.uniform(ks[6], (I,), jnp.float32), 'up_A': jax.random.normal(ks[7], (H, R), jnp.float32), 'up_B': jax.random.normal(ks[8], (R, I), jnp.float32), 'down_q': jax.random.randint(ks[9], (H, I), 0, NLEV, jnp.int32), 'down_scale': jax.random.uniform(ks[10], (H,), jnp.float32), 'down_A': jax.random.normal(ks[11], (I, R), jnp.float32), 'down_B': jax.random.normal(ks[12], (R, H), jnp.float32)}
        return inp
    _L0_ffn_in = _L0_ffn_setup()
    _d = {'L0_attn_hidden_states': _L0_attn_in['hidden_states'], 'L0_attn_W_in': _L0_attn_in['W_in'], 'L0_attn_conv_w': _L0_attn_in['conv_w'], 'L0_attn_conv_b': _L0_attn_in['conv_b'], 'L0_attn_W_x': _L0_attn_in['W_x'], 'L0_attn_W_dt': _L0_attn_in['W_dt'], 'L0_attn_b_dt': _L0_attn_in['b_dt'], 'L0_attn_A_log': _L0_attn_in['A_log'], 'L0_attn_D': _L0_attn_in['D'], 'L0_attn_W_out': _L0_attn_in['W_out'], 'L0_ffn_gate_q': _L0_ffn_in['gate_q'], 'L0_ffn_gate_scale': _L0_ffn_in['gate_scale'], 'L0_ffn_gate_A': _L0_ffn_in['gate_A'], 'L0_ffn_gate_B': _L0_ffn_in['gate_B'], 'L0_ffn_up_q': _L0_ffn_in['up_q'], 'L0_ffn_up_scale': _L0_ffn_in['up_scale'], 'L0_ffn_up_A': _L0_ffn_in['up_A'], 'L0_ffn_up_B': _L0_ffn_in['up_B'], 'L0_ffn_down_q': _L0_ffn_in['down_q'], 'L0_ffn_down_scale': _L0_ffn_in['down_scale'], 'L0_ffn_down_A': _L0_ffn_in['down_A'], 'L0_ffn_down_B': _L0_ffn_in['down_B']}
    _x0 = _d['L0_attn_hidden_states']
    _d['L0_attn_hidden_states'] = jax.random.normal(jax.random.fold_in(jax.random.key(seed), 1), (1, 2048, 1024), dtype=_x0.dtype)
    del _x0
    return _d

def reference(L0_attn_hidden_states, L0_attn_W_in, L0_attn_conv_w, L0_attn_conv_b, L0_attn_W_x, L0_attn_W_dt, L0_attn_b_dt, L0_attn_A_log, L0_attn_D, L0_attn_W_out, L0_ffn_gate_q, L0_ffn_gate_scale, L0_ffn_gate_A, L0_ffn_gate_B, L0_ffn_up_q, L0_ffn_up_scale, L0_ffn_up_A, L0_ffn_up_B, L0_ffn_down_q, L0_ffn_down_scale, L0_ffn_down_A, L0_ffn_down_B):

    def _L0_attn_ref(hidden_states, W_in, conv_w, conv_b, W_x, W_dt, b_dt, A_log, D, W_out):
        import jax, jax.numpy as jnp
        import numpy as np
        H = 1024
        D_IN = 2048
        N = 16
        K = 4
        R = 64
        EPS = 1e-06

        def rms_forward(x, eps=EPS):
            xf = x.astype(jnp.float32)
            var = jnp.mean(xf * xf, axis=-1, keepdims=True)
            return (xf * jax.lax.rsqrt(var + eps)).astype(x.dtype)
        b, L, _ = hidden_states.shape
        proj = hidden_states @ W_in.T
        x, gate = (proj[..., :D_IN], proj[..., D_IN:])
        xpad = jnp.pad(x, ((0, 0), (K - 1, 0), (0, 0)))
        xc = conv_b
        for j in range(K):
            xc = xc + conv_w[:, j] * xpad[:, j:j + L, :]
        x = jax.nn.silu(xc)
        ssm = x @ W_x.T
        ts, Bm, Cm = (ssm[..., :R], ssm[..., R:R + N], ssm[..., R + N:])
        ts = rms_forward(ts)
        Bm = rms_forward(Bm)
        Cm = rms_forward(Cm)
        dt = jax.nn.softplus(ts @ W_dt.T + b_dt)
        A = -jnp.exp(A_log.astype(jnp.float32))

        def step(state, inp):
            dt_t, B_t, C_t, u_t = inp
            dA = jnp.exp(dt_t[..., None] * A)
            state = state * dA + (dt_t * u_t)[..., None] * B_t[:, None, :]
            y = jnp.einsum('bdn,bn->bd', state, C_t)
            return (state, y)
        init = jnp.zeros((b, D_IN, N), dtype=jnp.float32)
        xs = (dt.transpose(1, 0, 2), Bm.transpose(1, 0, 2), Cm.transpose(1, 0, 2), x.transpose(1, 0, 2))
        _, ys = jax.lax.scan(step, init, xs)
        y = ys.transpose(1, 0, 2) + x * D
        y = y * jax.nn.silu(gate)
        return y @ W_out.T

    def _L0_ffn_ref(x, gate_q, gate_scale, gate_A, gate_B, up_q, up_scale, up_A, up_B, down_q, down_scale, down_A, down_B):
        import jax, jax.numpy as jnp
        import numpy as np
        H = 1024
        I = 2752
        R = 32
        NLEV = 16
        Q_ZERO = 7.5
        Q_STEP = 0.005
        LR_SCALE = 0.02

        def _qlinear(x, q, scale, A, Bm):
            w = (q.astype(jnp.float32) - Q_ZERO) * (scale * Q_STEP)[:, None]
            y = jnp.einsum('bsh,oh->bso', x, w)
            return y + LR_SCALE * (x @ A @ Bm)
        g = _qlinear(x, gate_q, gate_scale, gate_A, gate_B)
        u = _qlinear(x, up_q, up_scale, up_A, up_B)
        h = jax.nn.silu(g) * u
        return _qlinear(h, down_q, down_scale, down_A, down_B)
    x = L0_attn_hidden_states
    xn = _layernorm(x, axis=-1)
    s = _L0_attn_ref(xn, L0_attn_W_in, L0_attn_conv_w, L0_attn_conv_b, L0_attn_W_x, L0_attn_W_dt, L0_attn_b_dt, L0_attn_A_log, L0_attn_D, L0_attn_W_out)
    g = _silu(_L0_ffn_ref(xn, L0_ffn_gate_q, L0_ffn_gate_scale, L0_ffn_gate_A, L0_ffn_gate_B, L0_ffn_up_q, L0_ffn_up_scale, L0_ffn_up_A, L0_ffn_up_B, L0_ffn_down_q, L0_ffn_down_scale, L0_ffn_down_A, L0_ffn_down_B))
    x = x + s * g
    return x

_drawn_inputs = setup_inputs


def setup_inputs(seed=0):
    import zlib

    import numpy as np

    out = dict(_drawn_inputs(seed))
    spreads = {'L0_attn_D': (1.0, 0.2)}
    factors = {'L0_attn_b_dt': 4.275}
    for name, (base, spread) in spreads.items():
        noise = np.random.default_rng([zlib.crc32(name.encode()), seed]).standard_normal(out[name].shape)
        drawn = base * np.exp(spread * noise) if base else spread * noise
        out[name] = jnp.asarray(drawn.astype(out[name].dtype))
    for name, factor in factors.items():
        out[name] = (out[name] * factor).astype(out[name].dtype)
    return out
```

```python
from contextlib import ExitStack

import concourse.bass as bass
from concourse import mybir

F32 = mybir.dt.float32
F16 = mybir.dt.float16
I32 = mybir.dt.int32
ALU = mybir.AluOpType
ACT = mybir.ActivationFunctionType
AX = mybir.AxisListType

P = 128
L, H, DI, N, R, K, I, LR = 2048, 1024, 2048, 16, 64, 4, 2752, 32
T = 512
C = L // T
TT = L // P
TPC = T // P
HK = H // P
DT = DI // P
J = 4
G = DT // J
IT = -(-I // P)
IPAD = IT * P
S3 = R + 2 * N
WS = 256.0
Q_ZERO, Q_STEP, LR_SCALE = 7.5, 0.005, 0.02
UNITS = C
LEAD = 1
SEMAPHORES = (
    "n_x0 n_x1 i_w0 i_w1 i_st0 i_st1 g_w0 g_w1 g_wd0 g_wd1 g_sg0 g_sg1 g_sd0 g_sd1 g_u0 g_u1 o_r0 o_r1 "
    "o_q0 o_q1 n_const n_dve n_xn n_tp n_hi n_lo n_a n_var n_sd n_beat i_const i_z i_hi i_lo i_mm i_ev "
    "i_cv i_e i_u i_ssm i_sm i_half r_a r_b r_v r_sm r_tp r_tb r_st r_ah r_al r_xa r_xh r_xl r_bh r_bl "
    "r_sd g_const g_hi g_lo g_mm g_ev g_e g_g g_pre g_mx g_ab g_sp g_dt g_du s_const s_gsc s_bb s_dt s_du "
    "s_us s_gs s_ys s_dec s_inj s_scan s_carry s_turn s_sum s_zero s_yt s_yev s_gate s_parts s_wq0 s_wq1 "
    "s_conv s_mm s_lrt s_gl s_ul s_ex s_sg s_h s_hi s_lo s_hs s_beat o_c o_ds o_hi o_lo o_dw o_dah o_dal "
    "o_dbh o_dbl o_h o_y o_x o_ha o_hah o_hal o_pl o_pd o_po o_l o_f o_e o_out o_st "
).split()
EXTRA = 8


def mixer_kernel(nc, x, win, convw, convb, wx, wdt, bdt, alog, dskip, wout, gu_q, g_scale, u_scale,
                 lr_a, g_b, u_b, dq, d_scale, d_a, d_b, ident_in, out,
                 u_s, gs_s, dt_s, du_s, bt_s, h_s, y_s):
    whole = ExitStack()
    with whole:
        def sb(stack, name, shape, dt=F32):
            return stack.enter_context(nc.sbuf_tensor(name, shape, dt))

        def pb(stack, name, shape, dt=F32):
            return stack.enter_context(nc.psum_tensor(name, shape, dt))

        semaphores = {name: whole.enter_context(nc.semaphore(name)) for name in SEMAPHORES}
        sem = semaphores.__getitem__

        def start_semaphores(eng, share):
            for name in SEMAPHORES[share::4]:
                eng.sem_inc(semaphores[name], LEAD)

        with nc.Block() as block:
            @block.gpsimd
            def _(pool):
                start_semaphores(pool, 0)

            @block.scalar
            def _(act):
                start_semaphores(act, 1)

            @block.vector
            def _(v):
                start_semaphores(v, 2)

            @block.sync
            def _(sp):
                start_semaphores(sp, 3)

        ident = sb(whole, "ident", [P, P])
        aneg = sb(whole, "aneg", [P, DT, N])
        cT = sb(whole, "cT", [P, TT, N])
        dsk = sb(whole, "dsk", [P, DT])
        upto_scan = whole.enter_context(ExitStack())
        xhi = sb(upto_scan, "xhi", [P, HK, L], F16)
        xlo = sb(upto_scan, "xlo", [P, HK, L], F16)
        xa = sb(upto_scan, "xa", [3 * LR, 2, L], F16)
        btab = sb(upto_scan, "btab", [3 * LR, 2, IPAD], F16)

        with ExitStack() as st:
            xt = sb(st, "xt", [P, 2, H])
            xn = sb(st, "xn", [P, 2, H])
            stats = sb(st, "stats", [P, 2, 2, 6])
            mv = sb(st, "mv", [P, 2, 2])
            var = sb(st, "var", [P, 2, 1])
            rstd = sb(st, "rstd", [P, 2, 1])
            al = sb(st, "al", [P, DT, N])
            xtp = [pb(st, f"xtp{b}", [P, HK, P]) for b in range(2)]
            n_x = [sem(f"n_x{b}") for b in range(2)]
            n_const, n_dve, n_xn, n_tp, n_hi, n_lo, n_a, n_var, n_sd, n_beat = (
                sem(s) for s in ("n_const", "n_dve", "n_xn", "n_tp", "n_hi", "n_lo", "n_a", "n_var", "n_sd", "n_beat"))
            with nc.Block() as block:

                @block.sync
                def _(sp):
                    sp.dma_start(ident[:, :], ident_in).then_inc(n_const, 16)
                    sp.dma_start(al[:, :, :], alog).then_inc(n_const, 16)
                    sp.dma_start(dsk[:, :], dskip).then_inc(n_const, 16)
                    with sp.Fori(0, TT // 2) as i:
                        for b in range(2):
                            sp.wait_ge(n_xn, LEAD + i * 2 + b)
                            sp.dma_start(xt[:, b, :], x[i * 2 + b]).then_inc(n_x[b], 16)

                @block.vector
                def _(v):
                    with v.Fori(0, TT // 2) as i:
                        for b in range(2):
                            v.wait_ge(n_x[b], LEAD + i * 16 + 16)
                            for h in range(2):
                                v.bn_stats(stats[:, b, h, :], xt[:, b, h * 512:(h + 1) * 512]).then_inc(n_dve, 1)
                            v.wait_ge(n_dve, LEAD + i * 8 + b * 4 + 2)
                            v.sem_inc(n_beat, 1)
                            v.bn_aggr(mv[:, b, :], stats[:, b, :, :].rearrange("p a s -> p (a s)")).then_inc(n_dve, 1)
                            v.wait_ge(n_dve, LEAD + i * 8 + b * 4 + 3)
                            v.tensor_scalar(var[:, b, :], mv[:, b, 1:2], 1e-5, None, ALU.add).then_inc(n_var, 1)
                            v.wait_ge(n_sd, LEAD + i * 2 + b + 1)
                            v.reciprocal(rstd[:, b, :], var[:, b, :]).then_inc(n_dve, 1)
                            v.wait_ge(n_dve, LEAD + i * 8 + b * 4 + 4)
                            v.wait_ge(n_tp, LEAD + i * 2 + b)
                            v.tensor_scalar(xn[:, b, :], xt[:, b, :], mv[:, b, 0:1], rstd[:, b, :],
                                            ALU.subtract, ALU.mult).then_inc(n_xn, 1)
                        for b in range(2):
                            v.wait_ge(n_hi, LEAD + i * 2 + b + 1)
                            tok = bass.ds((i * 2 + b) * P, P)
                            v.tensor_tensor(xlo[:, :, tok], xtp[b][:, :, :], xhi[:, :, tok],
                                            ALU.subtract).then_inc(n_lo, 1)

                @block.tensor
                def _(pe):
                    pe.wait_ge(n_const, LEAD + 48)
                    with pe.Fori(0, TT // 2) as i:
                        for b in range(2):
                            pe.wait_ge(n_xn, LEAD + i * 2 + b + 1)
                            pe.wait_ge(n_lo, LEAD + i * 2 + b)
                            for k in range(HK):
                                mm = pe.transpose(xtp[b][:, k, :], xn[:, b, k * P:(k + 1) * P], ident[:, :])
                            mm.then_inc(n_tp, 1)

                @block.scalar
                def _(act):
                    act.wait_ge(n_const, LEAD + 48)
                    act.activation(al[:, :, :], al[:, :, :], ACT.Exp).then_inc(n_a, 1)
                    act.wait_ge(n_a, LEAD + 1)
                    act.mul(aneg[:, :, :], al[:, :, :], -1.0).then_inc(n_a, 1)
                    with act.Fori(0, TT // 2) as i:
                        for b in range(2):
                            act.wait_ge(n_var, LEAD + i * 2 + b + 1)
                            act.activation(var[:, b, :], var[:, b, :], ACT.Sqrt).then_inc(n_sd, 1)
                        for b in range(2):
                            act.wait_ge(n_tp, LEAD + i * 2 + b + 1)
                            act.activation(xhi[:, :, bass.ds((i * 2 + b) * P, P)], xtp[b][:, :, :],
                                           ACT.Copy).then_inc(n_hi, 1)

        proj = ExitStack()
        with proj:
            wraw = sb(proj, "wraw", [P, 2, HK * P])
            whi = sb(proj, "whi", [P, 2, HK * P], F16)
            wlo = sb(proj, "wlo", [P, 2, HK * P], F16)
            xp = sb(proj, "xp", [P, 2, L + K - 1])
            eb = sb(proj, "eb", [P, L])
            sm = sb(proj, "sm", [P, TT, S3])
            main = [pb(proj, f"main{t}", [P, T]) for t in range(C)]
            four = pb(proj, "four", [P, C, T])

            with ExitStack() as st:
                xc = sb(st, "xc", [P, 2, L])
                ub = sb(st, "ub", [P, 2, L])
                zero = sb(st, "zero", [P, T])
                wx_sb = sb(st, "wx_sb", [P, DT, S3])
                cw = sb(st, "cw", [P, DT, K])
                cb = sb(st, "cb", [P, DT])
                i_w = [sem(f"i_w{b}") for b in range(2)]
                (i_const, i_z, i_hi, i_lo, i_mm, i_ev, i_cv, i_e, i_u, i_ssm, i_sm, i_half) = (
                    sem(s) for s in ("i_const", "i_z", "i_hi", "i_lo", "i_mm", "i_ev", "i_cv",
                                     "i_e", "i_u", "i_ssm", "i_sm", "i_half"))
                i_st = [sem(f"i_st{b}") for b in range(2)]
                with nc.Block() as block:

                    @block.sync
                    def _(sp):
                        sp.dma_start(wraw[:, 0, :], win[0]).then_inc(i_w[0], 16)
                        for dst, src in ((wx_sb, wx), (cw, convw), (cb, convb)):
                            sp.dma_start(dst[:], src).then_inc(i_const, 16)
                        with sp.Fori(0, DT // 2) as i:
                            for b in range(2):
                                w = i * 2 + b
                                sp.wait_ge(i_lo, LEAD + w)
                                nb = 1 - b
                                sp.dma_start(wraw[:, nb, :], win[w + 1]).then_inc(i_w[nb], 16)
                                sp.wait_ge(i_u, LEAD + w + 1)
                                sp.dma_start(u_s[i // 2, :, :, (i % 2) * 2 + b, :].rearrange("c p t -> p c t"),
                                             ub[:, b, :].rearrange("p (c t) -> p c t", c=C)).then_inc(i_st[b], 16)
                        for b in range(2):
                            sp.wait_ge(i_st[b], LEAD + 16 * (DT // 2))

                    @block.scalar
                    def _(act):
                        act.wait_ge(i_w[0], LEAD + 16)
                        act.activation(whi[:, 0, :], wraw[:, 0, :], ACT.Copy, scale=WS).then_inc(i_hi, 1)
                        act.wait_ge(i_z, LEAD + 3)
                        with act.Fori(0, DT // 2) as i:
                            for b in range(2):
                                w = i * 2 + b
                                nb = 1 - b
                                act.wait_ge(i_w[nb], LEAD + i * 16 + 16 * (1 + b))
                                act.wait_ge(i_mm, LEAD + w * C)
                                act.activation(whi[:, nb, :], wraw[:, nb, :], ACT.Copy, scale=WS).then_inc(i_hi, 1)
                                for c in range(C):
                                    act.wait_ge(i_mm, LEAD + w * C + c + 1)
                                    if c == 0:
                                        act.wait_ge(i_cv, LEAD + w * 4)
                                    act.activation(xp[:, b, K - 1 + c * T:K - 1 + (c + 1) * T], main[c][:, :],
                                                   ACT.Copy, scale=1.0 / WS).then_inc(i_ev, 1)
                                act.wait_ge(i_cv, LEAD + w * 4 + 4)
                                act.wait_ge(i_u, LEAD + w)
                                act.activation(eb[:, :], xc[:, b, :], ACT.Tanh).then_inc(i_e, 1)

                    @block.vector
                    def _(v):
                        v.memset(zero[:, :], 0.0).then_inc(i_z, 1)
                        for b in range(2):
                            v.memset(xp[:, b, 0:K - 1], 0.0).then_inc(i_z, 1)
                        v.wait_ge(i_hi, LEAD + 1)
                        v.scalar_tensor_tensor(wlo[:, 0, :], wraw[:, 0, :], WS, whi[:, 0, :],
                                               ALU.mult, ALU.subtract).then_inc(i_lo, 1)
                        v.wait_ge(i_const, LEAD + 48)
                        v.tensor_scalar(cw[:, :, :], cw[:, :, :], 0.5, None, ALU.mult).then_inc(i_half, 1)
                        v.tensor_scalar(cb[:, :], cb[:, :], 0.5, None, ALU.mult).then_inc(i_half, 1)
                        v.wait_ge(i_half, LEAD + 2)
                        with v.Fori(0, DT // 2) as i:
                            for b in range(2):
                                w = i * 2 + b
                                nb = 1 - b
                                v.wait_ge(i_hi, LEAD + w + 2)
                                v.scalar_tensor_tensor(wlo[:, nb, :], wraw[:, nb, :], WS, whi[:, nb, :],
                                                       ALU.mult, ALU.subtract).then_inc(i_lo, 1)
                                v.wait_ge(i_ev, LEAD + w * C + C)
                                v.wait_ge(i_e, LEAD + w)
                                v.tensor_scalar(xc[:, b, :], xp[:, b, 0:L], cw[:, w, 0:1], cb[:, bass.ds(w, 1)],
                                                ALU.mult, ALU.add).then_inc(i_cv, 1)
                                for j in range(1, K):
                                    v.wait_ge(i_cv, LEAD + w * 4 + j)
                                    v.scalar_tensor_tensor(xc[:, b, :], xp[:, b, j:j + L], cw[:, w, j:j + 1],
                                                           xc[:, b, :], ALU.mult, ALU.add).then_inc(i_cv, 1)
                                v.wait_ge(i_e, LEAD + w + 1)
                                v.wait_ge(i_st[b], LEAD + i * 16)
                                v.wait_ge(i_ssm, LEAD + w)
                                v.scalar_tensor_tensor(ub[:, b, :], eb[:, :], 1.0, xc[:, b, :],
                                                       ALU.add, ALU.mult).then_inc(i_u, 1)
                        v.wait_ge(i_ssm, LEAD + DT + 1)
                        v.tensor_copy(sm[:, :, :].rearrange("p (a t) s -> p a (t s)", a=C),
                                      four[:, :, 0:TPC * S3]).then_inc(i_sm, 1)

                    @block.tensor
                    def _(pe):
                        def w_x(b, w):
                            pe.wait_ge(i_u, LEAD + w + 1)
                            for t in range(TT):
                                mm = pe.matmul(four[:, t // TPC, (t % TPC) * S3:(t % TPC + 1) * S3],
                                               ub[:, b, t * P:(t + 1) * P], wx_sb[:, w, :],
                                               start=False, stop=False, skip_group_check=True)
                            mm.then_inc(i_ssm, 1)

                        def tile(b, w):
                            pe.wait_ge(i_lo, LEAD + w + 1)
                            for c in range(C):
                                if not isinstance(w, int):
                                    pe.wait_ge(i_ev, LEAD + (w - 1) * C + c + 1)
                                elif w > 0:
                                    pe.wait_ge(i_ev, LEAD + (w - 1) * C + c + 1)
                                for k in range(HK):
                                    hi = whi[:, b, k * P:(k + 1) * P]
                                    lo = wlo[:, b, k * P:(k + 1) * P]
                                    xh = xhi[:, k, c * T:(c + 1) * T]
                                    xl = xlo[:, k, c * T:(c + 1) * T]
                                    pe.matmul(main[c][:, :], hi, xh, start=(k == 0), stop=False)
                                    pe.matmul(main[c][:, :], hi, xl, start=False, stop=False)
                                    mm = pe.matmul(main[c][:, :], lo, xh, start=False, stop=(k == HK - 1))
                                mm.then_inc(i_mm, 1)

                        pe.wait_ge(i_z, LEAD + 1)
                        for c in range(C):
                            mm = pe.matmul(four[:, c, :], zero[:, 0:P], zero[:, :], start=True, stop=False,
                                           skip_group_check=True)
                        mm.then_inc(i_ssm, 1)
                        pe.wait_ge(i_const, LEAD + 48)
                        tile(0, 0)
                        tile(1, 1)
                        w_x(0, 0)
                        with pe.Fori(1, DT // 2) as i:
                            for b in range(2):
                                tile(b, i * 2 + b)
                                w_x(1 - b, i * 2 + b - 1)
                        w_x(1, DT - 1)

            tsb = sb(proj, "tsb", [R + N, L])
            with ExitStack() as st:
                sq = sb(st, "sq", [P, TT, S3])
                ms = sb(st, "ms", [P, 3, TT])
                araw = sb(st, "araw", [P, 2, HK, 3 * LR])
                ahi = sb(st, "ahi", [P, 2, HK, 3 * LR], F16)
                alo = sb(st, "alo", [P, 2, HK, 3 * LR], F16)
                braw = sb(st, "braw", [3 * LR, IPAD])
                (r_a, r_b, r_v, r_sm, r_tp, r_tb, r_st, r_ah, r_al, r_xa, r_xh, r_xl, r_bh, r_bl, r_sd) = (
                    sem(s) for s in ("r_a", "r_b", "r_v", "r_sm", "r_tp", "r_tb", "r_st", "r_ah", "r_al",
                                     "r_xa", "r_xh", "r_xl", "r_bh", "r_bl", "r_sd"))
                groups = ((0, R), (R, N), (R + N, N))
                with nc.Block() as block:

                    @block.sync
                    def _(sp):
                        for m in range(2):
                            for r in range(3):
                                sp.dma_start(araw[:, m, :, r * LR:(r + 1) * LR], lr_a[m]).then_inc(r_a, 16)
                        for m, src in enumerate((g_b, u_b)):
                            if m:
                                sp.wait_ge(r_bl, LEAD + 1)
                            for r in range(3):
                                sp.dma_start(braw[r * LR:(r + 1) * LR, :], src).then_inc(r_b, 16)
                        sp.wait_ge(r_tb, LEAD + C)
                        sp.dma_start(bt_s, tsb[R:R + N, :]).then_inc(r_st, 16)
                        sp.wait_ge(r_st, LEAD + 16)

                    @block.vector
                    def _(v):
                        v.tensor_tensor(sq[:, :, :], sm[:, :, :], sm[:, :, :], ALU.mult).then_inc(r_v, 1)
                        v.wait_ge(r_v, LEAD + 1)
                        for g, (o, n) in enumerate(groups):
                            v.reduce_sum(ms[:, g, :], sq[:, :, o:o + n], axis=AX.X).then_inc(r_v, 1)
                        v.wait_ge(r_v, LEAD + 4)
                        for g, (o, n) in enumerate(groups):
                            v.tensor_scalar(ms[:, g, :], ms[:, g, :], 1.0 / n, 1e-6, ALU.mult, ALU.add
                                            ).then_inc(r_v, 1)
                        v.wait_ge(r_v, LEAD + 7)
                        v.wait_ge(r_sd, LEAD + 1)
                        v.reciprocal(ms[:, :, :], ms[:, :, :]).then_inc(r_v, 1)
                        v.wait_ge(r_v, LEAD + 8)
                        for g, (o, n) in enumerate(groups):
                            dst = cT[:, :, :] if g == 2 else sm[:, :, o:o + n]
                            v.tensor_tensor(dst, sm[:, :, o:o + n],
                                            ms[:, g, :].unsqueeze(2).broadcast_to([P, TT, n]), ALU.mult
                                            ).then_inc(r_sm, 1)
                        v.wait_ge(r_ah, LEAD + 1)
                        v.tensor_tensor(alo[:, :, :, :].rearrange("p a b c -> p (a b c)"),
                                        araw[:, :, :, :].rearrange("p a b c -> p (a b c)"),
                                        ahi[:, :, :, :].rearrange("p a b c -> p (a b c)"),
                                        ALU.subtract).then_inc(r_al, 1)
                        for m in range(2):
                            v.wait_ge(r_bh, LEAD + m + 1)
                            v.scalar_tensor_tensor(btab[2 * LR:3 * LR, m, :], braw[2 * LR:3 * LR, :], WS,
                                                   btab[2 * LR:3 * LR, m, :], ALU.mult, ALU.subtract
                                                   ).then_inc(r_bl, 1)
                        for q in range(2 * C):
                            m, c = divmod(q, C)
                            v.wait_ge(r_xh, LEAD + q + 1)
                            dst = xa[LR:2 * LR, m, c * T:(c + 1) * T]
                            v.tensor_tensor(dst, main[q % 4][LR:2 * LR, :], dst, ALU.subtract).then_inc(r_xl, 1)

                    @block.scalar
                    def _(act):
                        act.wait_ge(r_v, LEAD + 7)
                        act.activation(ms[:, :, :], ms[:, :, :], ACT.Sqrt).then_inc(r_sd, 1)
                        act.wait_ge(r_a, LEAD + 96)
                        act.activation(ahi[:, :, :, :].rearrange("p a b c -> p (a b c)"),
                                       araw[:, :, :, :].rearrange("p a b c -> p (a b c)"),
                                       ACT.Copy).then_inc(r_ah, 1)
                        for m in range(2):
                            act.wait_ge(r_b, LEAD + 48 * (m + 1))
                            act.activation(btab[:, m, :], braw[:, :], ACT.Copy, scale=WS).then_inc(r_bh, 1)
                        for c in range(C):
                            act.wait_ge(r_tp, LEAD + c + 1)
                            act.activation(tsb[:, c * T:(c + 1) * T], four[0:R + N, c, :], ACT.Copy
                                           ).then_inc(r_tb, 1)
                        for q in range(2 * C):
                            m, c = divmod(q, C)
                            act.wait_ge(r_xa, LEAD + q + 1)
                            act.activation(xa[:, m, c * T:(c + 1) * T], main[q % 4][0:3 * LR, :], ACT.Copy
                                           ).then_inc(r_xh, 1)

                    @block.tensor
                    def _(pe):
                        pe.wait_ge(r_sm, LEAD + 2)
                        for c in range(C):
                            for t in range(TPC):
                                mm = pe.transpose(four[0:R + N, c, t * P:(t + 1) * P],
                                                  sm[:, c * TPC + t, 0:R + N], ident[:, :])
                            mm.then_inc(r_tp, 1)
                        pe.wait_ge(r_al, LEAD + 1)
                        for q in range(2 * C):
                            m, c = divmod(q, C)
                            if q >= 4:
                                pe.wait_ge(r_xl, LEAD + q - 3)
                            for k in range(HK):
                                for a, xx, z in ((ahi, xhi, 0), (ahi, xlo, 1), (alo, xhi, 2)):
                                    mm = pe.matmul(main[q % 4][0:3 * LR, :], a[:, m, k, :],
                                                   xx[:, k, c * T:(c + 1) * T],
                                                   start=(k == 0 and z == 0), stop=(k == HK - 1 and z == 2))
                            mm.then_inc(r_xa, 1)

            with ExitStack() as st:
                wd = sb(st, "wd", [R, 2, P])
                bd = sb(st, "bd", [P, DT])
                gsb = sb(st, "gsb", [P, 2, L])
                mx = sb(st, "mx", [P, 2, L])
                ab = sb(st, "ab", [P, L])
                du = sb(st, "du", [P, 2, L])
                g_w = [sem(f"g_w{b}") for b in range(2)]
                g_wd = [sem(f"g_wd{b}") for b in range(2)]
                g_sg = [sem(f"g_sg{b}") for b in range(2)]
                g_sd = [sem(f"g_sd{b}") for b in range(2)]
                g_u = [sem(f"g_u{b}") for b in range(2)]
                (g_const, g_hi, g_lo, g_mm, g_ev, g_e, g_g, g_pre, g_mx, g_ab, g_sp, g_dt, g_du) = (
                    sem(s) for s in ("g_const", "g_hi", "g_lo", "g_mm", "g_ev", "g_e", "g_g", "g_pre",
                                     "g_mx", "g_ab", "g_sp", "g_dt", "g_du"))
                with nc.Block() as block:
                    def store(dram, i, b, tile):
                        return (dram[i // 2, :, :, (i % 2) * 2 + b, :].rearrange("c p t -> p c t"),
                                tile.rearrange("p (c t) -> p c t", c=C))

                    @block.sync
                    def _(sp):
                        sp.dma_start(bd[:, :], bdt).then_inc(g_const, 16)
                        with sp.Fori(0, DT // 2) as i:
                            for b in range(2):
                                w = i * 2 + b
                                sp.wait_ge(g_mx, LEAD + w)
                                sp.dma_start(wd[:, b, :], wdt[w]).then_inc(g_wd[b], 16)
                                sp.wait_ge(g_lo, LEAD + w)
                                sp.dma_start(wraw[:, b, :], win[w + DT]).then_inc(g_w[b], 16)
                                sp.wait_ge(g_sd[b], LEAD + i * 32)
                                dst, src = du[:, b, :].rearrange("p (c t) -> p c t", c=C), \
                                    u_s[i // 2, :, :, (i % 2) * 2 + b, :].rearrange("c p t -> p c t")
                                sp.dma_start(dst, src).then_inc(g_u[b], 16)
                                sp.wait_ge(g_du, LEAD + w + 1)
                                sp.dma_start(*store(dt_s, i, b, mx[:, b, :])).then_inc(g_sd[b], 16)
                                sp.dma_start(*store(du_s, i, b, du[:, b, :])).then_inc(g_sd[b], 16)
                        for b in range(2):
                            sp.wait_ge(g_sd[b], LEAD + 32 * (DT // 2))

                    @block.scalar
                    def _(act):
                        act.wait_ge(g_const, LEAD + 16)
                        with act.Fori(0, DT // 2) as i:
                            for b in range(2):
                                w = i * 2 + b
                                act.wait_ge(g_w[b], LEAD + i * 16 + 16)
                                act.wait_ge(g_ev, LEAD + w * C)
                                act.activation(whi[:, b, :], wraw[:, b, :], ACT.Copy, scale=WS).then_inc(g_hi, 1)
                                act.wait_ge(g_pre, LEAD + w + 1)
                                act.wait_ge(g_dt, LEAD + w)
                                act.activation(ab[:, :], four[:, :, :].rearrange("p c t -> p (c t)"), ACT.Abs,
                                               bias=bd[:, bass.ds(w, 1)]).then_inc(g_ab, 1)
                                act.wait_ge(g_ab, LEAD + w * 2 + 1)
                                act.activation(ab[:, :], ab[:, :], ACT.Exp, scale=-1.0).then_inc(g_ab, 1)
                                act.wait_ge(g_ab, LEAD + w * 2 + 2)
                                act.activation(ab[:, :], ab[:, :], ACT.Ln, bias=1.0).then_inc(g_sp, 1)
                                for c in range(C):
                                    act.wait_ge(g_mm, LEAD + w * C + c + 1)
                                    if c == 0:
                                        act.wait_ge(g_g, LEAD + w)
                                    act.activation(xp[:, b, c * T:(c + 1) * T], main[c][:, :],
                                                   ACT.Copy, scale=0.5 / WS).then_inc(g_ev, 1)
                                act.wait_ge(g_ev, LEAD + w * C + C)
                                act.activation(eb[:, :], xp[:, b, 0:L], ACT.Tanh).then_inc(g_e, 1)
                                act.wait_ge(g_g, LEAD + w + 1)
                                act.dma_start(*store(gs_s, i, b, gsb[:, b, :])).then_inc(g_sg[b], 16)
                        for b in range(2):
                            act.wait_ge(g_sg[b], LEAD + 16 * (DT // 2))

                    @block.vector
                    def _(v):
                        v.wait_ge(g_const, LEAD + 16)
                        with v.Fori(0, DT // 2) as i:
                            for b in range(2):
                                w = i * 2 + b
                                v.wait_ge(g_hi, LEAD + w + 1)
                                v.scalar_tensor_tensor(wlo[:, b, :], wraw[:, b, :], WS, whi[:, b, :],
                                                       ALU.mult, ALU.subtract).then_inc(g_lo, 1)
                                v.wait_ge(g_pre, LEAD + w + 1)
                                v.wait_ge(g_sd[b], LEAD + i * 32)
                                v.wait_ge(g_ab, LEAD + w * 2 + 1)
                                v.wait_ge(g_du, LEAD + w)
                                v.tensor_scalar(mx[:, b, :], four[:, :, :].rearrange("p c t -> p (c t)"),
                                                bd[:, bass.ds(w, 1)], 0.0, ALU.add, ALU.max).then_inc(g_mx, 1)
                                v.wait_ge(g_sp, LEAD + w + 1)
                                v.wait_ge(g_mx, LEAD + w + 1)
                                v.tensor_tensor(mx[:, b, :], mx[:, b, :], ab[:, :], ALU.add).then_inc(g_dt, 1)
                                v.wait_ge(g_e, LEAD + w + 1)
                                v.wait_ge(g_sg[b], LEAD + i * 16)
                                v.scalar_tensor_tensor(gsb[:, b, :], eb[:, :], 1.0, xp[:, b, 0:L],
                                                       ALU.add, ALU.mult).then_inc(g_g, 1)

                    @block.gpsimd
                    def _(pool):
                        with pool.Fori(0, DT // 2) as i:
                            for b in range(2):
                                w = i * 2 + b
                                pool.wait_ge(g_dt, LEAD + w + 1)
                                pool.wait_ge(g_u[b], LEAD + i * 16 + 16)
                                pool.tensor_tensor(du[:, b, :], mx[:, b, :], du[:, b, :], ALU.mult
                                                   ).then_inc(g_du, 1)

                    @block.tensor
                    def _(pe):
                        with pe.Fori(0, DT // 2) as i:
                            for b in range(2):
                                w = i * 2 + b
                                pe.wait_ge(g_wd[b], LEAD + i * 16 + 16)
                                pe.wait_ge(g_mx, LEAD + w)
                                for c in range(C):
                                    mm = pe.matmul(four[:, c, :], wd[:, b, :], tsb[0:R, c * T:(c + 1) * T],
                                                   start=True, stop=True)
                                mm.then_inc(g_pre, 1)
                                pe.wait_ge(g_lo, LEAD + w + 1)
                                for c in range(C):
                                    if b == 0:
                                        pe.wait_ge(g_ev, LEAD + w * C)
                                    else:
                                        pe.wait_ge(g_ev, LEAD + (w - 1) * C + c + 1)
                                    for k in range(HK):
                                        hi = whi[:, b, k * P:(k + 1) * P]
                                        lo = wlo[:, b, k * P:(k + 1) * P]
                                        xh = xhi[:, k, c * T:(c + 1) * T]
                                        xl = xlo[:, k, c * T:(c + 1) * T]
                                        pe.matmul(main[c][:, :], hi, xh, start=(k == 0), stop=False)
                                        pe.matmul(main[c][:, :], hi, xl, start=False, stop=False)
                                        mm = pe.matmul(main[c][:, :], lo, xh, start=False, stop=(k == HK - 1))
                                    mm.then_inc(g_mm, 1)

        with ExitStack() as st:
            bb = sb(st, "bb", [P, N, T])
            dtb = sb(st, "dtb", [P, J, T])
            dub = sb(st, "dub", [P, J, T])
            inj = sb(st, "inj", [P, 2, J, T])
            state = sb(st, "state", [P, J, T])
            ysum = sb(st, "ysum", [P, TPC, T])
            us = sb(st, "us", [P, J * T])
            gs = sb(st, "gs", [P, J * T])
            carry = sb(st, "carry", [P, DT, N])
            gsc = sb(st, "gsc", [P, 2, IT])
            wq = sb(st, "wq", [P, 2, 512], I32)
            w16 = sb(st, "w16", [P, 2, 2 * HK * P], F16)
            lrt = sb(st, "lrt", [P, T])
            gl = sb(st, "gl", [P, T])
            ul = sb(st, "ul", [P, T])
            ex = sb(st, "ex", [P, T])
            hh = sb(st, "hh", [P, 2, T], F16)
            decay = [pb(st, f"decay{b}", [P, T]) for b in range(2)]
            turned = [pb(st, f"turned{b}", [P, T]) for b in range(2)]
            bank = [pb(st, f"bank{m}", [P, T]) for m in range(2)]
            lrb = pb(st, "lrb", [P, T])
            us16 = us[:, :].bitcast(F16)

            (s_const, s_gsc, s_bb, s_dt, s_du, s_us, s_gs, s_ys, s_dec, s_inj, s_scan, s_carry, s_turn, s_sum,
             s_zero, s_yt, s_yev, s_gate, s_parts, s_wq0, s_wq1, s_conv, s_mm, s_lrt, s_gl, s_ul, s_ex, s_sg,
             s_h, s_hi, s_lo, s_hs, s_beat) = (sem("s_" + s) for s in (
                "const gsc bb dt du us gs ys dec inj scan carry turn sum zero yt yev gate parts wq0 wq1 conv "
                "mm lrt gl ul ex sg h hi lo hs beat").split())
            s_wq = [s_wq0, s_wq1]
            FF_STEPS = IT // 2

            def run_steps(eng, step_fn):
                with eng.Fori(0, 2) as c:
                    step_fn(eng, c, None, True, "chunk")
                    with eng.Fori(0, G) as g:
                        step_fn(eng, c, g, True, "step")
                step_fn(eng, 2, None, True, "chunk")
                with eng.Fori(0, G - 1) as g:
                    step_fn(eng, 2, g, True, "step")
                step_fn(eng, 2, G - 1, False, "step")
                step_fn(eng, 3, None, False, "chunk")
                with eng.Fori(0, G) as g:
                    step_fn(eng, 3, g, False, "step")

            def run_pairs(eng, step, ff, pair_fn):
                if ff:
                    with eng.Fori(0, 2) as half:
                        with eng.Fori(0, UNITS) as p:
                            pair_fn(step, half * UNITS + p, step * 2 + half, p)
                else:
                    with eng.Fori(0, N // 2) as p:
                        pair_fn(step, p, None, None)

            with nc.Block() as block:
                @block.sync
                def _(sp):
                    for m, src in enumerate((g_scale, u_scale)):
                        sp.dma_start(gsc[:, m, :], src).then_inc(s_const, 16)
                    for k in range(UNITS):
                        if k >= 2:
                            sp.wait_ge(s_conv, LEAD + k - 1)
                        sp.dma_start(wq[:, k % 2, :], gu_q[0, :, k * 512:(k + 1) * 512]).then_inc(s_wq[k % 2], 16)

                    def step_fn(eng, c, g, ff, what):
                        if what == "chunk":
                            eng.wait_ge(s_inj, LEAD + c * (G * N))
                            eng.dma_start(bb[:, :, :], bt_s[:, bass.ts(c, T)].partition_broadcast(P)
                                          ).then_inc(s_bb, 16)
                            return
                        step = c * G + g
                        eng.wait_ge(s_dec, LEAD + step * (N * J))
                        eng.dma_start(dtb[:, :, :], dt_s[g, c]).then_inc(s_dt, 16)
                        eng.wait_ge(s_inj, LEAD + step * N)
                        eng.dma_start(dub[:, :, :], du_s[g, c]).then_inc(s_du, 16)
                        eng.wait_ge(s_ys, LEAD + step * 16)
                        eng.dma_start(us[:, :], u_s[g, c]).then_inc(s_us, 16)
                        eng.dma_start(gs[:, :], gs_s[g, c]).then_inc(s_gs, 16)

                        def pair(step, pair_no, i, p):
                            if i is None:
                                return
                            k = i * UNITS + p
                            eng.wait_ge(s_conv, LEAD + k + UNITS)
                            eng.dma_start(wq[:, p % 2, :], gu_q[i + 1, :, bass.ts(p, 512)]).then_inc(s_wq0, 16)
                            eng.wait_ge(s_lo, LEAD + k + 1)
                            eng.dma_start(h_s[p, :, i], hh[:, :, :]).then_inc(s_hs, 16)

                        if ff:
                            run_pairs(eng, step, ff, pair)
                        eng.wait_ge(s_parts, LEAD + step * 2 + 2)
                        eng.dma_start(y_s[c, :, :, bass.ts(g, J), :],
                                      us16.rearrange("p (a j t) -> p a j t", a=2, j=J)).then_inc(s_ys, 16)

                    run_steps(sp, step_fn)
                    sp.wait_ge(s_ys, LEAD + 16 * C * G)
                    sp.wait_ge(s_hs, LEAD + 16 * IT * UNITS)

                @block.scalar
                def _(act):
                    act.wait_ge(s_const, LEAD + 32)
                    for m, half in enumerate((0.5, 1.0)):
                        act.activation(gsc[:, m, :], gsc[:, m, :], ACT.Copy, scale=half * Q_STEP).then_inc(s_gsc, 1)
                    for k in range(UNITS):
                        act.wait_ge(s_wq[k % 2], LEAD + 16 * (k // 2 + 1))
                        act.activation(w16[:, 0, k * 512:(k + 1) * 512], wq[:, k % 2, :], ACT.Copy,
                                       bias=-Q_ZERO).then_inc(s_conv, 1)

                    def step_fn(eng, c, g, ff, what):
                        if what == "chunk":
                            return
                        step = c * G + g
                        eng.wait_ge(s_dt, LEAD + step * 16 + 16)

                        def pair(step, pr, i, p):
                            for q in range(2):
                                slot = step * N + pr * 2 + q
                                for j in range(J):
                                    eng.wait_ge(s_scan, LEAD + slot * J + j + EXTRA - 1)
                                    eng.activation(decay[j % 2][:, :], dtb[:, j, :], ACT.Exp,
                                                   scale=aneg[:, g * J + j, bass.ds(pr * 2 + q, 1)]
                                                   ).then_inc(s_dec, 1)
                                    if i is not None and q == 1 and j == 1:
                                        k = i * UNITS + p
                                        eng.wait_ge(s_gl, LEAD + k + 1)
                                        eng.wait_ge(s_sg, LEAD + k)
                                        eng.activation(ex[:, :], gl[:, :], ACT.Tanh).then_inc(s_ex, 1)
                                if i is not None:
                                    k = i * UNITS + p
                                    eng.wait_ge(s_mm, LEAD + k * 2 + q + 1)
                                    eng.wait_ge((s_ul, s_gl)[q], LEAD + k + q)
                                    eng.activation(lrt[:, :], lrb[:, :], ACT.Copy,
                                                   scale=(0.5, 1.0)[q] * LR_SCALE / WS).then_inc(s_lrt, 1)
                                eng.wait_ge(s_scan, LEAD + slot * J + J + EXTRA)
                                eng.activation(carry[:, bass.ds(g * J, J), bass.ds(pr * 2 + q, 1)],
                                               state[:, :, T - 1:T], ACT.Copy).then_inc(s_carry, 1)
                            if i is not None:
                                k = i * UNITS + p
                                eng.wait_ge(s_wq0, LEAD + k * 16 + 48)
                                eng.wait_ge(s_mm, LEAD + i * (2 * UNITS))
                                eng.activation(w16[:, (i + 1) % 2, bass.ts(p, 512)], wq[:, p % 2, :], ACT.Copy,
                                               bias=-Q_ZERO).then_inc(s_conv, 1)

                        run_pairs(eng, step, ff, pair)

                    run_steps(act, step_fn)

                @block.vector
                def _(v):
                    v.memset(carry[:, :, :], 0.0).then_inc(s_carry, 1)
                    v.sem_inc(s_scan, EXTRA)
                    v.sem_inc(s_sum, J)
                    v.sem_inc(s_yev, 2)
                    v.wait_ge(s_gsc, LEAD + 2)
                    v.wait_ge(s_carry, LEAD + 1)

                    def step_fn(eng, c, g, ff, what):
                        if what == "chunk":
                            return
                        step = c * G + g

                        def pair(step, pr, i, p):
                            for q in range(2):
                                slot = step * N + pr * 2 + q
                                n = bass.ds(pr * 2 + q, 1)
                                eng.wait_ge(s_inj, LEAD + slot + 1)
                                eng.wait_ge(s_carry, LEAD + slot + 1)
                                eng.wait_ge(s_turn, LEAD + slot * TPC)
                                for j in range(J):
                                    eng.wait_ge(s_dec, LEAD + slot * J + j + 1)
                                    eng.tensor_tensor_scan(state[:, j, :], decay[j % 2][:, :], inj[:, q, j, :],
                                                           carry[:, g * J + j, n], ALU.mult, ALU.add
                                                           ).then_inc(s_scan, 1)
                                if i is not None:
                                    k = i * UNITS + p
                                    eng.wait_ge(s_lrt, LEAD + k * 2 + q + 1)
                                    if q == 0:
                                        eng.wait_ge(s_h, LEAD + k)
                                        eng.scalar_tensor_tensor(gl[:, :], bank[0][:, :], gsc[:, 0, bass.ds(i, 1)],
                                                                 lrt[:, :], ALU.mult, ALU.add).then_inc(s_gl, 1)
                                    else:
                                        eng.wait_ge(s_lo, LEAD + k)
                                        eng.scalar_tensor_tensor(ul[:, :], bank[1][:, :], gsc[:, 1, bass.ds(i, 1)],
                                                                 lrt[:, :], ALU.mult, ALU.add).then_inc(s_ul, 1)
                                        eng.wait_ge(s_ex, LEAD + k + 1)
                                        eng.scalar_tensor_tensor(gl[:, :], ex[:, :], 1.0, gl[:, :],
                                                                 ALU.add, ALU.mult).then_inc(s_sg, 1)
                                eng.wait_ge(s_zero, LEAD + step + 1)
                                for t in range(TPC):
                                    eng.wait_ge(s_turn, LEAD + slot * TPC + t + 1)
                                    eng.wait_ge(s_sum, LEAD + slot * TPC + t + 1)
                                    eng.scalar_tensor_tensor(ysum[:, t, :], turned[t % 2][:, :],
                                                             cT[:, c * TPC + t, n], ysum[:, t, :],
                                                             ALU.mult, ALU.add).then_inc(s_sum, 1)

                        run_pairs(eng, step, ff, pair)
                        eng.wait_ge(s_us, LEAD + step * 16 + 16)
                        for j in range(J):
                            eng.wait_ge(s_yt, LEAD + step * J + j + 1)
                            eng.scalar_tensor_tensor(us[:, j * T:(j + 1) * T], us[:, j * T:(j + 1) * T],
                                                     dsk[:, bass.ds(g * J + j, 1)], turned[j % 2][:, :],
                                                     ALU.mult, ALU.add).then_inc(s_yev, 1)

                    run_steps(v, step_fn)

                @block.gpsimd
                def _(pool):
                    pool.memset(ysum[:, :, :], 0.0).then_inc(s_zero, 1)

                    def step_fn(eng, c, g, ff, what):
                        if what == "chunk":
                            eng.wait_ge(s_bb, LEAD + c * 16 + 16)
                            eng.sem_inc(s_beat, 1)
                            return
                        step = c * G + g
                        eng.wait_ge(s_du, LEAD + step * 16 + 16)
                        eng.sem_inc(s_beat, 1)

                        def pair(step, pr, i, p):
                            for q in range(2):
                                slot = step * N + pr * 2 + q
                                eng.wait_ge(s_scan, LEAD + slot * J + EXTRA - J)
                                eng.tensor_tensor(inj[:, q, :, :], dub[:, :, :],
                                                  bb[:, bass.ds(pr * 2 + q, 1), :].broadcast_to([P, J, T]),
                                                  ALU.mult).then_inc(s_inj, 1)
                            if i is not None:
                                k = i * UNITS + p
                                eng.wait_ge(s_sg, LEAD + k + 1)
                                eng.tensor_tensor(ul[:, :], gl[:, :], ul[:, :], ALU.mult).then_inc(s_h, 1)
                                eng.wait_ge(s_h, LEAD + k + 1)
                                eng.wait_ge(s_hs, LEAD + k * 16)
                                eng.sem_inc(s_beat, 1)
                                eng.tensor_copy(hh[:, 0, :], ul[:, :]).then_inc(s_hi, 1)
                                eng.wait_ge(s_hi, LEAD + k + 1)
                                eng.tensor_tensor(hh[:, 1, :], ul[:, :], hh[:, 0, :], ALU.subtract
                                                  ).then_inc(s_lo, 1)

                        run_pairs(eng, step, ff, pair)
                        eng.wait_ge(s_yt, LEAD + step * J + J)
                        eng.sem_inc(s_beat, 1)
                        eng.memset(ysum[:, :, :], 0.0).then_inc(s_zero, 1)
                        eng.wait_ge(s_yev, LEAD + step * J + J + 2)
                        eng.wait_ge(s_gs, LEAD + step * 16 + 16)
                        eng.tensor_tensor(gs[:, :], us[:, :], gs[:, :], ALU.mult).then_inc(s_gate, 1)
                        eng.wait_ge(s_gate, LEAD + step + 1)
                        eng.sem_inc(s_beat, 1)
                        eng.tensor_copy(us16[:, 0:J * T], gs[:, :]).then_inc(s_parts, 1)
                        eng.wait_ge(s_parts, LEAD + step * 2 + 1)
                        eng.tensor_tensor(us16[:, J * T:2 * J * T], gs[:, :], us16[:, 0:J * T], ALU.subtract
                                          ).then_inc(s_parts, 1)

                    run_steps(pool, step_fn)

                @block.tensor
                def _(pe):
                    def step_fn(eng, c, g, ff, what):
                        if what == "chunk":
                            return
                        step = c * G + g

                        def pair(step, pr, i, p):
                            for q in range(2):
                                slot = step * N + pr * 2 + q
                                if i is not None:
                                    k = i * UNITS + p
                                    if q == 0:
                                        eng.wait_ge(s_conv, LEAD + i * UNITS + UNITS)
                                    eng.wait_ge((s_gl, s_ul)[q], LEAD + k)
                                    for h in range(HK):
                                        w = w16[:, i % 2, (q * HK + h) * P:(q * HK + h + 1) * P]
                                        eng.matmul(bank[q][:, :], w, xhi[:, h, bass.ts(p, T)],
                                                   start=(h == 0), stop=False)
                                        eng.matmul(bank[q][:, :], w, xlo[:, h, bass.ts(p, T)],
                                                   start=False, stop=(h == HK - 1))
                                    eng.wait_ge(s_lrt, LEAD + k * 2 + q)
                                    eng.matmul(lrb[:, :], btab[:, q, bass.ts(i, P)], xa[:, q, bass.ts(p, T)],
                                               start=True, stop=True).then_inc(s_mm, 1)
                                eng.wait_ge(s_scan, LEAD + slot * J + J + EXTRA)
                                if q == 0:
                                    eng.wait_ge(s_yev, LEAD + step * J + 2)
                                for t in range(TPC):
                                    eng.wait_ge(s_sum, LEAD + slot * TPC + t + 3)
                                    for j in range(J):
                                        mm = eng.transpose(turned[t % 2][:, j * P:(j + 1) * P],
                                                           state[:, j, t * P:(t + 1) * P], ident[:, :])
                                    mm.then_inc(s_turn, 1)

                        run_pairs(eng, step, ff, pair)
                        eng.wait_ge(s_sum, LEAD + step * (N * TPC) + N * TPC + J)
                        for j in range(J):
                            eng.wait_ge(s_yev, LEAD + step * J + j + 1)
                            for t in range(TPC):
                                mm = eng.transpose(turned[j % 2][:, t * P:(t + 1) * P],
                                                   ysum[:, t, j * P:(j + 1) * P], ident[:, :])
                            mm.then_inc(s_yt, 1)

                    run_steps(pe, step_fn)
        upto_scan.close()

        with ExitStack() as st:
            wo_hi = sb(st, "wo_hi", [P, DT, H], F16)
            wo_lo = sb(st, "wo_lo", [P, DT, H], F16)
            dw = sb(st, "dw", [P, IT, H], F16)
            da_hi = sb(st, "da_hi", [P, IT, 3 * LR], F16)
            da_lo = sb(st, "da_lo", [P, IT, 3 * LR], F16)
            db = sb(st, "db", [3 * LR, H], F16)
            raw = sb(st, "raw", [P, 2, H])
            rawi = sb(st, "rawi", [P, 2, H], I32)
            dar = sb(st, "dar", [P, IT, LR])
            dbr = sb(st, "dbr", [3 * LR, H])
            dscale = sb(st, "dscale", [P, H])
            hc = sb(st, "hc", [P, IT, 2, P], F16)
            yc = sb(st, "yc", [P, 2, DT, P], F16)
            ha = sb(st, "ha", [3 * LR, P], F16)
            xr = sb(st, "xr", [P, H])
            f1 = sb(st, "f1", [P, H])
            f2 = sb(st, "f2", [P, H])
            po = pb(st, "po", [P, 2, 512])
            pd = pb(st, "pd", [P, 2, 512])
            pl = pb(st, "pl", [P, 2, 512])
            pa = pb(st, "pa", [P, P])
            o_r = [sem(f"o_r{b}") for b in range(2)]
            o_q = [sem(f"o_q{b}") for b in range(2)]
            (o_c, o_ds, o_hi, o_lo, o_dw, o_dah, o_dal, o_dbh, o_dbl, o_h, o_y, o_x, o_ha, o_hah, o_hal, o_pl,
             o_pd, o_po, o_l, o_f, o_e, o_out, o_st) = (sem("o_" + s) for s in (
                "c ds hi lo dw dah dal dbh dbl h y x ha hah hal pl pd po l f e out st").split())
            flat = "p a b -> p (a b)"
            with nc.Block() as block:

                @block.sync
                def _(sp):
                    sp.dma_start(dar[:, :, :], d_a).then_inc(o_c, 16)
                    for r in range(3):
                        sp.dma_start(dbr[r * LR:(r + 1) * LR, :], d_b).then_inc(o_c, 16)
                    sp.dma_start(dscale[:, :], d_scale.partition_broadcast(P)).then_inc(o_c, 16)
                    with sp.Fori(0, DT // 2) as i:
                        for b in range(2):
                            sp.wait_ge(o_lo, LEAD + i * 2 + b)
                            sp.dma_start(raw[:, b, :], wout[i * 2 + b]).then_inc(o_r[b], 16)
                    with sp.Fori(0, IT // 2) as i:
                        for b in range(2):
                            sp.wait_ge(o_dw, LEAD + i * 2 + b)
                            sp.dma_start(rawi[:, b, :], dq[i * 2 + b]).then_inc(o_q[b], 16)
                    with sp.Fori(0, C) as c:
                        with sp.Fori(0, TPC) as t:
                            tt = c * TPC + t
                            sp.wait_ge(o_pl, LEAD + tt)
                            sp.dma_start(hc[:, :, :, :], h_s[c, :, :, :, bass.ts(t, P)]).then_inc(o_h, 16)
                            sp.dma_start(yc[:, :, :, :], y_s[c, :, :, :, bass.ts(t, P)]).then_inc(o_y, 16)
                            sp.wait_ge(o_st, LEAD + tt * 16)
                            sp.dma_start(xr[:, :], x[tt]).then_inc(o_x, 16)
                            sp.wait_ge(o_out, LEAD + tt + 1)
                            sp.dma_start(out[tt], xr[:, :]).then_inc(o_st, 16)
                    sp.wait_ge(o_st, LEAD + 16 * TT)

                @block.scalar
                def _(act):
                    act.wait_ge(o_c, LEAD + 80)
                    for r in range(3):
                        act.activation(da_hi[:, :, r * LR:(r + 1) * LR], dar[:, :, :], ACT.Copy).then_inc(o_dah, 1)
                    act.activation(db[:, :], dbr[:, :], ACT.Copy, scale=WS).then_inc(o_dbh, 1)
                    act.activation(dscale[:, :], dscale[:, :], ACT.Copy, scale=0.5 * Q_STEP).then_inc(o_ds, 1)
                    with act.Fori(0, DT // 2) as i:
                        for b in range(2):
                            act.wait_ge(o_r[b], LEAD + i * 16 + 16)
                            act.activation(wo_hi[:, bass.ds(i * 2 + b, 1), :], raw[:, bass.ds(b, 1), :], ACT.Copy,
                                           scale=WS).then_inc(o_hi, 1)
                    with act.Fori(0, IT // 2) as i:
                        for b in range(2):
                            act.wait_ge(o_q[b], LEAD + i * 16 + 16)
                            act.activation(dw[:, bass.ds(i * 2 + b, 1), :], rawi[:, bass.ds(b, 1), :], ACT.Copy,
                                           bias=-Q_ZERO).then_inc(o_dw, 1)
                    with act.Fori(0, TT) as t:
                        act.wait_ge(o_ha, LEAD + t + 1)
                        act.wait_ge(o_pl, LEAD + t)
                        act.activation(ha[:, :], pa[0:3 * LR, :], ACT.Copy).then_inc(o_hah, 1)
                        act.wait_ge(o_pl, LEAD + t + 1)
                        act.wait_ge(o_out, LEAD + t)
                        act.activation(f2[:, :], pl[:, :, :].rearrange(flat), ACT.Copy,
                                       scale=0.5 * LR_SCALE / WS).then_inc(o_l, 1)
                        act.wait_ge(o_f, LEAD + t * 2 + 2)
                        act.activation(f2[:, :], f1[:, :], ACT.Tanh).then_inc(o_e, 1)

                @block.vector
                def _(v):
                    v.wait_ge(o_dah, LEAD + 3)
                    for r in range(3):
                        v.tensor_tensor(da_lo[:, :, r * LR:(r + 1) * LR], dar[:, :, :],
                                        da_hi[:, :, r * LR:(r + 1) * LR], ALU.subtract).then_inc(o_dal, 1)
                    v.wait_ge(o_dbh, LEAD + 1)
                    v.scalar_tensor_tensor(db[2 * LR:3 * LR, :], dbr[2 * LR:3 * LR, :], WS, db[2 * LR:3 * LR, :],
                                           ALU.mult, ALU.subtract).then_inc(o_dbl, 1)
                    with v.Fori(0, DT) as i:
                        v.wait_ge(o_hi, LEAD + i + 1)
                        v.scalar_tensor_tensor(wo_lo[:, bass.ds(i, 1), :], raw[:, bass.ds(i % 2, 1), :], WS,
                                               wo_hi[:, bass.ds(i, 1), :], ALU.mult, ALU.subtract
                                               ).then_inc(o_lo, 1)
                    v.wait_ge(o_ds, LEAD + 1)
                    with v.Fori(0, TT) as t:
                        v.wait_ge(o_hah, LEAD + t + 1)
                        v.tensor_tensor(ha[LR:2 * LR, :], pa[LR:2 * LR, :], ha[LR:2 * LR, :], ALU.subtract
                                        ).then_inc(o_hal, 1)
                        v.wait_ge(o_pd, LEAD + t + 1)
                        v.tensor_tensor(f1[:, :], pd[:, :, :].rearrange(flat), dscale[:, :], ALU.mult
                                        ).then_inc(o_f, 1)
                        v.wait_ge(o_l, LEAD + t + 1)
                        v.wait_ge(o_f, LEAD + t * 2 + 1)
                        v.tensor_tensor(f1[:, :], f1[:, :], f2[:, :], ALU.add).then_inc(o_f, 1)
                        v.wait_ge(o_e, LEAD + t + 1)
                        v.scalar_tensor_tensor(f1[:, :], f2[:, :], 1.0, f1[:, :], ALU.add, ALU.mult).then_inc(o_hal, 1)
                        v.wait_ge(o_hal, LEAD + t * 3 + 2)
                        v.wait_ge(o_po, LEAD + t + 1)
                        v.scalar_tensor_tensor(f1[:, :], po[:, :, :].rearrange(flat), 1.0 / WS, f1[:, :],
                                               ALU.mult, ALU.mult).then_inc(o_hal, 1)
                        v.wait_ge(o_hal, LEAD + t * 3 + 3)
                        v.wait_ge(o_x, LEAD + t * 16 + 16)
                        v.tensor_tensor(xr[:, :], xr[:, :], f1[:, :], ALU.add).then_inc(o_out, 1)

                @block.tensor
                def _(pe):
                    pe.wait_ge(o_dal, LEAD + 3)
                    pe.wait_ge(o_dbl, LEAD + 1)
                    pe.wait_ge(o_lo, LEAD + DT)
                    pe.wait_ge(o_dw, LEAD + IT)
                    with pe.Fori(0, TT) as t:
                        pe.wait_ge(o_h, LEAD + t * 16 + 16)
                        pe.wait_ge(o_hal, LEAD + t * 3)
                        for i in range(IT):
                            for z, (a, part) in enumerate(((da_hi, 0), (da_hi, 1), (da_lo, 0))):
                                mm = pe.matmul(pa[0:3 * LR, :], a[:, i, :], hc[:, i, part, :],
                                               start=(i == 0 and z == 0), stop=(i == IT - 1 and z == 2))
                        mm.then_inc(o_ha, 1)
                        pe.wait_ge(o_f, LEAD + t * 2)
                        for half in range(2):
                            cols = slice(half * 512, half * 512 + 512)
                            for i in range(IT):
                                for part in range(2):
                                    mm = pe.matmul(pd[:, half, :], hc[:, i, part, :], dw[:, i, cols],
                                                   start=(i == 0 and part == 0), stop=(i == IT - 1 and part == 1))
                        mm.then_inc(o_pd, 1)
                        pe.wait_ge(o_y, LEAD + t * 16 + 16)
                        pe.wait_ge(o_out, LEAD + t)
                        for half in range(2):
                            cols = slice(half * 512, half * 512 + 512)
                            for i in range(DT):
                                for z, (part, w) in enumerate(((0, wo_hi), (1, wo_hi), (0, wo_lo))):
                                    mm = pe.matmul(po[:, half, :], yc[:, part, i, :], w[:, i, cols],
                                                   start=(i == 0 and z == 0), stop=(i == DT - 1 and z == 2))
                        mm.then_inc(o_po, 1)
                        pe.wait_ge(o_hal, LEAD + t * 3 + 1)
                        pe.wait_ge(o_l, LEAD + t)
                        for half in range(2):
                            cols = slice(half * 512, half * 512 + 512)
                            mm = pe.matmul(pl[:, half, :], ha[:, :], db[:, cols], start=True, stop=True)
                        mm.then_inc(o_pl, 1)


def kernel(L0_attn_hidden_states, L0_attn_W_in, L0_attn_conv_w, L0_attn_conv_b, L0_attn_W_x, L0_attn_W_dt,
           L0_attn_b_dt, L0_attn_A_log, L0_attn_D, L0_attn_W_out, L0_ffn_gate_q, L0_ffn_gate_scale,
           L0_ffn_gate_A, L0_ffn_gate_B, L0_ffn_up_q, L0_ffn_up_scale, L0_ffn_up_A, L0_ffn_up_B,
           L0_ffn_down_q, L0_ffn_down_scale, L0_ffn_down_A, L0_ffn_down_B):
    import numpy as np
    import concourse.bacc as bacc
    from concourse.bass_utils import run_bass_kernel_spmd as run

    def arr(a):
        return np.ascontiguousarray(np.asarray(a))

    def rows(a, n):
        a = np.asarray(a)
        return np.concatenate([a, np.zeros((n - a.shape[0],) + a.shape[1:], a.dtype)])

    def qtiles(q):
        return rows(q, IPAD).reshape(IT, P, HK, P).transpose(0, 3, 2, 1).reshape(IT, P, HK * P)

    def cols(a):
        return np.asarray(a).reshape(DT, P).T

    gu = np.concatenate([qtiles(L0_ffn_gate_q), qtiles(L0_ffn_up_q)], axis=2)
    ins = dict(
        x=np.asarray(L0_attn_hidden_states).reshape(TT, P, H),
        win=np.asarray(L0_attn_W_in).reshape(2 * DT, P, HK, P).transpose(0, 3, 2, 1).reshape(2 * DT, P, HK * P),
        convw=np.asarray(L0_attn_conv_w).reshape(DT, P, K).transpose(1, 0, 2),
        convb=cols(L0_attn_conv_b),
        wx=np.asarray(L0_attn_W_x).T.reshape(DT, P, S3).transpose(1, 0, 2),
        wdt=np.asarray(L0_attn_W_dt).reshape(DT, P, R).transpose(0, 2, 1),
        bdt=cols(L0_attn_b_dt),
        alog=np.asarray(L0_attn_A_log).reshape(DT, P, N).transpose(1, 0, 2),
        dskip=cols(L0_attn_D),
        wout=np.asarray(L0_attn_W_out).T.reshape(DT, P, H),
        gu_q=rows(gu, IT + 1),
        g_scale=rows(L0_ffn_gate_scale, IPAD).reshape(IT, P).T,
        u_scale=rows(L0_ffn_up_scale, IPAD).reshape(IT, P).T,
        lr_a=np.stack([np.asarray(a).reshape(HK, P, LR).transpose(1, 0, 2) for a in (L0_ffn_gate_A, L0_ffn_up_A)]),
        g_b=rows(np.asarray(L0_ffn_gate_B).T, IPAD).T,
        u_b=rows(np.asarray(L0_ffn_up_B).T, IPAD).T,
        dq=rows(np.asarray(L0_ffn_down_q).T, IPAD).reshape(IT, P, H),
        d_scale=np.asarray(L0_ffn_down_scale),
        d_a=rows(L0_ffn_down_A, IPAD).reshape(IT, P, LR).transpose(1, 0, 2),
        d_b=np.asarray(L0_ffn_down_B),
        ident_in=np.eye(P, dtype=np.float32),
    )
    nc = bacc.Bacc("TRN2", target_bir_lowering=False, num_devices=1)
    arrays, args = {}, []
    for name, a in ins.items():
        arrays["in_" + name] = arr(a)
        args.append(nc.dram_tensor("in_" + name, a.shape, mybir.dt.from_np(a.dtype), kind="ExternalInput").ap())
    args.append(nc.dram_tensor("out_0", (TT, P, H), F32, kind="ExternalOutput").ap())
    for name, shape, dt in (("u_s", (G, C, P, J, T), F32), ("gs_s", (G, C, P, J, T), F32),
                            ("dt_s", (G, C, P, J, T), F32), ("du_s", (G, C, P, J, T), F32),
                            ("bt_s", (N, L), F32), ("h_s", (C, P, IT, 2, T), F16),
                            ("y_s", (C, P, 2, DT, T), F16)):
        args.append(nc.dram_tensor(name, shape, dt, kind="Internal").ap())
    mixer_kernel(nc, *args)
    r = run(nc, [arrays], core_ids=[0])
    return r.results[0]["out_0"].reshape(1, L, H)
```

```python
from contextlib import ExitStack

import concourse.bass as bass
from concourse import mybir

F32 = mybir.dt.float32
F16 = mybir.dt.float16
I32 = mybir.dt.int32
ALU = mybir.AluOpType
ACT = mybir.ActivationFunctionType
AX = mybir.AxisListType

P = 128
L, H, DI, N, R, K, I, LR = 2048, 1024, 2048, 16, 64, 4, 2752, 32
T = 512
C = L // T
TT = L // P
TPC = T // P
HK = H // P
DT = DI // P
J = 4
G = DT // J
IT = -(-I // P)
IPAD = IT * P
S3 = R + 2 * N
WS = 256.0
Q_ZERO, Q_STEP, LR_SCALE = 7.5, 0.005, 0.02
UNITS = C
LEAD = 1
SEMAPHORES = (
    "n_x0 n_x1 i_w0 i_w1 i_st0 i_st1 g_w0 g_w1 g_wd0 g_wd1 g_sg0 g_sg1 g_sd0 g_sd1 g_u0 g_u1 o_r0 o_r1 "
    "o_q0 o_q1 n_const n_dve n_xn n_tp n_hi n_lo n_a n_var n_sd n_beat i_const i_z i_hi i_lo i_mm i_ev "
    "i_cv i_e i_u i_ssm i_sm i_half r_a r_b r_v r_sm r_tp r_tb r_st r_ah r_al r_xa r_xh r_xl r_bh r_bl "
    "r_sd g_const g_hi g_lo g_mm g_ev g_e g_g g_pre g_mx g_ab g_sp g_dt g_du s_const s_gsc s_bb0 s_bb1 s_ffz s_yhi s_dt s_du "
    "s_us s_gs s_ys s_dec s_inj s_scan s_carry s_turn s_sum s_yt s_yev s_gate s_parts s_wq0 s_wq1 "
    "s_conv s_mm s_lrt s_gl s_ul s_ex s_sg s_h s_hi s_lo s_hs s_beat o_c o_ds o_hi o_lo o_dw o_dah o_dal "
    "o_dbh o_dbl o_h0 o_h1 o_y0 o_y1 o_x o_ha o_hah o_hal o_pl o_pd o_po o_l o_f o_e o_out o_st "
).split()
EXTRA = 8


def mixer_kernel(nc, x, win, convw, convb, wx, wdt, bdt, alog, dskip, wout, gu_q, g_scale, u_scale,
                 lr_a, g_b, u_b, dq, d_scale, d_a, d_b, ident_in, out,
                 u_s, gs_s, dt_s, du_s, bt_s, h_s, y_s):
    whole = ExitStack()
    with whole:
        def sb(stack, name, shape, dt=F32):
            return stack.enter_context(nc.sbuf_tensor(name, shape, dt))

        def pb(stack, name, shape, dt=F32):
            return stack.enter_context(nc.psum_tensor(name, shape, dt))

        semaphores = {name: whole.enter_context(nc.semaphore(name)) for name in SEMAPHORES}
        sem = semaphores.__getitem__

        def start_semaphores(eng, share):
            for name in SEMAPHORES[share::4]:
                eng.sem_inc(semaphores[name], LEAD)

        with nc.Block() as block:
            @block.gpsimd
            def _(pool):
                start_semaphores(pool, 0)

            @block.scalar
            def _(act):
                start_semaphores(act, 1)

            @block.vector
            def _(v):
                start_semaphores(v, 2)

            @block.sync
            def _(sp):
                start_semaphores(sp, 3)

        ident = sb(whole, "ident", [P, P])
        aneg = sb(whole, "aneg", [P, DT, N])
        cT = sb(whole, "cT", [P, TT, N])
        dsk = sb(whole, "dsk", [P, DT])
        upto_scan = whole.enter_context(ExitStack())
        xhi = sb(upto_scan, "xhi", [P, HK, L], F16)
        xlo = sb(upto_scan, "xlo", [P, HK, L], F16)
        xa = sb(upto_scan, "xa", [3 * LR, 2, L], F16)
        btab = sb(upto_scan, "btab", [3 * LR, 2, IPAD], F16)

        with ExitStack() as st:
            xt = sb(st, "xt", [P, 2, H])
            xn = sb(st, "xn", [P, 2, H])
            stats = sb(st, "stats", [P, 2, 2, 6])
            mv = sb(st, "mv", [P, 2, 2])
            var = sb(st, "var", [P, 2, 1])
            rstd = sb(st, "rstd", [P, 2, 1])
            al = sb(st, "al", [P, DT, N])
            xtp = [pb(st, f"xtp{b}", [P, HK, P]) for b in range(2)]
            n_x = [sem(f"n_x{b}") for b in range(2)]
            n_const, n_dve, n_xn, n_tp, n_hi, n_lo, n_a, n_var, n_sd, n_beat = (
                sem(s) for s in ("n_const", "n_dve", "n_xn", "n_tp", "n_hi", "n_lo", "n_a", "n_var", "n_sd", "n_beat"))
            with nc.Block() as block:

                @block.sync
                def _(sp):
                    sp.dma_start(ident[:, :], ident_in).then_inc(n_const, 16)
                    sp.dma_start(al[:, :, :], alog).then_inc(n_const, 16)
                    sp.dma_start(dsk[:, :], dskip).then_inc(n_const, 16)
                    with sp.Fori(0, TT // 2) as i:
                        for b in range(2):
                            sp.wait_ge(n_xn, LEAD + i * 2 + b)
                            sp.dma_start(xt[:, b, :], x[i * 2 + b]).then_inc(n_x[b], 16)

                @block.vector
                def _(v):
                    with v.Fori(0, TT // 2) as i:
                        for b in range(2):
                            v.wait_ge(n_x[b], LEAD + i * 16 + 16)
                            for h in range(2):
                                v.bn_stats(stats[:, b, h, :], xt[:, b, h * 512:(h + 1) * 512]).then_inc(n_dve, 1)
                            v.wait_ge(n_dve, LEAD + i * 8 + b * 4 + 2)
                            v.sem_inc(n_beat, 1)
                            v.bn_aggr(mv[:, b, :], stats[:, b, :, :].rearrange("p a s -> p (a s)")).then_inc(n_dve, 1)
                            v.wait_ge(n_dve, LEAD + i * 8 + b * 4 + 3)
                            v.tensor_scalar(var[:, b, :], mv[:, b, 1:2], 1e-5, None, ALU.add).then_inc(n_var, 1)
                            v.wait_ge(n_sd, LEAD + i * 2 + b + 1)
                            v.reciprocal(rstd[:, b, :], var[:, b, :]).then_inc(n_dve, 1)
                            v.wait_ge(n_dve, LEAD + i * 8 + b * 4 + 4)
                            v.wait_ge(n_tp, LEAD + i * 2 + b)
                            v.tensor_scalar(xn[:, b, :], xt[:, b, :], mv[:, b, 0:1], rstd[:, b, :],
                                            ALU.subtract, ALU.mult).then_inc(n_xn, 1)
                        for b in range(2):
                            v.wait_ge(n_hi, LEAD + i * 2 + b + 1)
                            tok = bass.ds((i * 2 + b) * P, P)
                            v.tensor_tensor(xlo[:, :, tok], xtp[b][:, :, :], xhi[:, :, tok],
                                            ALU.subtract).then_inc(n_lo, 1)

                @block.tensor
                def _(pe):
                    pe.wait_ge(n_const, LEAD + 48)
                    with pe.Fori(0, TT // 2) as i:
                        for b in range(2):
                            pe.wait_ge(n_xn, LEAD + i * 2 + b + 1)
                            pe.wait_ge(n_lo, LEAD + i * 2 + b)
                            for k in range(HK):
                                mm = pe.transpose(xtp[b][:, k, :], xn[:, b, k * P:(k + 1) * P], ident[:, :])
                            mm.then_inc(n_tp, 1)

                @block.scalar
                def _(act):
                    act.wait_ge(n_const, LEAD + 48)
                    act.activation(al[:, :, :], al[:, :, :], ACT.Exp).then_inc(n_a, 1)
                    act.wait_ge(n_a, LEAD + 1)
                    act.mul(aneg[:, :, :], al[:, :, :], -1.0).then_inc(n_a, 1)
                    with act.Fori(0, TT // 2) as i:
                        for b in range(2):
                            act.wait_ge(n_var, LEAD + i * 2 + b + 1)
                            act.activation(var[:, b, :], var[:, b, :], ACT.Sqrt).then_inc(n_sd, 1)
                        for b in range(2):
                            act.wait_ge(n_tp, LEAD + i * 2 + b + 1)
                            act.activation(xhi[:, :, bass.ds((i * 2 + b) * P, P)], xtp[b][:, :, :],
                                           ACT.Copy).then_inc(n_hi, 1)

        proj = ExitStack()
        with proj:
            wraw = sb(proj, "wraw", [P, 2, HK * P])
            whi = sb(proj, "whi", [P, 2, HK * P], F16)
            wlo = sb(proj, "wlo", [P, 2, HK * P], F16)
            xp = sb(proj, "xp", [P, 2, L + K - 1])
            eb = sb(proj, "eb", [P, L])
            sm = sb(proj, "sm", [P, TT, S3])
            main = [pb(proj, f"main{t}", [P, T]) for t in range(C)]
            four = pb(proj, "four", [P, C, T])

            with ExitStack() as st:
                xc = sb(st, "xc", [P, 2, L])
                ub = sb(st, "ub", [P, 2, L])
                zero = sb(st, "zero", [P, T])
                wx_sb = sb(st, "wx_sb", [P, DT, S3])
                cw = sb(st, "cw", [P, DT, K])
                cb = sb(st, "cb", [P, DT])
                i_w = [sem(f"i_w{b}") for b in range(2)]
                (i_const, i_z, i_hi, i_lo, i_mm, i_ev, i_cv, i_e, i_u, i_ssm, i_sm, i_half) = (
                    sem(s) for s in ("i_const", "i_z", "i_hi", "i_lo", "i_mm", "i_ev", "i_cv",
                                     "i_e", "i_u", "i_ssm", "i_sm", "i_half"))
                i_st = [sem(f"i_st{b}") for b in range(2)]
                with nc.Block() as block:

                    @block.sync
                    def _(sp):
                        sp.dma_start(wraw[:, 0, :], win[0]).then_inc(i_w[0], 16)
                        for dst, src in ((wx_sb, wx), (cw, convw), (cb, convb)):
                            sp.dma_start(dst[:], src).then_inc(i_const, 16)
                        with sp.Fori(0, DT // 2) as i:
                            for b in range(2):
                                w = i * 2 + b
                                sp.wait_ge(i_lo, LEAD + w)
                                nb = 1 - b
                                sp.dma_start(wraw[:, nb, :], win[w + 1]).then_inc(i_w[nb], 16)
                                sp.wait_ge(i_u, LEAD + w + 1)
                                sp.dma_start(u_s[i // 2, :, :, (i % 2) * 2 + b, :].rearrange("c p t -> p c t"),
                                             ub[:, b, :].rearrange("p (c t) -> p c t", c=C)).then_inc(i_st[b], 16)
                        for b in range(2):
                            sp.wait_ge(i_st[b], LEAD + 16 * (DT // 2))

                    @block.scalar
                    def _(act):
                        act.wait_ge(i_w[0], LEAD + 16)
                        act.activation(whi[:, 0, :], wraw[:, 0, :], ACT.Copy, scale=WS).then_inc(i_hi, 1)
                        act.wait_ge(i_z, LEAD + 3)
                        with act.Fori(0, DT // 2) as i:
                            for b in range(2):
                                w = i * 2 + b
                                nb = 1 - b
                                act.wait_ge(i_w[nb], LEAD + i * 16 + 16 * (1 + b))
                                act.wait_ge(i_mm, LEAD + w * C)
                                act.activation(whi[:, nb, :], wraw[:, nb, :], ACT.Copy, scale=WS).then_inc(i_hi, 1)
                                for c in range(C):
                                    act.wait_ge(i_mm, LEAD + w * C + c + 1)
                                    if c == 0:
                                        act.wait_ge(i_cv, LEAD + w * 4)
                                    act.activation(xp[:, b, K - 1 + c * T:K - 1 + (c + 1) * T], main[c][:, :],
                                                   ACT.Copy, scale=1.0 / WS).then_inc(i_ev, 1)
                                act.wait_ge(i_cv, LEAD + w * 4 + 4)
                                act.wait_ge(i_u, LEAD + w)
                                act.activation(eb[:, :], xc[:, b, :], ACT.Tanh).then_inc(i_e, 1)

                    @block.vector
                    def _(v):
                        v.memset(zero[:, :], 0.0).then_inc(i_z, 1)
                        for b in range(2):
                            v.memset(xp[:, b, 0:K - 1], 0.0).then_inc(i_z, 1)
                        v.wait_ge(i_hi, LEAD + 1)
                        v.scalar_tensor_tensor(wlo[:, 0, :], wraw[:, 0, :], WS, whi[:, 0, :],
                                               ALU.mult, ALU.subtract).then_inc(i_lo, 1)
                        v.wait_ge(i_const, LEAD + 48)
                        v.tensor_scalar(cw[:, :, :], cw[:, :, :], 0.5, None, ALU.mult).then_inc(i_half, 1)
                        v.tensor_scalar(cb[:, :], cb[:, :], 0.5, None, ALU.mult).then_inc(i_half, 1)
                        v.wait_ge(i_half, LEAD + 2)
                        with v.Fori(0, DT // 2) as i:
                            for b in range(2):
                                w = i * 2 + b
                                nb = 1 - b
                                v.wait_ge(i_hi, LEAD + w + 2)
                                v.scalar_tensor_tensor(wlo[:, nb, :], wraw[:, nb, :], WS, whi[:, nb, :],
                                                       ALU.mult, ALU.subtract).then_inc(i_lo, 1)
                                v.wait_ge(i_ev, LEAD + w * C + C)
                                v.wait_ge(i_e, LEAD + w)
                                v.tensor_scalar(xc[:, b, :], xp[:, b, 0:L], cw[:, w, 0:1], cb[:, bass.ds(w, 1)],
                                                ALU.mult, ALU.add).then_inc(i_cv, 1)
                                for j in range(1, K):
                                    v.wait_ge(i_cv, LEAD + w * 4 + j)
                                    v.scalar_tensor_tensor(xc[:, b, :], xp[:, b, j:j + L], cw[:, w, j:j + 1],
                                                           xc[:, b, :], ALU.mult, ALU.add).then_inc(i_cv, 1)
                                v.wait_ge(i_e, LEAD + w + 1)
                                v.wait_ge(i_st[b], LEAD + i * 16)
                                v.wait_ge(i_ssm, LEAD + w)
                                v.scalar_tensor_tensor(ub[:, b, :], eb[:, :], 1.0, xc[:, b, :],
                                                       ALU.add, ALU.mult).then_inc(i_u, 1)
                        v.wait_ge(i_ssm, LEAD + DT + 1)
                        v.tensor_copy(sm[:, :, :].rearrange("p (a t) s -> p a (t s)", a=C),
                                      four[:, :, 0:TPC * S3]).then_inc(i_sm, 1)

                    @block.tensor
                    def _(pe):
                        def w_x(b, w):
                            pe.wait_ge(i_u, LEAD + w + 1)
                            for t in range(TT):
                                mm = pe.matmul(four[:, t // TPC, (t % TPC) * S3:(t % TPC + 1) * S3],
                                               ub[:, b, t * P:(t + 1) * P], wx_sb[:, w, :],
                                               start=False, stop=False, skip_group_check=True)
                            mm.then_inc(i_ssm, 1)

                        def tile(b, w):
                            pe.wait_ge(i_lo, LEAD + w + 1)
                            for c in range(C):
                                if not isinstance(w, int):
                                    pe.wait_ge(i_ev, LEAD + (w - 1) * C + c + 1)
                                elif w > 0:
                                    pe.wait_ge(i_ev, LEAD + (w - 1) * C + c + 1)
                                for k in range(HK):
                                    hi = whi[:, b, k * P:(k + 1) * P]
                                    lo = wlo[:, b, k * P:(k + 1) * P]
                                    xh = xhi[:, k, c * T:(c + 1) * T]
                                    xl = xlo[:, k, c * T:(c + 1) * T]
                                    pe.matmul(main[c][:, :], hi, xh, start=(k == 0), stop=False)
                                    pe.matmul(main[c][:, :], hi, xl, start=False, stop=False)
                                    mm = pe.matmul(main[c][:, :], lo, xh, start=False, stop=(k == HK - 1))
                                mm.then_inc(i_mm, 1)

                        pe.wait_ge(i_z, LEAD + 1)
                        for c in range(C):
                            mm = pe.matmul(four[:, c, :], zero[:, 0:P], zero[:, :], start=True, stop=False,
                                           skip_group_check=True)
                        mm.then_inc(i_ssm, 1)
                        pe.wait_ge(i_const, LEAD + 48)
                        tile(0, 0)
                        tile(1, 1)
                        w_x(0, 0)
                        with pe.Fori(1, DT // 2) as i:
                            for b in range(2):
                                tile(b, i * 2 + b)
                                w_x(1 - b, i * 2 + b - 1)
                        w_x(1, DT - 1)

            tsb = sb(proj, "tsb", [R + N, L])
            with ExitStack() as st:
                sq = sb(st, "sq", [P, TT, S3])
                ms = sb(st, "ms", [P, 3, TT])
                araw = sb(st, "araw", [P, 2, HK, 3 * LR])
                ahi = sb(st, "ahi", [P, 2, HK, 3 * LR], F16)
                alo = sb(st, "alo", [P, 2, HK, 3 * LR], F16)
                braw = sb(st, "braw", [3 * LR, IPAD])
                (r_a, r_b, r_v, r_sm, r_tp, r_tb, r_st, r_ah, r_al, r_xa, r_xh, r_xl, r_bh, r_bl, r_sd) = (
                    sem(s) for s in ("r_a", "r_b", "r_v", "r_sm", "r_tp", "r_tb", "r_st", "r_ah", "r_al",
                                     "r_xa", "r_xh", "r_xl", "r_bh", "r_bl", "r_sd"))
                groups = ((0, R), (R, N), (R + N, N))
                with nc.Block() as block:

                    @block.sync
                    def _(sp):
                        for m in range(2):
                            for r in range(3):
                                sp.dma_start(araw[:, m, :, r * LR:(r + 1) * LR], lr_a[m]).then_inc(r_a, 16)
                        for m, src in enumerate((g_b, u_b)):
                            if m:
                                sp.wait_ge(r_bl, LEAD + 1)
                            for r in range(3):
                                sp.dma_start(braw[r * LR:(r + 1) * LR, :], src).then_inc(r_b, 16)
                        sp.wait_ge(r_tb, LEAD + C)
                        sp.dma_start(bt_s, tsb[R:R + N, :]).then_inc(r_st, 16)
                        sp.wait_ge(r_st, LEAD + 16)

                    @block.vector
                    def _(v):
                        v.tensor_tensor(sq[:, :, :], sm[:, :, :], sm[:, :, :], ALU.mult).then_inc(r_v, 1)
                        v.wait_ge(r_v, LEAD + 1)
                        for g, (o, n) in enumerate(groups):
                            v.reduce_sum(ms[:, g, :], sq[:, :, o:o + n], axis=AX.X).then_inc(r_v, 1)
                        v.wait_ge(r_v, LEAD + 4)
                        for g, (o, n) in enumerate(groups):
                            v.tensor_scalar(ms[:, g, :], ms[:, g, :], 1.0 / n, 1e-6, ALU.mult, ALU.add
                                            ).then_inc(r_v, 1)
                        v.wait_ge(r_v, LEAD + 7)
                        v.wait_ge(r_sd, LEAD + 1)
                        v.reciprocal(ms[:, :, :], ms[:, :, :]).then_inc(r_v, 1)
                        v.wait_ge(r_v, LEAD + 8)
                        for g, (o, n) in enumerate(groups):
                            dst = cT[:, :, :] if g == 2 else sm[:, :, o:o + n]
                            v.tensor_tensor(dst, sm[:, :, o:o + n],
                                            ms[:, g, :].unsqueeze(2).broadcast_to([P, TT, n]), ALU.mult
                                            ).then_inc(r_sm, 1)
                        v.wait_ge(r_ah, LEAD + 1)
                        v.tensor_tensor(alo[:, :, :, :].rearrange("p a b c -> p (a b c)"),
                                        araw[:, :, :, :].rearrange("p a b c -> p (a b c)"),
                                        ahi[:, :, :, :].rearrange("p a b c -> p (a b c)"),
                                        ALU.subtract).then_inc(r_al, 1)
                        for m in range(2):
                            v.wait_ge(r_bh, LEAD + m + 1)
                            v.scalar_tensor_tensor(btab[2 * LR:3 * LR, m, :], braw[2 * LR:3 * LR, :], WS,
                                                   btab[2 * LR:3 * LR, m, :], ALU.mult, ALU.subtract
                                                   ).then_inc(r_bl, 1)
                        for q in range(2 * C):
                            m, c = divmod(q, C)
                            v.wait_ge(r_xh, LEAD + q + 1)
                            dst = xa[LR:2 * LR, m, c * T:(c + 1) * T]
                            v.tensor_tensor(dst, main[q % 4][LR:2 * LR, :], dst, ALU.subtract).then_inc(r_xl, 1)

                    @block.scalar
                    def _(act):
                        act.wait_ge(r_v, LEAD + 7)
                        act.activation(ms[:, :, :], ms[:, :, :], ACT.Sqrt).then_inc(r_sd, 1)
                        act.wait_ge(r_a, LEAD + 96)
                        act.activation(ahi[:, :, :, :].rearrange("p a b c -> p (a b c)"),
                                       araw[:, :, :, :].rearrange("p a b c -> p (a b c)"),
                                       ACT.Copy).then_inc(r_ah, 1)
                        for m in range(2):
                            act.wait_ge(r_b, LEAD + 48 * (m + 1))
                            act.activation(btab[:, m, :], braw[:, :], ACT.Copy, scale=WS).then_inc(r_bh, 1)
                        for c in range(C):
                            act.wait_ge(r_tp, LEAD + c + 1)
                            act.activation(tsb[:, c * T:(c + 1) * T], four[0:R + N, c, :], ACT.Copy
                                           ).then_inc(r_tb, 1)
                        for q in range(2 * C):
                            m, c = divmod(q, C)
                            act.wait_ge(r_xa, LEAD + q + 1)
                            act.activation(xa[:, m, c * T:(c + 1) * T], main[q % 4][0:3 * LR, :], ACT.Copy
                                           ).then_inc(r_xh, 1)

                    @block.tensor
                    def _(pe):
                        pe.wait_ge(r_sm, LEAD + 2)
                        for c in range(C):
                            for t in range(TPC):
                                mm = pe.transpose(four[0:R + N, c, t * P:(t + 1) * P],
                                                  sm[:, c * TPC + t, 0:R + N], ident[:, :])
                            mm.then_inc(r_tp, 1)
                        pe.wait_ge(r_al, LEAD + 1)
                        for q in range(2 * C):
                            m, c = divmod(q, C)
                            if q >= 4:
                                pe.wait_ge(r_xl, LEAD + q - 3)
                            for k in range(HK):
                                for a, xx, z in ((ahi, xhi, 0), (ahi, xlo, 1), (alo, xhi, 2)):
                                    mm = pe.matmul(main[q % 4][0:3 * LR, :], a[:, m, k, :],
                                                   xx[:, k, c * T:(c + 1) * T],
                                                   start=(k == 0 and z == 0), stop=(k == HK - 1 and z == 2))
                            mm.then_inc(r_xa, 1)

            with ExitStack() as st:
                wd = sb(st, "wd", [R, 2, P])
                bd = sb(st, "bd", [P, DT])
                gsb = sb(st, "gsb", [P, 2, L])
                mx = sb(st, "mx", [P, 2, L])
                ab = sb(st, "ab", [P, L])
                du = sb(st, "du", [P, 2, L])
                g_w = [sem(f"g_w{b}") for b in range(2)]
                g_wd = [sem(f"g_wd{b}") for b in range(2)]
                g_sg = [sem(f"g_sg{b}") for b in range(2)]
                g_sd = [sem(f"g_sd{b}") for b in range(2)]
                g_u = [sem(f"g_u{b}") for b in range(2)]
                (g_const, g_hi, g_lo, g_mm, g_ev, g_e, g_g, g_pre, g_mx, g_ab, g_sp, g_dt, g_du) = (
                    sem(s) for s in ("g_const", "g_hi", "g_lo", "g_mm", "g_ev", "g_e", "g_g", "g_pre",
                                     "g_mx", "g_ab", "g_sp", "g_dt", "g_du"))
                with nc.Block() as block:
                    def store(dram, i, b, tile):
                        return (dram[i // 2, :, :, (i % 2) * 2 + b, :].rearrange("c p t -> p c t"),
                                tile.rearrange("p (c t) -> p c t", c=C))

                    @block.sync
                    def _(sp):
                        sp.dma_start(bd[:, :], bdt).then_inc(g_const, 16)
                        with sp.Fori(0, DT // 2) as i:
                            for b in range(2):
                                w = i * 2 + b
                                sp.wait_ge(g_mx, LEAD + w)
                                sp.dma_start(wd[:, b, :], wdt[w]).then_inc(g_wd[b], 16)
                                sp.wait_ge(g_lo, LEAD + w)
                                sp.dma_start(wraw[:, b, :], win[w + DT]).then_inc(g_w[b], 16)
                                sp.wait_ge(g_sd[b], LEAD + i * 32)
                                dst, src = du[:, b, :].rearrange("p (c t) -> p c t", c=C), \
                                    u_s[i // 2, :, :, (i % 2) * 2 + b, :].rearrange("c p t -> p c t")
                                sp.dma_start(dst, src).then_inc(g_u[b], 16)
                                sp.wait_ge(g_du, LEAD + w + 1)
                                sp.dma_start(*store(dt_s, i, b, mx[:, b, :])).then_inc(g_sd[b], 16)
                                sp.dma_start(*store(du_s, i, b, du[:, b, :])).then_inc(g_sd[b], 16)
                        for b in range(2):
                            sp.wait_ge(g_sd[b], LEAD + 32 * (DT // 2))

                    @block.scalar
                    def _(act):
                        act.wait_ge(g_const, LEAD + 16)
                        with act.Fori(0, DT // 2) as i:
                            for b in range(2):
                                w = i * 2 + b
                                act.wait_ge(g_w[b], LEAD + i * 16 + 16)
                                act.wait_ge(g_ev, LEAD + w * C)
                                act.activation(whi[:, b, :], wraw[:, b, :], ACT.Copy, scale=WS).then_inc(g_hi, 1)
                                act.wait_ge(g_pre, LEAD + w + 1)
                                act.wait_ge(g_dt, LEAD + w)
                                act.activation(ab[:, :], four[:, :, :].rearrange("p c t -> p (c t)"), ACT.Abs,
                                               bias=bd[:, bass.ds(w, 1)]).then_inc(g_ab, 1)
                                act.wait_ge(g_ab, LEAD + w * 2 + 1)
                                act.activation(ab[:, :], ab[:, :], ACT.Exp, scale=-1.0).then_inc(g_ab, 1)
                                act.wait_ge(g_ab, LEAD + w * 2 + 2)
                                act.activation(ab[:, :], ab[:, :], ACT.Ln, bias=1.0).then_inc(g_sp, 1)
                                for c in range(C):
                                    act.wait_ge(g_mm, LEAD + w * C + c + 1)
                                    if c == 0:
                                        act.wait_ge(g_g, LEAD + w)
                                    act.activation(xp[:, b, c * T:(c + 1) * T], main[c][:, :],
                                                   ACT.Copy, scale=0.5 / WS).then_inc(g_ev, 1)
                                act.wait_ge(g_ev, LEAD + w * C + C)
                                act.activation(eb[:, :], xp[:, b, 0:L], ACT.Tanh).then_inc(g_e, 1)
                                act.wait_ge(g_g, LEAD + w + 1)
                                act.dma_start(*store(gs_s, i, b, gsb[:, b, :])).then_inc(g_sg[b], 16)
                        for b in range(2):
                            act.wait_ge(g_sg[b], LEAD + 16 * (DT // 2))

                    @block.vector
                    def _(v):
                        v.wait_ge(g_const, LEAD + 16)
                        with v.Fori(0, DT // 2) as i:
                            for b in range(2):
                                w = i * 2 + b
                                v.wait_ge(g_hi, LEAD + w + 1)
                                v.scalar_tensor_tensor(wlo[:, b, :], wraw[:, b, :], WS, whi[:, b, :],
                                                       ALU.mult, ALU.subtract).then_inc(g_lo, 1)
                                v.wait_ge(g_pre, LEAD + w + 1)
                                v.wait_ge(g_sd[b], LEAD + i * 32)
                                v.wait_ge(g_ab, LEAD + w * 2 + 1)
                                v.wait_ge(g_du, LEAD + w)
                                v.tensor_scalar(mx[:, b, :], four[:, :, :].rearrange("p c t -> p (c t)"),
                                                bd[:, bass.ds(w, 1)], 0.0, ALU.add, ALU.max).then_inc(g_mx, 1)
                                v.wait_ge(g_sp, LEAD + w + 1)
                                v.wait_ge(g_mx, LEAD + w + 1)
                                v.tensor_tensor(mx[:, b, :], mx[:, b, :], ab[:, :], ALU.add).then_inc(g_dt, 1)
                                v.wait_ge(g_e, LEAD + w + 1)
                                v.wait_ge(g_sg[b], LEAD + i * 16)
                                v.scalar_tensor_tensor(gsb[:, b, :], eb[:, :], 1.0, xp[:, b, 0:L],
                                                       ALU.add, ALU.mult).then_inc(g_g, 1)

                    @block.gpsimd
                    def _(pool):
                        with pool.Fori(0, DT // 2) as i:
                            for b in range(2):
                                w = i * 2 + b
                                pool.wait_ge(g_dt, LEAD + w + 1)
                                pool.wait_ge(g_u[b], LEAD + i * 16 + 16)
                                pool.tensor_tensor(du[:, b, :], mx[:, b, :], du[:, b, :], ALU.mult
                                                   ).then_inc(g_du, 1)

                    @block.tensor
                    def _(pe):
                        with pe.Fori(0, DT // 2) as i:
                            for b in range(2):
                                w = i * 2 + b
                                pe.wait_ge(g_wd[b], LEAD + i * 16 + 16)
                                pe.wait_ge(g_mx, LEAD + w)
                                for c in range(C):
                                    mm = pe.matmul(four[:, c, :], wd[:, b, :], tsb[0:R, c * T:(c + 1) * T],
                                                   start=True, stop=True)
                                mm.then_inc(g_pre, 1)
                                pe.wait_ge(g_lo, LEAD + w + 1)
                                for c in range(C):
                                    if b == 0:
                                        pe.wait_ge(g_ev, LEAD + w * C)
                                    else:
                                        pe.wait_ge(g_ev, LEAD + (w - 1) * C + c + 1)
                                    for k in range(HK):
                                        hi = whi[:, b, k * P:(k + 1) * P]
                                        lo = wlo[:, b, k * P:(k + 1) * P]
                                        xh = xhi[:, k, c * T:(c + 1) * T]
                                        xl = xlo[:, k, c * T:(c + 1) * T]
                                        pe.matmul(main[c][:, :], hi, xh, start=(k == 0), stop=False)
                                        pe.matmul(main[c][:, :], hi, xl, start=False, stop=False)
                                        mm = pe.matmul(main[c][:, :], lo, xh, start=False, stop=(k == HK - 1))
                                    mm.then_inc(g_mm, 1)

        with ExitStack() as st:
            bb = sb(st, "bb", [P, N, T])
            dtb = sb(st, "dtb", [P, J, T])
            dub = sb(st, "dub", [P, J, T])
            inj = sb(st, "inj", [P, 2, J, T])
            state = sb(st, "state", [P, J, T])
            ysum = sb(st, "ysum", [P, TPC, T])
            us = sb(st, "us", [P, J * T])
            gs = sb(st, "gs", [P, J * T])
            carry = sb(st, "carry", [P, DT, N])
            gsc = sb(st, "gsc", [P, 2, IT])
            wq = sb(st, "wq", [P, 2, 512], I32)
            w16 = sb(st, "w16", [P, 2, 2 * HK * P], F16)
            lrt = sb(st, "lrt", [P, T])
            gl = sb(st, "gl", [P, T])
            ul = sb(st, "ul", [P, T])
            ex = sb(st, "ex", [P, T])
            hh = sb(st, "hh", [P, 2, T], F16)
            decay = [pb(st, f"decay{b}", [P, T]) for b in range(2)]
            turned = [pb(st, f"turned{b}", [P, T]) for b in range(2)]
            bank = [pb(st, f"bank{m}", [P, T]) for m in range(2)]
            lrb = pb(st, "lrb", [P, T])
            us16 = us[:, :].bitcast(F16)

            (s_const, s_gsc, s_bb0, s_bb1, s_ffz, s_yhi, s_dt, s_du, s_us, s_gs, s_ys, s_dec, s_inj, s_scan, s_carry, s_turn, s_sum,
             s_yt, s_yev, s_gate, s_parts, s_wq0, s_wq1, s_conv, s_mm, s_lrt, s_gl, s_ul, s_ex, s_sg,
             s_h, s_hi, s_lo, s_hs, s_beat) = (sem("s_" + s) for s in (
                "const gsc bb0 bb1 ffz yhi dt du us gs ys dec inj scan carry turn sum yt yev gate parts wq0 wq1 conv "
                "mm lrt gl ul ex sg h hi lo hs beat").split())
            s_wq = [s_wq0, s_wq1]
            s_bb = [s_bb0, s_bb1]
            FF_STEPS = IT // 2

            def run_steps(step_fn, after_ff):
                for c in range(C):
                    ffs = min(max(FF_STEPS - c * G, 0), G)
                    loop = (1, G - 1)
                    step_fn(c, 0, ffs > 0)
                    with_ff = (loop[0], min(ffs, loop[1]))
                    if with_ff[0] < with_ff[1]:
                        yield c, with_ff, True
                    if c * G + ffs == FF_STEPS:
                        if ffs == G - 1:
                            after_ff()
                    if max(ffs, loop[0]) < loop[1]:
                        yield c, (max(ffs, loop[0]), loop[1]), False
                    step_fn(c, G - 1, ffs == G)

            def steps(eng, step_fn, after_ff=lambda: None):
                for c, (a, b), ff in run_steps(step_fn, after_ff):
                    with eng.Fori(a, b) as g:
                        step_fn(c, g, ff)

            def pairs(eng, step, ff, pair_fn, mid=lambda at: None):
                pair_fn(0, step * 2 if ff else None, 0)
                mid(0)
                pair_fn(1, step * 2 if ff else None, 1)
                mid(1)
                with eng.Fori(2, UNITS) as p:
                    pair_fn(p, step * 2 if ff else None, p)
                mid(2)
                with eng.Fori(0, UNITS) as p:
                    pair_fn(p + UNITS, step * 2 + 1 if ff else None, p)

            with nc.Block() as block:
                @block.sync
                def _(sp):
                    for m, src in enumerate((g_scale, u_scale)):
                        sp.dma_start(gsc[:, m, :], src).then_inc(s_const, 16)
                    for k in range(UNITS):
                        if k >= 2:
                            sp.wait_ge(s_conv, LEAD + k - 1)
                        sp.dma_start(wq[:, k % 2, :], gu_q[0, :, k * 512:(k + 1) * 512]).then_inc(s_wq[k % 2], 16)

                    def load_b(c, half):
                        n = slice(half * N // 2, (half + 1) * N // 2)
                        sp.dma_start(bb[:, n, :], bt_s[n, c * T:(c + 1) * T].partition_broadcast(P)
                                     ).then_inc(s_bb[half], 16)

                    def store_y(step):
                        sp.wait_ge(s_parts, LEAD + step + 1)
                        sp.dma_start(y_s[step], us16.rearrange("p (a t) -> p a t", a=2)).then_inc(s_ys, 16)

                    def step_fn(c, g, ff):
                        step = c * G + g
                        if c == 0 and isinstance(g, int) and g == 0:
                            load_b(0, 0)
                        else:
                            sp.wait_ge(s_dec, LEAD + step * (N * J))
                        sp.dma_start(dtb[:, :, :], dt_s[g, c]).then_inc(s_dt, 16)
                        if not (c == 0 and isinstance(g, int) and g == 0):
                            sp.wait_ge(s_inj, LEAD + step * N)
                        sp.dma_start(dub[:, :, :], du_s[g, c]).then_inc(s_du, 16)
                        if isinstance(g, int) and g == 0:
                            load_b(c, 1)

                        def pair(pr, i, p):
                            if i is None:
                                return
                            k = i * UNITS + p
                            sp.wait_ge(s_conv, LEAD + k + UNITS)
                            sp.dma_start(wq[:, p % 2, :], gu_q[i + 1, :, bass.ts(p, 512)]).then_inc(s_wq0, 16)
                            sp.wait_ge(s_lo, LEAD + k + 1)
                            sp.dma_start(h_s[k], hh[:, :, :]).then_inc(s_hs, 16)

                        def mid(at):
                            if at < 2:
                                return
                            if not (c == 0 and isinstance(g, int) and g == 0):
                                store_y(step - 1)
                                sp.wait_ge(s_ys, LEAD + step * 16)
                            sp.dma_start(us[:, :], u_s[g, c]).then_inc(s_us, 16)
                            sp.dma_start(gs[:, :], gs_s[g, c]).then_inc(s_gs, 16)
                            if isinstance(g, int) and g == G - 1 and c < C - 1:
                                sp.wait_ge(s_inj, LEAD + step * N + N // 2)
                                load_b(c + 1, 0)

                        pairs(sp, step, ff, pair, mid)

                    def after_ff():
                        sp.wait_ge(s_lo, LEAD + IT * UNITS + 1)
                        sp.dma_start(h_s[IT * UNITS], hh[:, :, :]).then_inc(s_hs, 16)

                    steps(sp, step_fn, after_ff)
                    store_y(C * G - 1)
                    sp.wait_ge(s_ys, LEAD + 16 * C * G)
                    sp.wait_ge(s_hs, LEAD + 16 * (IT * UNITS + 1))

                @block.scalar
                def _(act):
                    act.wait_ge(s_const, LEAD + 32)
                    for m, half in enumerate((0.5, 1.0)):
                        act.activation(gsc[:, m, :], gsc[:, m, :], ACT.Copy, scale=half * Q_STEP).then_inc(s_gsc, 1)
                    for k in range(UNITS):
                        act.wait_ge(s_wq[k % 2], LEAD + 16 * (k // 2 + 1))
                        act.activation(w16[:, 0, k * 512:(k + 1) * 512], wq[:, k % 2, :], ACT.Copy,
                                       bias=-Q_ZERO).then_inc(s_conv, 1)

                    def h_high(k):
                        act.wait_ge(s_h, LEAD + k + 1)
                        act.wait_ge(s_hs, LEAD + k * 16)
                        act.activation(hh[:, 0, :], ul[:, :], ACT.Copy).then_inc(s_hi, 1)

                    def y_high(step):
                        act.wait_ge(s_gate, LEAD + step + 1)
                        act.activation(us16[:, 0:J * T], gs[:, :], ACT.Copy).then_inc(s_yhi, 1)

                    def step_fn(c, g, ff):
                        step = c * G + g
                        act.wait_ge(s_dt, LEAD + step * 16 + 16)

                        def pair(pr, i, p):
                            for q in range(2):
                                slot = step * N + pr * 2 + q
                                for j in range(J):
                                    act.wait_ge(s_scan, LEAD + slot * J + j + EXTRA - 1)
                                    act.activation(decay[j % 2][:, :], dtb[:, j, :], ACT.Exp,
                                                   scale=aneg[:, g * J + j, bass.ds(pr * 2 + q, 1)]
                                                   ).then_inc(s_dec, 1)
                                if i is not None:
                                    k = i * UNITS + p
                                    if q == 0:
                                        h_high(k)
                                        act.wait_ge(s_wq0, LEAD + k * 16 + 48)
                                        act.wait_ge(s_mm, LEAD + i * (2 * UNITS))
                                        act.activation(w16[:, (i + 1) % 2, bass.ts(p, 512)], wq[:, p % 2, :],
                                                       ACT.Copy, bias=-Q_ZERO).then_inc(s_conv, 1)
                                    else:
                                        act.wait_ge(s_gl, LEAD + k + 1)
                                        act.wait_ge(s_sg, LEAD + k)
                                        act.activation(ex[:, :], gl[:, :], ACT.Tanh).then_inc(s_ex, 1)
                                        low_rank(k, q)
                                act.wait_ge(s_scan, LEAD + slot * J + J + EXTRA)
                                act.activation(carry[:, bass.ds(g * J, J), bass.ds(pr * 2 + q, 1)],
                                               state[:, :, T - 1:T], ACT.Copy).then_inc(s_carry, 1)
                                if i is not None and q == 0:
                                    low_rank(k, q)

                        def low_rank(k, q):
                            act.wait_ge(s_mm, LEAD + k * 2 + q + 1)
                            act.wait_ge((s_ul, s_gl)[q], LEAD + k + q)
                            act.activation(lrt[:, :], lrb[:, :], ACT.Copy,
                                           scale=(0.5, 1.0)[q] * LR_SCALE / WS).then_inc(s_lrt, 1)

                        def mid(at):
                            if at == 1 and not (c == 0 and isinstance(g, int) and g == 0):
                                y_high(step - 1)

                        pairs(act, step, ff, pair, mid)

                    steps(act, step_fn, lambda: h_high(IT * UNITS))
                    y_high(C * G - 1)

                @block.vector
                def _(v):
                    v.memset(carry[:, :, :], 0.0).then_inc(s_carry, 1)
                    v.sem_inc(s_scan, EXTRA)
                    v.sem_inc(s_sum, J)
                    v.sem_inc(s_yev, 2)
                    v.wait_ge(s_gsc, LEAD + 2)
                    v.wait_ge(s_carry, LEAD + 1)

                    def step_fn(c, g, ff):
                        step = c * G + g

                        def scan(slot, q, n, j):
                            v.wait_ge(s_dec, LEAD + slot * J + j + 1)
                            v.tensor_tensor_scan(state[:, j, :], decay[j % 2][:, :], inj[:, q, j, :],
                                                 carry[:, g * J + j, n], ALU.mult, ALU.add).then_inc(s_scan, 1)

                        def pair(pr, i, p):
                            for q in range(2):
                                slot = step * N + pr * 2 + q
                                n = bass.ds(pr * 2 + q, 1)
                                v.wait_ge(s_inj, LEAD + slot + 1)
                                v.wait_ge(s_carry, LEAD + slot + 1)
                                v.wait_ge(s_turn, LEAD + slot * TPC)
                                scan(slot, q, n, 0)
                                scan(slot, q, n, 1)
                                if i is not None and q == 1:
                                    k = i * UNITS + p
                                    v.wait_ge(s_lrt, LEAD + k * 2 + 1)
                                    v.wait_ge(s_h, LEAD + k + 1)
                                    v.scalar_tensor_tensor(gl[:, :], bank[0][:, :], gsc[:, 0, bass.ds(i, 1)],
                                                           lrt[:, :], ALU.mult, ALU.add).then_inc(s_gl, 1)
                                scan(slot, q, n, 2)
                                scan(slot, q, n, 3)
                                if i is not None and q == 1:
                                    v.wait_ge(s_lrt, LEAD + k * 2 + 2)
                                    v.wait_ge(s_lo, LEAD + k + 1)
                                    v.scalar_tensor_tensor(ul[:, :], bank[1][:, :], gsc[:, 1, bass.ds(i, 1)],
                                                           lrt[:, :], ALU.mult, ALU.add).then_inc(s_ul, 1)
                                    v.wait_ge(s_ex, LEAD + k + 1)
                                    v.scalar_tensor_tensor(gl[:, :], ex[:, :], 1.0, gl[:, :],
                                                           ALU.add, ALU.mult).then_inc(s_sg, 1)
                                for t in range(TPC):
                                    v.wait_ge(s_turn, LEAD + slot * TPC + t + 1)
                                    v.wait_ge(s_sum, LEAD + slot * TPC + t + 1)
                                    if q == 0 and isinstance(pr, int) and pr == 0:
                                        v.tensor_scalar(ysum[:, t, :], turned[t % 2][:, :],
                                                        cT[:, c * TPC + t, n], None, ALU.mult).then_inc(s_sum, 1)
                                    else:
                                        v.scalar_tensor_tensor(ysum[:, t, :], turned[t % 2][:, :],
                                                               cT[:, c * TPC + t, n], ysum[:, t, :],
                                                               ALU.mult, ALU.add).then_inc(s_sum, 1)

                        pairs(v, step, ff, pair)
                        v.wait_ge(s_us, LEAD + step * 16 + 16)
                        for j in range(J):
                            v.wait_ge(s_yt, LEAD + step * J + j + 1)
                            v.scalar_tensor_tensor(us[:, j * T:(j + 1) * T], us[:, j * T:(j + 1) * T],
                                                   dsk[:, bass.ds(g * J + j, 1)], turned[j % 2][:, :],
                                                   ALU.mult, ALU.add).then_inc(s_yev, 1)

                    steps(v, step_fn)

                @block.gpsimd
                def _(pool):
                    pool.memset(gl[:, :], 0.0).then_inc(s_ffz, 1)
                    pool.memset(ul[:, :], 0.0).then_inc(s_ffz, 1)
                    pool.wait_ge(s_ffz, LEAD + 2)

                    def h_product(k):
                        pool.wait_ge(s_sg, LEAD + k)
                        pool.tensor_tensor(ul[:, :], gl[:, :], ul[:, :], ALU.mult).then_inc(s_h, 1)

                    def h_low(k):
                        pool.wait_ge(s_hi, LEAD + k + 1)
                        pool.tensor_tensor(hh[:, 1, :], ul[:, :], hh[:, 0, :], ALU.subtract).then_inc(s_lo, 1)

                    def y_gate(step):
                        pool.wait_ge(s_yev, LEAD + step * J + J + 2)
                        pool.wait_ge(s_gs, LEAD + step * 16 + 16)
                        pool.tensor_tensor(gs[:, :], us[:, :], gs[:, :], ALU.mult).then_inc(s_gate, 1)

                    def y_low(step):
                        pool.wait_ge(s_yhi, LEAD + step + 1)
                        pool.tensor_tensor(us16[:, J * T:2 * J * T], gs[:, :], us16[:, 0:J * T], ALU.subtract
                                           ).then_inc(s_parts, 1)

                    def step_fn(c, g, ff):
                        step = c * G + g
                        pool.wait_ge(s_bb[0], LEAD + c * 16 + 16)
                        pool.wait_ge(s_du, LEAD + step * 16 + 16)

                        def pair(pr, i, p):
                            for q in range(2):
                                slot = step * N + pr * 2 + q
                                pool.wait_ge(s_scan, LEAD + slot * J + EXTRA - J)
                                pool.tensor_tensor(inj[:, q, :, :], dub[:, :, :],
                                                   bb[:, bass.ds(pr * 2 + q, 1), :].broadcast_to([P, J, T]),
                                                   ALU.mult).then_inc(s_inj, 1)
                                if i is not None:
                                    (h_product, h_low)[q](i * UNITS + p)

                        def mid(at):
                            if at < 2 and not (c == 0 and isinstance(g, int) and g == 0):
                                (y_gate, y_low)[at](step - 1)
                            if at == 2:
                                pool.wait_ge(s_bb[1], LEAD + c * 16 + 16)
                                pool.sem_inc(s_beat, 1)

                        pairs(pool, step, ff, pair, mid)

                    def after_ff():
                        h_product(IT * UNITS)
                        h_low(IT * UNITS)

                    steps(pool, step_fn, after_ff)
                    y_gate(C * G - 1)
                    y_low(C * G - 1)

                @block.tensor
                def _(pe):
                    def step_fn(c, g, ff):
                        step = c * G + g

                        def turn(slot, t):
                            pe.wait_ge(s_sum, LEAD + slot * TPC + t + 3)
                            for j in range(J):
                                mm = pe.transpose(turned[t % 2][:, j * P:(j + 1) * P],
                                                  state[:, j, t * P:(t + 1) * P], ident[:, :])
                            mm.then_inc(s_turn, 1)

                        def products(i, p, q, h0, h1):
                            for h in range(h0, h1):
                                w = w16[:, i % 2, (q * HK + h) * P:(q * HK + h + 1) * P]
                                pe.matmul(bank[q][:, :], w, xhi[:, h, bass.ts(p, T)],
                                          start=(h == 0), stop=False)
                                pe.matmul(bank[q][:, :], w, xlo[:, h, bass.ts(p, T)],
                                          start=False, stop=(h == HK - 1))

                        def low_rank(i, p, q):
                            pe.wait_ge(s_lrt, LEAD + (i * UNITS + p) * 2 + q)
                            pe.matmul(lrb[:, :], btab[:, q, bass.ts(i, P)], xa[:, q, bass.ts(p, T)],
                                      start=True, stop=True).then_inc(s_mm, 1)

                        def pair(pr, i, p):
                            slot = step * N + pr * 2
                            if i is not None:
                                k = i * UNITS + p
                                pe.wait_ge(s_conv, LEAD + i * UNITS + UNITS)
                                pe.wait_ge(s_gl, LEAD + k)
                                products(i, p, 0, 0, 6)
                            pe.wait_ge(s_scan, LEAD + slot * J + J + EXTRA)
                            pe.wait_ge(s_yev, LEAD + step * J + 2)
                            turn(slot, 0)
                            turn(slot, 1)
                            if i is not None:
                                products(i, p, 0, 6, HK)
                                low_rank(i, p, 0)
                            turn(slot, 2)
                            if i is not None:
                                pe.wait_ge(s_ul, LEAD + k)
                                products(i, p, 1, 0, 2)
                            turn(slot, 3)
                            if i is not None:
                                products(i, p, 1, 2, HK)
                                low_rank(i, p, 1)
                            pe.wait_ge(s_scan, LEAD + slot * J + 2 * J + EXTRA)
                            for t in range(TPC):
                                turn(slot + 1, t)

                        pairs(pe, step, ff, pair)
                        pe.wait_ge(s_sum, LEAD + step * (N * TPC) + N * TPC + J)
                        for j in range(J):
                            pe.wait_ge(s_yev, LEAD + step * J + j + 1)
                            for t in range(TPC):
                                mm = pe.transpose(turned[j % 2][:, t * P:(t + 1) * P],
                                                  ysum[:, t, j * P:(j + 1) * P], ident[:, :])
                            mm.then_inc(s_yt, 1)

                    steps(pe, step_fn)
        upto_scan.close()

        with ExitStack() as st:
            wo_hi = sb(st, "wo_hi", [P, DT, H], F16)
            wo_lo = sb(st, "wo_lo", [P, DT, H], F16)
            dw = sb(st, "dw", [P, IT, H], F16)
            da_hi = sb(st, "da_hi", [P, IT, 3 * LR], F16)
            da_lo = sb(st, "da_lo", [P, IT, 3 * LR], F16)
            db = sb(st, "db", [3 * LR, H], F16)
            raw = sb(st, "raw", [P, 2, H])
            rawi = sb(st, "rawi", [P, 2, H], I32)
            dar = sb(st, "dar", [P, IT, LR])
            dbr = sb(st, "dbr", [3 * LR, H])
            dscale = sb(st, "dscale", [P, H])
            hc = sb(st, "hc", [P, 2, IT, 2, P], F16)
            yc = sb(st, "yc", [P, 2, G, 2, J, P], F16)
            ha = sb(st, "ha", [3 * LR, P], F16)
            xr = sb(st, "xr", [P, H])
            f1 = sb(st, "f1", [P, H])
            f2 = sb(st, "f2", [P, H])
            po = pb(st, "po", [P, 2, 512])
            pd = pb(st, "pd", [P, 2, 512])
            pl = pb(st, "pl", [P, 2, 512])
            pa = pb(st, "pa", [P, P])
            o_r = [sem(f"o_r{b}") for b in range(2)]
            o_q = [sem(f"o_q{b}") for b in range(2)]
            (o_c, o_ds, o_hi, o_lo, o_dw, o_dah, o_dal, o_dbh, o_dbl, o_h0, o_h1, o_y0, o_y1, o_x, o_ha, o_hah, o_hal, o_pl,
             o_pd, o_po, o_l, o_f, o_e, o_out, o_st) = (sem("o_" + s) for s in (
                "c ds hi lo dw dah dal dbh dbl h0 h1 y0 y1 x ha hah hal pl pd po l f e out st").split())
            o_h, o_y = (o_h0, o_h1), (o_y0, o_y1)
            flat = "p a b -> p (a b)"
            with nc.Block() as block:

                @block.sync
                def _(sp):
                    sp.dma_start(dar[:, :, :], d_a).then_inc(o_c, 16)
                    for r in range(3):
                        sp.dma_start(dbr[r * LR:(r + 1) * LR, :], d_b).then_inc(o_c, 16)
                    sp.dma_start(dscale[:, :], d_scale.partition_broadcast(P)).then_inc(o_c, 16)
                    with sp.Fori(0, DT // 2) as i:
                        for b in range(2):
                            sp.wait_ge(o_lo, LEAD + i * 2 + b)
                            sp.dma_start(raw[:, b, :], wout[i * 2 + b]).then_inc(o_r[b], 16)
                    with sp.Fori(0, IT // 2) as i:
                        for b in range(2):
                            sp.wait_ge(o_dw, LEAD + i * 2 + b)
                            sp.dma_start(rawi[:, b, :], dq[i * 2 + b]).then_inc(o_q[b], 16)
                    units = h_s[1:, :, :, :].rearrange("(i c) p a t -> c p i a t", c=C)

                    def load(c, t, b):
                        for part in range(2):
                            sp.dma_start(hc[:, b, :, part, :],
                                         units[c, :, :, part, t * P:(t + 1) * P]).then_inc(o_h[b], 16)
                        for g in range(G):
                            sp.dma_start(yc[:, b, g, :, :, :].rearrange("p a j t -> p (a j) t"),
                                         y_s[c * G + g].rearrange("p a (j t) -> p (a j) t", j=J)[
                                             :, :, t * P:(t + 1) * P]).then_inc(o_y[b], 16)

                    def tiles(c, c_next):
                        for t in range(TPC):
                            tt = c * TPC + t
                            if t < TPC - 1 or c_next is not None:
                                sp.wait_ge(o_pl, LEAD + tt)
                                load(*((c, t + 1) if t < TPC - 1 else (c_next, 0)), (t + 1) % 2)
                            sp.wait_ge(o_st, LEAD + tt * 16)
                            sp.dma_start(xr[:, :], x[tt]).then_inc(o_x, 16)
                            sp.wait_ge(o_out, LEAD + tt + 1)
                            sp.dma_start(out[tt], xr[:, :]).then_inc(o_st, 16)

                    load(0, 0, 0)
                    with sp.Fori(0, C - 1) as c:
                        tiles(c, c + 1)
                    tiles(C - 1, None)
                    sp.wait_ge(o_st, LEAD + 16 * TT)

                @block.scalar
                def _(act):
                    act.wait_ge(o_c, LEAD + 80)
                    for r in range(3):
                        act.activation(da_hi[:, :, r * LR:(r + 1) * LR], dar[:, :, :], ACT.Copy).then_inc(o_dah, 1)
                    act.activation(db[:, :], dbr[:, :], ACT.Copy, scale=WS).then_inc(o_dbh, 1)
                    act.activation(dscale[:, :], dscale[:, :], ACT.Copy, scale=0.5 * Q_STEP).then_inc(o_ds, 1)
                    with act.Fori(0, DT // 2) as i:
                        for b in range(2):
                            act.wait_ge(o_r[b], LEAD + i * 16 + 16)
                            act.activation(wo_hi[:, bass.ds(i * 2 + b, 1), :], raw[:, bass.ds(b, 1), :], ACT.Copy,
                                           scale=WS).then_inc(o_hi, 1)
                    with act.Fori(0, IT // 2) as i:
                        for b in range(2):
                            act.wait_ge(o_q[b], LEAD + i * 16 + 16)
                            act.activation(dw[:, bass.ds(i * 2 + b, 1), :], rawi[:, bass.ds(b, 1), :], ACT.Copy,
                                           bias=-Q_ZERO).then_inc(o_dw, 1)
                    with act.Fori(0, TT) as t:
                        act.wait_ge(o_ha, LEAD + t + 1)
                        act.wait_ge(o_pl, LEAD + t)
                        act.activation(ha[:, :], pa[0:3 * LR, :], ACT.Copy).then_inc(o_hah, 1)
                        act.wait_ge(o_pl, LEAD + t + 1)
                        act.wait_ge(o_out, LEAD + t)
                        act.activation(f2[:, :], pl[:, :, :].rearrange(flat), ACT.Copy,
                                       scale=0.5 * LR_SCALE / WS).then_inc(o_l, 1)
                        act.wait_ge(o_f, LEAD + t * 2 + 2)
                        act.activation(f2[:, :], f1[:, :], ACT.Tanh).then_inc(o_e, 1)

                @block.vector
                def _(v):
                    v.wait_ge(o_dah, LEAD + 3)
                    for r in range(3):
                        v.tensor_tensor(da_lo[:, :, r * LR:(r + 1) * LR], dar[:, :, :],
                                        da_hi[:, :, r * LR:(r + 1) * LR], ALU.subtract).then_inc(o_dal, 1)
                    v.wait_ge(o_dbh, LEAD + 1)
                    v.scalar_tensor_tensor(db[2 * LR:3 * LR, :], dbr[2 * LR:3 * LR, :], WS, db[2 * LR:3 * LR, :],
                                           ALU.mult, ALU.subtract).then_inc(o_dbl, 1)
                    with v.Fori(0, DT) as i:
                        v.wait_ge(o_hi, LEAD + i + 1)
                        v.scalar_tensor_tensor(wo_lo[:, bass.ds(i, 1), :], raw[:, bass.ds(i % 2, 1), :], WS,
                                               wo_hi[:, bass.ds(i, 1), :], ALU.mult, ALU.subtract
                                               ).then_inc(o_lo, 1)
                    v.wait_ge(o_ds, LEAD + 1)
                    with v.Fori(0, TT) as t:
                        v.wait_ge(o_hah, LEAD + t + 1)
                        v.tensor_tensor(ha[LR:2 * LR, :], pa[LR:2 * LR, :], ha[LR:2 * LR, :], ALU.subtract
                                        ).then_inc(o_hal, 1)
                        v.wait_ge(o_pd, LEAD + t + 1)
                        v.wait_ge(o_out, LEAD + t)
                        v.tensor_tensor(f1[:, :], pd[:, :, :].rearrange(flat), dscale[:, :], ALU.mult
                                        ).then_inc(o_f, 1)
                        v.wait_ge(o_l, LEAD + t + 1)
                        v.wait_ge(o_f, LEAD + t * 2 + 1)
                        v.tensor_tensor(f1[:, :], f1[:, :], f2[:, :], ALU.add).then_inc(o_f, 1)
                        v.wait_ge(o_e, LEAD + t + 1)
                        v.scalar_tensor_tensor(f1[:, :], f2[:, :], 1.0, f1[:, :], ALU.add, ALU.mult).then_inc(o_hal, 1)
                        v.wait_ge(o_hal, LEAD + t * 3 + 2)
                        v.wait_ge(o_po, LEAD + t + 1)
                        v.scalar_tensor_tensor(f1[:, :], po[:, :, :].rearrange(flat), 1.0 / WS, f1[:, :],
                                               ALU.mult, ALU.mult).then_inc(o_hal, 1)
                        v.wait_ge(o_hal, LEAD + t * 3 + 3)
                        v.wait_ge(o_x, LEAD + t * 16 + 16)
                        v.tensor_tensor(xr[:, :], xr[:, :], f1[:, :], ALU.add).then_inc(o_out, 1)

                @block.tensor
                def _(pe):
                    pe.wait_ge(o_dal, LEAD + 3)
                    pe.wait_ge(o_dbl, LEAD + 1)
                    pe.wait_ge(o_lo, LEAD + DT)
                    pe.wait_ge(o_dw, LEAD + IT)
                    with pe.Fori(0, TT // 2) as pair:
                        for b in range(2):
                            t = pair * 2 + b
                            pe.wait_ge(o_h[b], LEAD + pair * 32 + 32)
                            pe.wait_ge(o_hal, LEAD + t * 3)
                            for i in range(IT):
                                for z, (a, part) in enumerate(((da_hi, 0), (da_hi, 1), (da_lo, 0))):
                                    mm = pe.matmul(pa[0:3 * LR, :], a[:, i, :], hc[:, b, i, part, :],
                                                   start=(i == 0 and z == 0), stop=(i == IT - 1 and z == 2))
                            mm.then_inc(o_ha, 1)
                            pe.wait_ge(o_f, LEAD + t * 2)
                            for half in range(2):
                                cols = slice(half * 512, half * 512 + 512)
                                for i in range(IT):
                                    for part in range(2):
                                        mm = pe.matmul(pd[:, half, :], hc[:, b, i, part, :], dw[:, i, cols],
                                                       start=(i == 0 and part == 0), stop=(i == IT - 1 and part == 1))
                            mm.then_inc(o_pd, 1)
                            pe.wait_ge(o_y[b], LEAD + pair * (16 * G) + 16 * G)
                            pe.wait_ge(o_out, LEAD + t)
                            for half in range(2):
                                cols = slice(half * 512, half * 512 + 512)
                                for i in range(DT):
                                    for z, (part, w) in enumerate(((0, wo_hi), (1, wo_hi), (0, wo_lo))):
                                        mm = pe.matmul(po[:, half, :], yc[:, b, i // J, part, i % J, :], w[:, i, cols],
                                                       start=(i == 0 and z == 0), stop=(i == DT - 1 and z == 2))
                            mm.then_inc(o_po, 1)
                            pe.wait_ge(o_hal, LEAD + t * 3 + 1)
                            pe.wait_ge(o_l, LEAD + t)
                            for half in range(2):
                                cols = slice(half * 512, half * 512 + 512)
                                mm = pe.matmul(pl[:, half, :], ha[:, :], db[:, cols], start=True, stop=True)
                            mm.then_inc(o_pl, 1)


def kernel(L0_attn_hidden_states, L0_attn_W_in, L0_attn_conv_w, L0_attn_conv_b, L0_attn_W_x, L0_attn_W_dt,
           L0_attn_b_dt, L0_attn_A_log, L0_attn_D, L0_attn_W_out, L0_ffn_gate_q, L0_ffn_gate_scale,
           L0_ffn_gate_A, L0_ffn_gate_B, L0_ffn_up_q, L0_ffn_up_scale, L0_ffn_up_A, L0_ffn_up_B,
           L0_ffn_down_q, L0_ffn_down_scale, L0_ffn_down_A, L0_ffn_down_B):
    import numpy as np
    import concourse.bacc as bacc
    from concourse.bass_utils import run_bass_kernel_spmd as run

    def arr(a):
        return np.ascontiguousarray(np.asarray(a))

    def rows(a, n):
        a = np.asarray(a)
        return np.concatenate([a, np.zeros((n - a.shape[0],) + a.shape[1:], a.dtype)])

    def qtiles(q):
        return rows(q, IPAD).reshape(IT, P, HK, P).transpose(0, 3, 2, 1).reshape(IT, P, HK * P)

    def cols(a):
        return np.asarray(a).reshape(DT, P).T

    gu = np.concatenate([qtiles(L0_ffn_gate_q), qtiles(L0_ffn_up_q)], axis=2)
    ins = dict(
        x=np.asarray(L0_attn_hidden_states).reshape(TT, P, H),
        win=np.asarray(L0_attn_W_in).reshape(2 * DT, P, HK, P).transpose(0, 3, 2, 1).reshape(2 * DT, P, HK * P),
        convw=np.asarray(L0_attn_conv_w).reshape(DT, P, K).transpose(1, 0, 2),
        convb=cols(L0_attn_conv_b),
        wx=np.asarray(L0_attn_W_x).T.reshape(DT, P, S3).transpose(1, 0, 2),
        wdt=np.asarray(L0_attn_W_dt).reshape(DT, P, R).transpose(0, 2, 1),
        bdt=cols(L0_attn_b_dt),
        alog=np.asarray(L0_attn_A_log).reshape(DT, P, N).transpose(1, 0, 2),
        dskip=cols(L0_attn_D),
        wout=np.asarray(L0_attn_W_out).T.reshape(DT, P, H),
        gu_q=rows(gu, IT + 1),
        g_scale=rows(L0_ffn_gate_scale, IPAD).reshape(IT, P).T,
        u_scale=rows(L0_ffn_up_scale, IPAD).reshape(IT, P).T,
        lr_a=np.stack([np.asarray(a).reshape(HK, P, LR).transpose(1, 0, 2) for a in (L0_ffn_gate_A, L0_ffn_up_A)]),
        g_b=rows(np.asarray(L0_ffn_gate_B).T, IPAD).T,
        u_b=rows(np.asarray(L0_ffn_up_B).T, IPAD).T,
        dq=rows(np.asarray(L0_ffn_down_q).T, IPAD).reshape(IT, P, H),
        d_scale=np.asarray(L0_ffn_down_scale),
        d_a=rows(L0_ffn_down_A, IPAD).reshape(IT, P, LR).transpose(1, 0, 2),
        d_b=np.asarray(L0_ffn_down_B),
        ident_in=np.eye(P, dtype=np.float32),
    )
    nc = bacc.Bacc("TRN2", target_bir_lowering=False, num_devices=1)
    arrays, args = {}, []
    for name, a in ins.items():
        arrays["in_" + name] = arr(a)
        args.append(nc.dram_tensor("in_" + name, a.shape, mybir.dt.from_np(a.dtype), kind="ExternalInput").ap())
    args.append(nc.dram_tensor("out_0", (TT, P, H), F32, kind="ExternalOutput").ap())
    for name, shape, dt in (("u_s", (G, C, P, J, T), F32), ("gs_s", (G, C, P, J, T), F32),
                            ("dt_s", (G, C, P, J, T), F32), ("du_s", (G, C, P, J, T), F32),
                            ("bt_s", (N, L), F32), ("h_s", (1 + IT * UNITS, P, 2, T), F16),
                            ("y_s", (C * G, P, 2, J * T), F16)):
        args.append(nc.dram_tensor(name, shape, dt, kind="Internal").ap())
    mixer_kernel(nc, *args)
    r = run(nc, [arrays], core_ids=[0])
    return r.results[0]["out_0"].reshape(1, L, H)
```

```python
from contextlib import ExitStack

import concourse.bass as bass
from concourse import mybir

F32 = mybir.dt.float32
F16 = mybir.dt.float16
I32 = mybir.dt.int32
ALU = mybir.AluOpType
ACT = mybir.ActivationFunctionType
AX = mybir.AxisListType

P = 128
L, H, DI, N, R, K, I, LR = 2048, 1024, 2048, 16, 64, 4, 2752, 32
T = 512
C = L // T
TT = L // P
TPC = T // P
HK = H // P
DT = DI // P
J = 4
G = DT // J
IT = -(-I // P)
IPAD = IT * P
S3 = R + 2 * N
WS = 256.0
Q_ZERO, Q_STEP, LR_SCALE = 7.5, 0.005, 0.02
UNITS = C
LEAD = 1
SEMAPHORES = (
    "n_x0 n_x1 n_const n_st n_ag n_rs n_xn n_tp n_hi n_lo n_a n_var n_sd i_w0 i_w1 i_st0 i_st1 i_const i_z "
    "i_hi i_lo i_mm i_ev i_cv i_e i_u i_ssm i_sm i_half r_a r_b r_v r_sm r_tp r_tb r_st r_ah r_al r_xa r_xh "
    "r_xl r_bh r_bl r_sd g_w0 g_w1 g_wd0 g_wd1 g_sg0 g_sg1 g_sd0 g_sd1 g_u0 g_u1 g_const g_hi g_lo g_mm g_ev "
    "g_e g_g g_pre g_mx g_ab g_sp g_dt g_du s_const s_gsc s_bb0 s_bb1 s_ffz s_yhi s_inj_half s_dt0 s_dt1 "
    "s_du0 s_du1 s_us s_gs s_ys s_dec s_inj s_scan s_carry s_turn s_sum s_yt s_yev s_gate s_parts s_wq0 s_wq1 "
    "s_conv s_mm s_lrt s_gl s_ul s_ex s_sg s_h s_hi s_lo s_hs s_beat t_raw t_hi t_lo t_y t_mm t_ev t_st o_q0 "
    "o_q1 o_q2 o_s o_m o_c o_ds o_dw o_dah o_dal o_dbh o_dbl o_h0 o_h1 o_y0 o_y1 o_x o_ha o_hah o_hal o_pl "
    "o_pd o_po o_l o_f o_e o_out o_st "
).split()
EXTRA = 8


def mixer_kernel(nc, x, win, convw, convb, wx, wdt, bdt, alog, dskip, wout, gu_q, g_scale, u_scale,
                 lr_a, g_b, u_b, dq, d_scale, d_a, d_b, ident_in, out,
                 u_s, gs_s, dt_s, du_s, bt_s, h_s, y_s, s_s):
    whole = ExitStack()
    with whole:
        def sb(stack, name, shape, dt=F32):
            return stack.enter_context(nc.sbuf_tensor(name, shape, dt))

        def pb(stack, name, shape, dt=F32):
            return stack.enter_context(nc.psum_tensor(name, shape, dt))

        semaphores = {name: whole.enter_context(nc.semaphore(name)) for name in SEMAPHORES}
        sem = semaphores.__getitem__

        def start_semaphores(eng, share):
            for name in SEMAPHORES[share::4]:
                eng.sem_inc(semaphores[name], LEAD)

        with nc.Block() as block:
            @block.gpsimd
            def _(pool):
                start_semaphores(pool, 0)

            @block.scalar
            def _(act):
                start_semaphores(act, 1)

            @block.vector
            def _(v):
                start_semaphores(v, 2)

            @block.sync
            def _(sp):
                start_semaphores(sp, 3)

        ident = sb(whole, "ident", [P, P])
        aneg = sb(whole, "aneg", [P, DT, N])
        cT = sb(whole, "cT", [P, TT, N])
        dsk = sb(whole, "dsk", [P, DT])
        xhi = sb(whole, "xhi", [P, HK, L], F16)
        xlo = sb(whole, "xlo", [P, HK, L], F16)
        wo_hi, wo_lo = (a[:, :, :].rearrange("p k t -> p (k t)").rearrange("p (i n) -> p i n", n=H)
                        for a in (xhi, xlo))
        upto_scan = whole.enter_context(ExitStack())
        xa = sb(upto_scan, "xa", [3 * LR, 2, L], F16)
        btab = sb(upto_scan, "btab", [3 * LR, 2, IPAD], F16)

        with ExitStack() as st:
            B4 = 4
            xt = [sb(st, f"xt{b}", [P, B4, H]) for b in range(2)]
            xn = [sb(st, f"xn{b}", [P, H]) for b in range(2)]
            stats = sb(st, "stats", [P, B4, 2, 6])
            mv = sb(st, "mv", [P, B4, 2])
            var = sb(st, "var", [P, B4, 1])
            rstd = sb(st, "rstd", [P, B4, 1])
            al = sb(st, "al", [P, DT, N])
            xtp = [pb(st, f"xtp{b}", [P, HK, P]) for b in range(3)]
            n_x = [sem(f"n_x{b}") for b in range(2)]
            (n_const, n_st, n_ag, n_rs, n_xn, n_tp, n_hi, n_lo, n_a, n_var, n_sd) = (
                sem(s) for s in ("n_const", "n_st", "n_ag", "n_rs", "n_xn", "n_tp", "n_hi", "n_lo", "n_a",
                                 "n_var", "n_sd"))
            with nc.Block() as block:
                @block.sync
                def _(sp):
                    for b in range(2):
                        sp.dma_start(xt[b][:, :, :], x[b * B4:(b + 1) * B4].rearrange("t p h -> p t h")
                                     ).then_inc(n_x[b], 16)
                    sp.dma_start(ident[:, :], ident_in).then_inc(n_const, 16)
                    sp.dma_start(al[:, :, :], alog).then_inc(n_const, 16)
                    sp.dma_start(dsk[:, :], dskip).then_inc(n_const, 16)
                    for b in range(2):
                        sp.wait_ge(n_xn, LEAD + (b + 1) * B4)
                        sp.dma_start(xt[b][:, :, :], x[(b + 2) * B4:(b + 3) * B4].rearrange("t p h -> p t h")
                                     ).then_inc(n_x[b], 16)

                @block.vector
                def _(v):
                    def low(t):
                        v.wait_ge(n_hi, LEAD + t + 1)
                        tok = slice(t * P, (t + 1) * P)
                        v.tensor_tensor(xlo[:, :, tok], xtp[t % 3][:, :, :], xhi[:, :, tok],
                                        ALU.subtract).then_inc(n_lo, 1)

                    for m in range(TT // B4):
                        b = m % 2
                        v.wait_ge(n_x[b], LEAD + 16 * (m // 2 + 1))
                        for t in range(B4):
                            for h in range(2):
                                v.bn_stats(stats[:, t, h, :], xt[b][:, t, h * 512:(h + 1) * 512]).then_inc(n_st, 1)
                        v.wait_ge(n_st, LEAD + 2 * B4 * (m + 1))
                        for t in range(B4):
                            v.bn_aggr(mv[:, t, :], stats[:, t, :, :].rearrange("p a s -> p (a s)")).then_inc(n_ag, 1)
                        v.wait_ge(n_ag, LEAD + B4 * (m + 1))
                        v.tensor_scalar(var[:, :, :], mv[:, :, 1:2], 1e-5, None, ALU.add).then_inc(n_var, 1)
                        if m:
                            low(m * B4 - 1)
                        v.wait_ge(n_sd, LEAD + m + 1)
                        v.reciprocal(rstd[:, :, :], var[:, :, :]).then_inc(n_rs, 1)
                        v.wait_ge(n_rs, LEAD + m + 1)
                        for t in range(B4):
                            n = m * B4 + t
                            if n >= 2:
                                v.wait_ge(n_tp, LEAD + n - 1)
                            v.tensor_scalar(xn[n % 2][:, :], xt[b][:, t, :], mv[:, t, 0:1], rstd[:, t, :],
                                            ALU.subtract, ALU.mult).then_inc(n_xn, 1)
                            if t:
                                low(n - 1)
                    low(TT - 1)

                @block.tensor
                def _(pe):
                    pe.wait_ge(n_const, LEAD + 48)
                    for n in range(TT):
                        pe.wait_ge(n_xn, LEAD + n + 1)
                        if n >= 3:
                            pe.wait_ge(n_lo, LEAD + n - 2)
                        for k in range(HK):
                            mm = pe.transpose(xtp[n % 3][:, k, :], xn[n % 2][:, k * P:(k + 1) * P], ident[:, :])
                        mm.then_inc(n_tp, 1)

                @block.scalar
                def _(act):
                    def high(n):
                        act.wait_ge(n_tp, LEAD + n + 1)
                        act.activation(xhi[:, :, n * P:(n + 1) * P], xtp[n % 3][:, :, :],
                                       ACT.Copy).then_inc(n_hi, 1)

                    for m in range(TT // B4):
                        act.wait_ge(n_var, LEAD + m + 1)
                        act.activation(var[:, :, :], var[:, :, :], ACT.Sqrt).then_inc(n_sd, 1)
                        for t in range(B4):
                            high(m * B4 + t)
                    act.wait_ge(n_const, LEAD + 48)
                    act.activation(al[:, :, :], al[:, :, :], ACT.Exp).then_inc(n_a, 1)
                    act.wait_ge(n_a, LEAD + 1)
                    act.mul(aneg[:, :, :], al[:, :, :], -1.0).then_inc(n_a, 1)

        proj = ExitStack()
        with proj:
            wraw = sb(proj, "wraw", [P, 2, HK * P])
            whi = sb(proj, "whi", [P, 2, HK * P], F16)
            wlo = sb(proj, "wlo", [P, 2, HK * P], F16)
            xp = sb(proj, "xp", [P, 2, L + K - 1])
            eb = sb(proj, "eb", [P, L])
            sm = sb(proj, "sm", [P, TT, S3])
            main = [pb(proj, f"main{t}", [P, T]) for t in range(C)]
            four = pb(proj, "four", [P, C, T])

            with ExitStack() as st:
                xc = sb(st, "xc", [P, 2, L])
                ub = sb(st, "ub", [P, 2, L])
                zero = sb(st, "zero", [P, T])
                wx_sb = sb(st, "wx_sb", [P, DT, S3])
                cw = sb(st, "cw", [P, DT, K])
                cb = sb(st, "cb", [P, DT])
                i_w = [sem(f"i_w{b}") for b in range(2)]
                (i_const, i_z, i_hi, i_lo, i_mm, i_ev, i_cv, i_e, i_u, i_ssm, i_sm, i_half) = (
                    sem(s) for s in ("i_const", "i_z", "i_hi", "i_lo", "i_mm", "i_ev", "i_cv",
                                     "i_e", "i_u", "i_ssm", "i_sm", "i_half"))
                i_st = [sem(f"i_st{b}") for b in range(2)]
                with nc.Block() as block:

                    @block.sync
                    def _(sp):
                        sp.dma_start(wraw[:, 0, :], win[0]).then_inc(i_w[0], 16)
                        for dst, src in ((wx_sb, wx), (cw, convw), (cb, convb)):
                            sp.dma_start(dst[:], src).then_inc(i_const, 16)
                        with sp.Fori(0, DT // 2) as i:
                            for b in range(2):
                                w = i * 2 + b
                                sp.wait_ge(i_lo, LEAD + w)
                                nb = 1 - b
                                sp.dma_start(wraw[:, nb, :], win[w + 1]).then_inc(i_w[nb], 16)
                                sp.wait_ge(i_u, LEAD + w + 1)
                                sp.dma_start(u_s[i // 2, :, :, (i % 2) * 2 + b, :].rearrange("c p t -> p c t"),
                                             ub[:, b, :].rearrange("p (c t) -> p c t", c=C)).then_inc(i_st[b], 16)
                        for b in range(2):
                            sp.wait_ge(i_st[b], LEAD + 16 * (DT // 2))

                    @block.scalar
                    def _(act):
                        act.wait_ge(i_w[0], LEAD + 16)
                        act.activation(whi[:, 0, :], wraw[:, 0, :], ACT.Copy, scale=WS).then_inc(i_hi, 1)
                        act.wait_ge(i_z, LEAD + 3)
                        with act.Fori(0, DT // 2) as i:
                            for b in range(2):
                                w = i * 2 + b
                                nb = 1 - b
                                act.wait_ge(i_w[nb], LEAD + i * 16 + 16 * (1 + b))
                                act.wait_ge(i_mm, LEAD + w * C)
                                act.activation(whi[:, nb, :], wraw[:, nb, :], ACT.Copy, scale=WS).then_inc(i_hi, 1)
                                for c in range(C):
                                    act.wait_ge(i_mm, LEAD + w * C + c + 1)
                                    if c == 0:
                                        act.wait_ge(i_cv, LEAD + w * 4)
                                    act.activation(xp[:, b, K - 1 + c * T:K - 1 + (c + 1) * T], main[c][:, :],
                                                   ACT.Copy, scale=1.0 / WS).then_inc(i_ev, 1)
                                act.wait_ge(i_cv, LEAD + w * 4 + 4)
                                act.wait_ge(i_u, LEAD + w)
                                act.activation(eb[:, :], xc[:, b, :], ACT.Tanh).then_inc(i_e, 1)

                    @block.vector
                    def _(v):
                        v.memset(zero[:, :], 0.0).then_inc(i_z, 1)
                        for b in range(2):
                            v.memset(xp[:, b, 0:K - 1], 0.0).then_inc(i_z, 1)
                        v.wait_ge(i_hi, LEAD + 1)
                        v.scalar_tensor_tensor(wlo[:, 0, :], wraw[:, 0, :], WS, whi[:, 0, :],
                                               ALU.mult, ALU.subtract).then_inc(i_lo, 1)
                        v.wait_ge(i_const, LEAD + 48)
                        v.tensor_scalar(cw[:, :, :], cw[:, :, :], 0.5, None, ALU.mult).then_inc(i_half, 1)
                        v.tensor_scalar(cb[:, :], cb[:, :], 0.5, None, ALU.mult).then_inc(i_half, 1)
                        v.wait_ge(i_half, LEAD + 2)
                        with v.Fori(0, DT // 2) as i:
                            for b in range(2):
                                w = i * 2 + b
                                nb = 1 - b
                                v.wait_ge(i_hi, LEAD + w + 2)
                                v.scalar_tensor_tensor(wlo[:, nb, :], wraw[:, nb, :], WS, whi[:, nb, :],
                                                       ALU.mult, ALU.subtract).then_inc(i_lo, 1)
                                v.wait_ge(i_ev, LEAD + w * C + C)
                                v.wait_ge(i_e, LEAD + w)
                                v.tensor_scalar(xc[:, b, :], xp[:, b, 0:L], cw[:, w, 0:1], cb[:, bass.ds(w, 1)],
                                                ALU.mult, ALU.add).then_inc(i_cv, 1)
                                for j in range(1, K):
                                    v.wait_ge(i_cv, LEAD + w * 4 + j)
                                    v.scalar_tensor_tensor(xc[:, b, :], xp[:, b, j:j + L], cw[:, w, j:j + 1],
                                                           xc[:, b, :], ALU.mult, ALU.add).then_inc(i_cv, 1)
                                v.wait_ge(i_e, LEAD + w + 1)
                                v.wait_ge(i_st[b], LEAD + i * 16)
                                v.wait_ge(i_ssm, LEAD + w)
                                v.scalar_tensor_tensor(ub[:, b, :], eb[:, :], 1.0, xc[:, b, :],
                                                       ALU.add, ALU.mult).then_inc(i_u, 1)
                        v.wait_ge(i_ssm, LEAD + DT + 1)
                        v.tensor_copy(sm[:, :, :].rearrange("p (a t) s -> p a (t s)", a=C),
                                      four[:, :, 0:TPC * S3]).then_inc(i_sm, 1)

                    @block.tensor
                    def _(pe):
                        def w_x(b, w):
                            pe.wait_ge(i_u, LEAD + w + 1)
                            for t in range(TT):
                                mm = pe.matmul(four[:, t // TPC, (t % TPC) * S3:(t % TPC + 1) * S3],
                                               ub[:, b, t * P:(t + 1) * P], wx_sb[:, w, :],
                                               start=False, stop=False, skip_group_check=True)
                            mm.then_inc(i_ssm, 1)

                        def tile(b, w):
                            pe.wait_ge(i_lo, LEAD + w + 1)
                            for c in range(C):
                                if not isinstance(w, int):
                                    pe.wait_ge(i_ev, LEAD + (w - 1) * C + c + 1)
                                elif w > 0:
                                    pe.wait_ge(i_ev, LEAD + (w - 1) * C + c + 1)
                                for k in range(HK):
                                    hi = whi[:, b, k * P:(k + 1) * P]
                                    lo = wlo[:, b, k * P:(k + 1) * P]
                                    xh = xhi[:, k, c * T:(c + 1) * T]
                                    xl = xlo[:, k, c * T:(c + 1) * T]
                                    pe.matmul(main[c][:, :], hi, xh, start=(k == 0), stop=False)
                                    pe.matmul(main[c][:, :], hi, xl, start=False, stop=False)
                                    mm = pe.matmul(main[c][:, :], lo, xh, start=False, stop=(k == HK - 1))
                                mm.then_inc(i_mm, 1)

                        pe.wait_ge(i_z, LEAD + 1)
                        for c in range(C):
                            mm = pe.matmul(four[:, c, :], zero[:, 0:P], zero[:, :], start=True, stop=False,
                                           skip_group_check=True)
                        mm.then_inc(i_ssm, 1)
                        pe.wait_ge(i_const, LEAD + 48)
                        tile(0, 0)
                        tile(1, 1)
                        w_x(0, 0)
                        with pe.Fori(1, DT // 2) as i:
                            for b in range(2):
                                tile(b, i * 2 + b)
                                w_x(1 - b, i * 2 + b - 1)
                        w_x(1, DT - 1)

            tsb = sb(proj, "tsb", [R + N, L])
            with ExitStack() as st:
                sq = sb(st, "sq", [P, TT, S3])
                ms = sb(st, "ms", [P, 3, TT])
                araw = sb(st, "araw", [P, 2, HK, 3 * LR])
                ahi = sb(st, "ahi", [P, 2, HK, 3 * LR], F16)
                alo = sb(st, "alo", [P, 2, HK, 3 * LR], F16)
                braw = sb(st, "braw", [3 * LR, IPAD])
                (r_a, r_b, r_v, r_sm, r_tp, r_tb, r_st, r_ah, r_al, r_xa, r_xh, r_xl, r_bh, r_bl, r_sd) = (
                    sem(s) for s in ("r_a", "r_b", "r_v", "r_sm", "r_tp", "r_tb", "r_st", "r_ah", "r_al",
                                     "r_xa", "r_xh", "r_xl", "r_bh", "r_bl", "r_sd"))
                groups = ((0, R), (R, N), (R + N, N))
                with nc.Block() as block:

                    @block.sync
                    def _(sp):
                        for m in range(2):
                            for r in range(3):
                                sp.dma_start(araw[:, m, :, r * LR:(r + 1) * LR], lr_a[m]).then_inc(r_a, 16)
                        for m, src in enumerate((g_b, u_b)):
                            if m:
                                sp.wait_ge(r_bl, LEAD + 1)
                            for r in range(3):
                                sp.dma_start(braw[r * LR:(r + 1) * LR, :], src).then_inc(r_b, 16)
                        sp.wait_ge(r_tb, LEAD + C)
                        sp.dma_start(bt_s, tsb[R:R + N, :]).then_inc(r_st, 16)
                        sp.wait_ge(r_st, LEAD + 16)

                    @block.vector
                    def _(v):
                        v.tensor_tensor(sq[:, :, :], sm[:, :, :], sm[:, :, :], ALU.mult).then_inc(r_v, 1)
                        v.wait_ge(r_v, LEAD + 1)
                        for g, (o, n) in enumerate(groups):
                            v.reduce_sum(ms[:, g, :], sq[:, :, o:o + n], axis=AX.X).then_inc(r_v, 1)
                        v.wait_ge(r_v, LEAD + 4)
                        for g, (o, n) in enumerate(groups):
                            v.tensor_scalar(ms[:, g, :], ms[:, g, :], 1.0 / n, 1e-6, ALU.mult, ALU.add
                                            ).then_inc(r_v, 1)
                        v.wait_ge(r_ah, LEAD + 1)
                        v.tensor_tensor(alo[:, :, :, :].rearrange("p a b c -> p (a b c)"),
                                        araw[:, :, :, :].rearrange("p a b c -> p (a b c)"),
                                        ahi[:, :, :, :].rearrange("p a b c -> p (a b c)"),
                                        ALU.subtract).then_inc(r_al, 1)
                        v.wait_ge(r_v, LEAD + 7)
                        v.wait_ge(r_sd, LEAD + 1)
                        v.reciprocal(ms[:, :, :], ms[:, :, :]).then_inc(r_v, 1)
                        v.wait_ge(r_v, LEAD + 8)
                        for g, (o, n) in enumerate(groups):
                            dst = cT[:, :, :] if g == 2 else sm[:, :, o:o + n]
                            v.tensor_tensor(dst, sm[:, :, o:o + n],
                                            ms[:, g, :].unsqueeze(2).broadcast_to([P, TT, n]), ALU.mult
                                            ).then_inc(r_sm, 1)
                        for m in range(2):
                            v.wait_ge(r_bh, LEAD + m + 1)
                            v.scalar_tensor_tensor(btab[2 * LR:3 * LR, m, :], braw[2 * LR:3 * LR, :], WS,
                                                   btab[2 * LR:3 * LR, m, :], ALU.mult, ALU.subtract
                                                   ).then_inc(r_bl, 1)
                        for q in range(2 * C):
                            m, c = divmod(q, C)
                            v.wait_ge(r_xh, LEAD + q + 1)
                            dst = xa[LR:2 * LR, m, c * T:(c + 1) * T]
                            v.tensor_tensor(dst, main[q % 4][LR:2 * LR, :], dst, ALU.subtract).then_inc(r_xl, 1)

                    @block.scalar
                    def _(act):
                        act.wait_ge(r_a, LEAD + 96)
                        act.activation(ahi[:, :, :, :].rearrange("p a b c -> p (a b c)"),
                                       araw[:, :, :, :].rearrange("p a b c -> p (a b c)"),
                                       ACT.Copy).then_inc(r_ah, 1)
                        act.wait_ge(r_v, LEAD + 7)
                        act.activation(ms[:, :, :], ms[:, :, :], ACT.Sqrt).then_inc(r_sd, 1)
                        for m in range(2):
                            act.wait_ge(r_b, LEAD + 48 * (m + 1))
                            act.activation(btab[:, m, :], braw[:, :], ACT.Copy, scale=WS).then_inc(r_bh, 1)
                        for c in range(C):
                            act.wait_ge(r_tp, LEAD + c + 1)
                            act.activation(tsb[:, c * T:(c + 1) * T], four[0:R + N, c, :], ACT.Copy
                                           ).then_inc(r_tb, 1)
                        for q in range(2 * C):
                            m, c = divmod(q, C)
                            act.wait_ge(r_xa, LEAD + q + 1)
                            act.activation(xa[:, m, c * T:(c + 1) * T], main[q % 4][0:3 * LR, :], ACT.Copy
                                           ).then_inc(r_xh, 1)

                    @block.tensor
                    def _(pe):
                        pe.wait_ge(r_al, LEAD + 1)
                        for q in range(2 * C):
                            if q == 2:
                                pe.wait_ge(r_sm, LEAD + 2)
                                for c in range(C):
                                    for t in range(TPC):
                                        mm = pe.transpose(four[0:R + N, c, t * P:(t + 1) * P],
                                                          sm[:, c * TPC + t, 0:R + N], ident[:, :])
                                    mm.then_inc(r_tp, 1)
                            m, c = divmod(q, C)
                            if q >= 4:
                                pe.wait_ge(r_xl, LEAD + q - 3)
                            for k in range(HK):
                                for a, xx, z in ((ahi, xhi, 0), (ahi, xlo, 1), (alo, xhi, 2)):
                                    mm = pe.matmul(main[q % 4][0:3 * LR, :], a[:, m, k, :],
                                                   xx[:, k, c * T:(c + 1) * T],
                                                   start=(k == 0 and z == 0), stop=(k == HK - 1 and z == 2))
                            mm.then_inc(r_xa, 1)

            with ExitStack() as st:
                wd = sb(st, "wd", [R, 2, P])
                bd = sb(st, "bd", [P, DT])
                gsb = sb(st, "gsb", [P, 2, L])
                mx = sb(st, "mx", [P, 2, L])
                ab = sb(st, "ab", [P, L])
                du = sb(st, "du", [P, 2, L])
                g_w = [sem(f"g_w{b}") for b in range(2)]
                g_wd = [sem(f"g_wd{b}") for b in range(2)]
                g_sg = [sem(f"g_sg{b}") for b in range(2)]
                g_sd = [sem(f"g_sd{b}") for b in range(2)]
                g_u = [sem(f"g_u{b}") for b in range(2)]
                (g_const, g_hi, g_lo, g_mm, g_ev, g_e, g_g, g_pre, g_mx, g_ab, g_sp, g_dt, g_du) = (
                    sem(s) for s in ("g_const", "g_hi", "g_lo", "g_mm", "g_ev", "g_e", "g_g", "g_pre",
                                     "g_mx", "g_ab", "g_sp", "g_dt", "g_du"))
                with nc.Block() as block:
                    def store(dram, i, b, tile):
                        return (dram[i // 2, :, :, (i % 2) * 2 + b, :].rearrange("c p t -> p c t"),
                                tile.rearrange("p (c t) -> p c t", c=C))

                    @block.sync
                    def _(sp):
                        sp.dma_start(wd[:, 0, :], wdt[0]).then_inc(g_wd[0], 16)
                        sp.dma_start(bd[:, :], bdt).then_inc(g_const, 16)
                        with sp.Fori(0, DT // 2) as i:
                            for b in range(2):
                                w = i * 2 + b
                                sp.wait_ge(g_mx, LEAD + w)
                                sp.dma_start(wd[:, 1 - b, :], wdt[w + 1]).then_inc(g_wd[1 - b], 16)
                                sp.wait_ge(g_lo, LEAD + w)
                                sp.dma_start(wraw[:, 1 - b, :], win[w + DT + 1]).then_inc(g_w[1 - b], 16)
                                sp.wait_ge(g_sd[b], LEAD + i * 32)
                                dst, src = du[:, b, :].rearrange("p (c t) -> p c t", c=C), \
                                    u_s[i // 2, :, :, (i % 2) * 2 + b, :].rearrange("c p t -> p c t")
                                sp.dma_start(dst, src).then_inc(g_u[b], 16)
                                sp.wait_ge(g_du, LEAD + w + 1)
                                sp.dma_start(*store(dt_s, i, b, mx[:, b, :])).then_inc(g_sd[b], 16)
                                sp.dma_start(*store(du_s, i, b, du[:, b, :])).then_inc(g_sd[b], 16)
                        for b in range(2):
                            sp.wait_ge(g_sd[b], LEAD + 32 * (DT // 2))
                            sp.wait_ge(g_wd[b], LEAD + 16 * (DT // 2 + 1 - b))

                    @block.scalar
                    def _(act):
                        act.wait_ge(g_const, LEAD + 16)
                        with act.Fori(0, DT // 2) as i:
                            for b in range(2):
                                w = i * 2 + b
                                act.wait_ge(g_pre, LEAD + w + 1)
                                act.wait_ge(g_dt, LEAD + w)
                                act.activation(ab[:, :], four[:, :, :].rearrange("p c t -> p (c t)"), ACT.Abs,
                                               bias=bd[:, bass.ds(w, 1)]).then_inc(g_ab, 1)
                                act.wait_ge(g_ab, LEAD + w * 2 + 1)
                                act.activation(ab[:, :], ab[:, :], ACT.Exp, scale=-1.0).then_inc(g_ab, 1)
                                act.wait_ge(g_ab, LEAD + w * 2 + 2)
                                act.activation(ab[:, :], ab[:, :], ACT.Ln, bias=1.0).then_inc(g_sp, 1)
                                nb = 1 - b
                                act.wait_ge(g_w[nb], LEAD + i * 16 + 16)
                                act.wait_ge(g_mm, LEAD + w * C)
                                act.activation(whi[:, nb, :], wraw[:, nb, :], ACT.Copy, scale=WS).then_inc(g_hi, 1)
                                for c in range(C):
                                    act.wait_ge(g_mm, LEAD + w * C + c + 1)
                                    if c == 0:
                                        act.wait_ge(g_g, LEAD + w)
                                    act.activation(xp[:, b, c * T:(c + 1) * T], main[c][:, :],
                                                   ACT.Copy, scale=0.5 / WS).then_inc(g_ev, 1)
                                act.wait_ge(g_ev, LEAD + w * C + C)
                                act.activation(eb[:, :], xp[:, b, 0:L], ACT.Tanh).then_inc(g_e, 1)
                                act.wait_ge(g_g, LEAD + w + 1)
                                act.dma_start(*store(gs_s, i, b, gsb[:, b, :])).then_inc(g_sg[b], 16)
                        for b in range(2):
                            act.wait_ge(g_sg[b], LEAD + 16 * (DT // 2))

                    @block.vector
                    def _(v):
                        v.wait_ge(g_const, LEAD + 16)
                        with v.Fori(0, DT // 2) as i:
                            for b in range(2):
                                w = i * 2 + b
                                v.wait_ge(g_pre, LEAD + w + 1)
                                v.wait_ge(g_sd[b], LEAD + i * 32)
                                v.wait_ge(g_ab, LEAD + w * 2 + 1)
                                v.wait_ge(g_du, LEAD + w)
                                v.tensor_scalar(mx[:, b, :], four[:, :, :].rearrange("p c t -> p (c t)"),
                                                bd[:, bass.ds(w, 1)], 0.0, ALU.add, ALU.max).then_inc(g_mx, 1)
                                v.wait_ge(g_sp, LEAD + w + 1)
                                v.wait_ge(g_mx, LEAD + w + 1)
                                v.tensor_tensor(mx[:, b, :], mx[:, b, :], ab[:, :], ALU.add).then_inc(g_dt, 1)
                                v.wait_ge(g_hi, LEAD + w + 1)
                                nb = 1 - b
                                v.scalar_tensor_tensor(wlo[:, nb, :], wraw[:, nb, :], WS, whi[:, nb, :],
                                                       ALU.mult, ALU.subtract).then_inc(g_lo, 1)
                                v.wait_ge(g_e, LEAD + w + 1)
                                v.wait_ge(g_sg[b], LEAD + i * 16)
                                v.scalar_tensor_tensor(gsb[:, b, :], eb[:, :], 1.0, xp[:, b, 0:L],
                                                       ALU.add, ALU.mult).then_inc(g_g, 1)

                    @block.gpsimd
                    def _(pool):
                        with pool.Fori(0, DT // 2) as i:
                            for b in range(2):
                                w = i * 2 + b
                                pool.wait_ge(g_dt, LEAD + w + 1)
                                pool.wait_ge(g_u[b], LEAD + i * 16 + 16)
                                pool.tensor_tensor(du[:, b, :], mx[:, b, :], du[:, b, :], ALU.mult
                                                   ).then_inc(g_du, 1)

                    @block.tensor
                    def _(pe):
                        with pe.Fori(0, DT // 2) as i:
                            for b in range(2):
                                w = i * 2 + b
                                pe.wait_ge(g_wd[b], LEAD + i * 16 + 16)
                                pe.wait_ge(g_mx, LEAD + w)
                                for c in range(C):
                                    mm = pe.matmul(four[:, c, :], wd[:, b, :], tsb[0:R, c * T:(c + 1) * T],
                                                   start=True, stop=True)
                                mm.then_inc(g_pre, 1)
                                pe.wait_ge(g_lo, LEAD + w)
                                for c in range(C):
                                    if b == 0:
                                        pe.wait_ge(g_ev, LEAD + w * C)
                                    else:
                                        pe.wait_ge(g_ev, LEAD + (w - 1) * C + c + 1)
                                    for k in range(HK):
                                        hi = whi[:, b, k * P:(k + 1) * P]
                                        lo = wlo[:, b, k * P:(k + 1) * P]
                                        xh = xhi[:, k, c * T:(c + 1) * T]
                                        xl = xlo[:, k, c * T:(c + 1) * T]
                                        pe.matmul(main[c][:, :], hi, xh, start=(k == 0), stop=False)
                                        pe.matmul(main[c][:, :], hi, xl, start=False, stop=False)
                                        mm = pe.matmul(main[c][:, :], lo, xh, start=False, stop=(k == HK - 1))
                                    mm.then_inc(g_mm, 1)

        with ExitStack() as st:
            bb = sb(st, "bb", [P, N, T])
            dtb = sb(st, "dtb", [P, J, T])
            dub = sb(st, "dub", [P, J, T])
            inj = sb(st, "inj", [P, 2, J, T])
            decay = sb(st, "decay", [P, J, T])
            ysum = sb(st, "ysum", [P, TPC, T])
            us = sb(st, "us", [P, J * T])
            gs = sb(st, "gs", [P, J * T])
            carry = sb(st, "carry", [P, DT, N])
            gsc = sb(st, "gsc", [P, 2, IT])
            wq = sb(st, "wq", [P, 2, 512], I32)
            w16 = sb(st, "w16", [P, 2, 2 * HK * P], F16)
            ffb = sb(st, "ffb", [P, 4, T])
            lrt, gl, ul, ex = (ffb[:, a, :] for a in range(4))
            hh = sb(st, "hh", [P, 2, T], F16)
            turned = [pb(st, f"turned{t}", [P, T]) for t in range(TPC)]
            back = pb(st, "back", [P, T])
            bank = [pb(st, f"bank{m}", [P, T]) for m in range(2)]
            lrb = pb(st, "lrb", [P, T])
            us16 = us[:, :].bitcast(F16)

            def y_part(part, j):
                return us16[:, bass.ds(j * 2 * T + part * T, T)]

            (s_const, s_gsc, s_bb0, s_bb1, s_ffz, s_yhi, s_inj_half, s_us, s_gs, s_ys,
             s_dec, s_inj, s_scan, s_carry, s_turn, s_sum,
             s_yt, s_yev, s_gate, s_parts, s_wq0, s_wq1, s_conv, s_mm, s_lrt, s_gl, s_ul, s_ex, s_sg,
             s_h, s_hi, s_lo, s_hs, s_beat) = (sem("s_" + s) for s in (
                "const gsc bb0 bb1 ffz yhi inj_half us gs ys dec inj scan carry turn sum yt yev gate parts "
                "wq0 wq1 conv "
                "mm lrt gl ul ex sg h hi lo hs beat").split())
            s_wq = [s_wq0, s_wq1]
            s_bb = [s_bb0, s_bb1]
            s_dt, s_du = ([sem(f"s_{x}{b}") for b in range(2)] for x in ("dt", "du"))
            FF_STEPS = IT // 2
            assert FF_STEPS % G == G - 1
            OUT_FROM = FF_STEPS + 1
            y_in = w16[:, :, 0:2 * J * P].rearrange("p b (x t) -> p b x t", t=P)
            made = wq[:, :, :].bitcast(F32)
            t_raw, t_hi, t_lo, t_y, t_mm, t_ev, t_st = (sem("t_" + x) for x in "raw hi lo y mm ev st".split())

            def work(c, g):
                step = c * G + (g if isinstance(g, int) else 1)
                return "ff" if step < FF_STEPS else "split" if step < OUT_FROM else "out"

            def steps(eng, step_fn, after_ff=lambda: None):
                for c in range(C):
                    ffs = min(max(FF_STEPS - c * G, 0), G)
                    step_fn(c, 0, ffs > 0)
                    edge = min(max(ffs, 1), G - 1)
                    for a, b, ff in ((1, edge, True), (edge, G - 1, False)):
                        if a < b:
                            with eng.Fori(a, b) as g:
                                step_fn(c, g, ff)
                        if ff and c * G + ffs == FF_STEPS:
                            after_ff()
                    step_fn(c, G - 1, ffs == G)

            def load_half(eng, c, g, dst, src, s_load, half):
                js = slice(half * J // 2, (half + 1) * J // 2)
                eng.dma_start(dst[:, js, :], src[g, c, :, js, :]).then_inc(s_load[half], 16)

            def after(c, g):
                if isinstance(g, int) and g == G - 1:
                    return (c + 1, 0) if c < C - 1 else None
                return c, g + 1

            def before(c, g):
                if isinstance(g, int) and g == 0:
                    return (c - 1, G - 1) if c else None
                return c, g - 1

            def pairs(eng, step, ff, pair_fn, half=lambda: None, unroll=()):
                for h in range(2):
                    i = step * 2 + h if ff else None
                    pair_fn(h * UNITS, i, 0, h)
                    if h in unroll:
                        for p in range(1, UNITS - 1):
                            pair_fn(p + h * UNITS, i, p, h)
                    else:
                        with eng.Fori(1, UNITS - 1) as p:
                            pair_fn(p + h * UNITS, i, p, h)
                    pair_fn((h + 1) * UNITS - 1, i, UNITS - 1, h)
                    if h == 0:
                        half()

            with nc.Block() as block:
                @block.sync
                def _(sp):
                    for m, src in enumerate((g_scale, u_scale)):
                        sp.dma_start(gsc[:, m, :], src).then_inc(s_const, 16)
                    for k in range(UNITS):
                        if k >= 2:
                            sp.wait_ge(s_conv, LEAD + k - 1)
                        sp.dma_start(wq[:, k % 2, :], gu_q[0, :, k * 512:(k + 1) * 512]).then_inc(s_wq[k % 2], 16)

                    def load_q(k):
                        sp.wait_ge(s_conv, LEAD + UNITS + k - 1)
                        sp.wait_ge(s_wq0, LEAD + 32 + k * 16)
                        sp.dma_start(wq[:, k % 2, :], gu_q[k // UNITS + 1, :, bass.ts(k % UNITS, 512)]
                                     ).then_inc(s_wq0, 16)

                    load_q(0)

                    def load_b(c, half):
                        n = slice(half * N // 2, (half + 1) * N // 2)
                        sp.dma_start(bb[:, n, :], bt_s[n, c * T:(c + 1) * T].partition_broadcast(P)
                                     ).then_inc(s_bb[half], 16)

                    def load_y(m):
                        if not isinstance(m, int) or m:
                            sp.wait_ge(t_y, LEAD + m * 16)
                        tok = bass.ds(m // G % TPC * P, P)
                        sp.dma_start(y_in[:, m % 2, :, :],
                                     y_s[m // (G * TPC) * G + m % G].rearrange("p (x t) -> p x t", t=T)[:, :, tok]
                                     ).then_inc(t_y, 16)

                    def store_made(tile):
                        sp.wait_ge(t_ev, LEAD + tile * 2 + 2)
                        sp.dma_start(s_s[tile], made.rearrange("p a t -> p (a t)")).then_inc(t_st, 16)

                    def store_y(step, j):
                        tile = bass.ds(j * 2 * T, 2 * T)
                        sp.dma_start(y_s[step, :, tile], us16[:, tile]).then_inc(s_ys, 16)
                        sp.wait_ge(s_ys, LEAD + (step * J + j) * 16 + 16)

                    def step_fn(c, g, ff):
                        step = c * G + g
                        first = before(c, g) is None
                        if first:
                            load_b(0, 0)
                            for half in range(2):
                                load_half(sp, 0, 0, dub, du_s, s_du, half)
                                load_half(sp, 0, 0, dtb, dt_s, s_dt, half)
                        elif work(*before(c, g)) == "out":
                            store_made(step * 2 - 1 - OUT_FROM * 2)
                        if isinstance(g, int) and g == 0:
                            if not first:
                                sp.wait_ge(s_inj, LEAD + step * N)
                            load_b(c, 1)

                        def pair(pr, i, p, h):
                            if work(c, g) == "split":
                                sp.wait_ge(t_lo, LEAD + pr)
                                sp.dma_start(ffb[:, :, :].rearrange("p (i a) t -> p i (a t)", i=2),
                                             wout[bass.ds(pr * 2, 2)].rearrange("i p h -> p i h")).then_inc(t_raw, 16)
                            if work(c, g) == "out":
                                m = (step - OUT_FROM) * (2 * G) + pr
                                sp.wait_ge(t_mm, LEAD + m)
                                load_y(m + 1)
                            if i is not None:
                                k = i * UNITS + p
                                load_q(k + 1)
                                sp.wait_ge(s_lo, LEAD + k + 1)
                                sp.dma_start(h_s[k], hh[:, :, :]).then_inc(s_hs, 16)
                            if h == 1:
                                if not first:
                                    sp.wait_ge(s_parts, LEAD + (step - 1) * J + p + 1)
                                sp.wait_ge(s_us, LEAD + (step * J + p) * 16)
                                sp.wait_ge(s_gs, LEAD + (step * J + p) * 16)
                                if not first:
                                    store_y(step - 1, p)
                                tile = bass.ds(p * T, T)
                                sp.dma_start(us[:, tile], u_s[g, c, :, p, :]).then_inc(s_us, 16)
                                sp.dma_start(gs[:, tile], gs_s[g, c, :, p, :]).then_inc(s_gs, 16)

                        def half():
                            if work(c, g) == "out":
                                store_made(step * 2 - OUT_FROM * 2)
                            if isinstance(g, int) and g == G - 1 and c < C - 1:
                                sp.wait_ge(s_inj, LEAD + step * N + N // 2)
                                load_b(c + 1, 0)

                        pairs(sp, step, ff, pair, half, unroll=(1,))
                        if work(c, g) == "split":
                            load_y(0)

                    def after_ff():
                        sp.wait_ge(s_wq0, LEAD + 48 + IT * UNITS * 16)
                        sp.wait_ge(s_lo, LEAD + IT * UNITS + 1)
                        sp.dma_start(h_s[IT * UNITS], hh[:, :, :]).then_inc(s_hs, 16)

                    steps(sp, step_fn, after_ff)
                    store_made(TT // 2 - 1)
                    for j in range(J):
                        sp.wait_ge(s_parts, LEAD + (C * G - 1) * J + j + 1)
                        store_y(C * G - 1, j)
                    sp.wait_ge(s_hs, LEAD + 16 * (IT * UNITS + 1))
                    sp.wait_ge(t_st, LEAD + 16 * (TT // 2))
                    sp.wait_ge(t_y, LEAD + 16 * (TT // 2 * G + 1))

                @block.scalar
                def _(act):
                    act.wait_ge(s_const, LEAD + 32)
                    for m, half in enumerate((0.5, 1.0)):
                        act.activation(gsc[:, m, :], gsc[:, m, :], ACT.Copy, scale=half * Q_STEP).then_inc(s_gsc, 1)
                    for k in range(UNITS):
                        act.wait_ge(s_wq[k % 2], LEAD + 16 * (k // 2 + 1))
                        act.activation(w16[:, 0, k * 512:(k + 1) * 512], wq[:, k % 2, :], ACT.Copy,
                                       bias=-Q_ZERO).then_inc(s_conv, 1)

                    def h_high(k):
                        act.wait_ge(s_h, LEAD + k + 1)
                        act.wait_ge(s_hs, LEAD + k * 16)
                        act.activation(hh[:, 0, :], ul[:, :], ACT.Copy).then_inc(s_hi, 1)

                    def y_high(step, j):
                        act.wait_ge(s_gate, LEAD + step * J + j + 1)
                        act.activation(y_part(0, j), gs[:, bass.ds(j * T, T)], ACT.Copy).then_inc(s_yhi, 1)

                    def step_fn(c, g, ff):
                        step = c * G + g
                        def pair(pr, i, p, h):
                            last = isinstance(pr, int) and pr == N // 2 - 1
                            for q in range(2):
                                slot = step * N + pr * 2 + q
                                for j in range(J):
                                    act.wait_ge(s_scan, LEAD + slot * J + j + EXTRA + 1 - J)
                                    if q == 0 and j % 2 == 0 and isinstance(pr, int) and pr == 0:
                                        act.wait_ge(s_dt[j // 2], LEAD + step * 16 + 16)
                                    act.activation(decay[:, j, :], dtb[:, j, :], ACT.Exp,
                                                   scale=aneg[:, g * J + j, bass.ds(pr * 2 + q, 1)]
                                                   ).then_inc(s_dec, 1)
                                    if last and q == 1 and after(c, g):
                                        if j == 0:
                                            act.wait_ge(s_inj, LEAD + slot + 1)
                                            for half in range(2):
                                                load_half(act, *after(c, g), dub, du_s, s_du, half)
                                        if j % 2:
                                            act.wait_ge(s_dec, LEAD + slot * J + j + 1)
                                            load_half(act, *after(c, g), dtb, dt_s, s_dt, j // 2)
                                    if i is not None and q == 1 and j == 0:
                                        low_rank(i * UNITS + p, 0)
                                if i is not None:
                                    k = i * UNITS + p
                                    if q == 0:
                                        act.wait_ge(s_wq0, LEAD + k * 16 + 48)
                                        act.wait_ge(s_mm, LEAD + i * (2 * UNITS))
                                        act.activation(w16[:, (i + 1) % 2, bass.ts(p, 512)], wq[:, p % 2, :],
                                                       ACT.Copy, bias=-Q_ZERO).then_inc(s_conv, 1)
                                    else:
                                        h_high(k)
                                        act.wait_ge(s_gl, LEAD + k + 1)
                                        act.wait_ge(s_sg, LEAD + k)
                                        act.activation(ex[:, :], gl[:, :], ACT.Tanh).then_inc(s_ex, 1)
                                if work(c, g) == "split" and q == 1:
                                    act.wait_ge(t_raw, LEAD + pr * 16 + 16)
                                    act.wait_ge(s_mm, LEAD + IT * UNITS * 2)
                                    act.activation(wo_hi[:, bass.ds(pr * 2, 2), :].rearrange("p i h -> p (i h)"),
                                                   ffb[:, :, :].rearrange("p a t -> p (a t)"), ACT.Copy, scale=WS
                                                   ).then_inc(t_hi, 1)
                                act.wait_ge(s_scan, LEAD + slot * J + J + EXTRA)
                                act.activation(carry[:, bass.ds(g * J, J), bass.ds(pr * 2 + q, 1)],
                                               inj[:, q, :, T - 1:T], ACT.Copy).then_inc(s_carry, 1)
                                if i is not None and q == 1:
                                    low_rank(k, 1)
                                if h == 0 and q == 1 and before(c, g):
                                    y_high(step - 1, p)

                        def low_rank(k, q):
                            act.wait_ge(s_mm, LEAD + k * 2 + q + 1)
                            act.wait_ge((s_ul, s_gl)[q], LEAD + k + q)
                            act.activation(lrt[:, :], lrb[:, :], ACT.Copy,
                                           scale=(0.5, 1.0)[q] * LR_SCALE / WS).then_inc(s_lrt, 1)

                        def evacuate(tile):
                            if work(c, g) == "out":
                                act.wait_ge(t_mm, LEAD + tile * G + G)
                                act.wait_ge(t_st, LEAD + tile * 16)
                                for m in range(2):
                                    act.activation(made[:, m, :], bank[m][:, :], ACT.Copy, scale=1.0 / WS
                                                   ).then_inc(t_ev, 1)

                        pairs(act, step, ff, pair,
                              lambda: evacuate((step - OUT_FROM) * 2))
                        evacuate((step - OUT_FROM) * 2 + 1)

                    steps(act, step_fn, lambda: h_high(IT * UNITS))
                    for j in range(J):
                        y_high(C * G - 1, j)

                @block.vector
                def _(v):
                    v.memset(carry[:, :, :], 0.0).then_inc(s_carry, 1)
                    v.sem_inc(s_scan, EXTRA)
                    v.sem_inc(s_sum, J)
                    v.sem_inc(s_turn, TPC)
                    v.wait_ge(s_gsc, LEAD + 2)
                    v.wait_ge(s_carry, LEAD + 1)

                    def add_up(slot, c, n, first):
                        for t in range(TPC):
                            v.wait_ge(s_turn, LEAD + slot * TPC + t + 1 + TPC)
                            v.wait_ge(s_sum, LEAD + slot * TPC + t + 1)
                            if first:
                                v.tensor_scalar(ysum[:, t, :], turned[t][:, :],
                                                cT[:, c * TPC + t, n], None, ALU.mult).then_inc(s_sum, 1)
                            else:
                                v.scalar_tensor_tensor(ysum[:, t, :], turned[t][:, :],
                                                       cT[:, c * TPC + t, n], ysum[:, t, :],
                                                       ALU.mult, ALU.add).then_inc(s_sum, 1)

                    def d_u(step, g, j):
                        v.wait_ge(s_us, LEAD + (step * J + j) * 16 + 16)
                        v.wait_ge(s_yt, LEAD + step * J + j + 1)
                        v.scalar_tensor_tensor(us[:, j * T:(j + 1) * T], us[:, j * T:(j + 1) * T],
                                               dsk[:, bass.ds(g * J + j, 1)], back[:, :],
                                               ALU.mult, ALU.add).then_inc(s_yev, 1)

                    def step_fn(c, g, ff):
                        step = c * G + g
                        last = before(c, g)

                        def scan(slot, q, n, j):
                            v.wait_ge(s_dec, LEAD + slot * J + j + 1)
                            v.tensor_tensor_scan(inj[:, q, j, :], decay[:, j, :], inj[:, q, j, :],
                                                 carry[:, g * J + j, n], ALU.mult, ALU.add).then_inc(s_scan, 1)

                        def pair(pr, i, p, h):
                            first = isinstance(pr, int) and pr == 0
                            for q in range(2):
                                slot = step * N + pr * 2 + q
                                n = bass.ds(pr * 2 + q, 1)
                                if not (first and q == 0):
                                    v.wait_ge(s_inj, LEAD + slot + 1)
                                for j in range(J):
                                    if first and q == 0 and j == 0:
                                        v.wait_ge(s_inj_half, LEAD + step + 1)
                                    if first and q == 0 and j == J // 2:
                                        v.wait_ge(s_inj, LEAD + slot + 1)
                                    scan(slot, q, n, j)
                                    if first and q == 1 and last and j:
                                        d_u(step - 1, last[1], j - 1)
                                    if i is not None and q == 1 and j == 1:
                                        k = i * UNITS + p
                                        v.wait_ge(s_lrt, LEAD + k * 2 + 1)
                                        v.wait_ge(s_h, LEAD + k + 1)
                                        v.scalar_tensor_tensor(gl[:, :], bank[0][:, :], gsc[:, 0, bass.ds(i, 1)],
                                                               lrt[:, :], ALU.mult, ALU.add).then_inc(s_gl, 1)
                                if first and q == 1 and last:
                                    d_u(step - 1, last[1], J - 1)
                                if q == 1:
                                    add_up(slot - 1, c, bass.ds(pr * 2, 1), first)
                                elif not first:
                                    add_up(slot - 1, c, bass.ds(pr * 2 - 1, 1), False)
                                elif last:
                                    add_up(slot - 1, last[0], slice(N - 1, N), False)
                            if work(c, g) == "split":
                                v.wait_ge(t_hi, LEAD + pr + 1)
                                v.scalar_tensor_tensor(wo_lo[:, bass.ds(pr * 2, 2), :].rearrange("p i h -> p (i h)"),
                                                       ffb[:, :, :].rearrange("p a t -> p (a t)"), WS,
                                                       wo_hi[:, bass.ds(pr * 2, 2), :].rearrange("p i h -> p (i h)"),
                                                       ALU.mult, ALU.subtract).then_inc(t_lo, 1)
                            if i is not None:
                                v.wait_ge(s_lrt, LEAD + k * 2 + 2)
                                v.wait_ge(s_lo, LEAD + k + 1)
                                v.scalar_tensor_tensor(ul[:, :], bank[1][:, :], gsc[:, 1, bass.ds(i, 1)],
                                                       lrt[:, :], ALU.mult, ALU.add).then_inc(s_ul, 1)
                                v.wait_ge(s_ex, LEAD + k + 1)
                                v.scalar_tensor_tensor(gl[:, :], ex[:, :], 1.0, gl[:, :],
                                                       ALU.add, ALU.mult).then_inc(s_sg, 1)

                        pairs(v, step, ff, pair)

                    steps(v, step_fn)
                    add_up(C * G * N - 1, C - 1, slice(N - 1, N), False)
                    for j in range(J):
                        d_u(C * G - 1, G - 1, j)
                        v.wait_ge(s_yev, LEAD + (C * G - 1) * J + j + 1)
                        v.wait_ge(s_gs, LEAD + ((C * G - 1) * J + j) * 16 + 16)
                        tok = slice(j * T, (j + 1) * T)
                        v.tensor_tensor(gs[:, tok], us[:, tok], gs[:, tok], ALU.mult).then_inc(s_gate, 1)

                @block.gpsimd
                def _(pool):
                    pool.memset(gl[:, :], 0.0).then_inc(s_ffz, 1)
                    pool.memset(ul[:, :], 0.0).then_inc(s_ffz, 1)
                    pool.wait_ge(s_ffz, LEAD + 2)

                    def h_product(k):
                        pool.wait_ge(s_sg, LEAD + k)
                        pool.tensor_tensor(ul[:, :], gl[:, :], ul[:, :], ALU.mult).then_inc(s_h, 1)

                    def h_low(k):
                        pool.wait_ge(s_hi, LEAD + k + 1)
                        pool.tensor_tensor(hh[:, 1, :], ul[:, :], hh[:, 0, :], ALU.subtract).then_inc(s_lo, 1)

                    def y_gate(step, j):
                        pool.wait_ge(s_yev, LEAD + step * J + j + 1)
                        pool.wait_ge(s_gs, LEAD + (step * J + j) * 16 + 16)
                        tok = bass.ds(j * T, T)
                        pool.tensor_tensor(gs[:, tok], us[:, tok], gs[:, tok], ALU.mult).then_inc(s_gate, 1)

                    def y_low(step, j):
                        pool.wait_ge(s_yhi, LEAD + step * J + j + 1)
                        pool.tensor_tensor(y_part(1, j), gs[:, bass.ds(j * T, T)], y_part(0, j), ALU.subtract
                                           ).then_inc(s_parts, 1)

                    def step_fn(c, g, ff):
                        step = c * G + g
                        pool.wait_ge(s_bb[0], LEAD + c * 16 + 16)

                        def pair(pr, i, p, h):
                            for q in range(2):
                                slot = step * N + pr * 2 + q
                                pool.wait_ge(s_turn, LEAD + slot * TPC)
                                pool.wait_ge(s_carry, LEAD + slot)
                                halves = 2 if q == 0 and isinstance(pr, int) and pr == 0 else 1
                                for part in range(halves):
                                    if halves == 2:
                                        pool.wait_ge(s_du[part], LEAD + step * 16 + 16)
                                    js = slice(part * J // halves, (part + 1) * J // halves)
                                    pool.tensor_tensor(inj[:, q, js, :], dub[:, js, :],
                                                       bb[:, bass.ds(pr * 2 + q, 1), :].broadcast_to(
                                                           [P, J // halves, T]), ALU.mult
                                                       ).then_inc(s_inj if part == halves - 1 else s_inj_half, 1)
                            if i is not None:
                                h_product(i * UNITS + p)
                            if before(c, g):
                                (y_gate, y_low)[h](step - 1, p)
                            if i is not None:
                                h_low(i * UNITS + p)

                        def half():
                            pool.wait_ge(s_bb[1], LEAD + c * 16 + 16)
                            pool.sem_inc(s_beat, 1)

                        pairs(pool, step, ff, pair, half)

                    def after_ff():
                        h_product(IT * UNITS)
                        h_low(IT * UNITS)

                    steps(pool, step_fn, after_ff)
                    for j in range(J):
                        y_low(C * G - 1, j)

                @block.tensor
                def _(pe):
                    def y_back(step, j):
                        pe.wait_ge(s_sum, LEAD + step * (N * TPC) + N * TPC + J)
                        pe.wait_ge(s_yev, LEAD + step * J + j)
                        for t in range(TPC):
                            mm = pe.transpose(back[:, t * P:(t + 1) * P], ysum[:, t, j * P:(j + 1) * P],
                                              ident[:, :])
                        mm.then_inc(s_yt, 1)

                    def step_fn(c, g, ff):
                        step = c * G + g

                        def turn(slot, q, t):
                            pe.wait_ge(s_sum, LEAD + slot * TPC + t + 1)
                            for j in range(J):
                                mm = pe.transpose(turned[t][:, j * P:(j + 1) * P],
                                                  inj[:, q, j, t * P:(t + 1) * P], ident[:, :])
                            mm.then_inc(s_turn, 1)

                        def products(i, p, q, h0, h1):
                            for h in range(h0, h1):
                                w = w16[:, i % 2, (q * HK + h) * P:(q * HK + h + 1) * P]
                                pe.matmul(bank[q][:, :], w, xhi[:, h, bass.ts(p, T)],
                                          start=(h == 0), stop=False)
                                pe.matmul(bank[q][:, :], w, xlo[:, h, bass.ts(p, T)],
                                          start=False, stop=(h == HK - 1))

                        def low_rank(i, p, q):
                            pe.wait_ge(s_lrt, LEAD + (i * UNITS + p) * 2 + q)
                            pe.matmul(lrb[:, :], btab[:, q, bass.ts(i, P)], xa[:, q, bass.ts(p, T)],
                                      start=True, stop=True).then_inc(s_mm, 1)

                        def out_products(m, p, half):
                            for j in range(J):
                                for z, (part, w) in enumerate(((0, wo_hi), (1, wo_hi), (0, wo_lo))):
                                    mm = pe.matmul(bank[half][:, :], y_in[:, m % 2, j * 2 + part, :],
                                                   w[:, p * J + j, half * T:(half + 1) * T],
                                                   start=(isinstance(p, int) and p == 0 and j == 0 and z == 0), stop=False,
                                                   skip_group_check=True)
                            return mm

                        def pair(pr, i, p, h):
                            slot = step * N + pr * 2
                            if work(c, g) == "out":
                                m = (step - OUT_FROM) * (2 * G) + pr
                                if isinstance(p, int) and p == 0:
                                    pe.wait_ge(t_lo, LEAD + DT // 2)
                                    pe.wait_ge(s_ul, LEAD + IT * UNITS)
                                    pe.wait_ge(t_ev, LEAD + (step - OUT_FROM) * 4 + (2 if pr else 0))
                                pe.wait_ge(t_y, LEAD + m * 16 + 16)
                                out_products(m, p, 0)
                            if i is not None:
                                k = i * UNITS + p
                                pe.wait_ge(s_conv, LEAD + i * UNITS + UNITS)
                                pe.wait_ge(s_gl, LEAD + k)
                                products(i, p, 0, 0, HK)
                                low_rank(i, p, 0)
                                pe.wait_ge(s_ul, LEAD + k)
                            pe.wait_ge(s_scan, LEAD + slot * J + J + EXTRA)
                            for t in range(TPC):
                                turn(slot, 0, t)
                                if i is not None and t < TPC - 1:
                                    products(i, p, 1, t, t + 1)
                            for j in range(J):
                                if before(c, g) and isinstance(pr, int) and pr == 0:
                                    y_back(step - 1, j)
                                if i is not None:
                                    products(i, p, 1, TPC + j - 1, TPC + j)
                            if i is not None:
                                products(i, p, 1, HK - 1, HK)
                                low_rank(i, p, 1)
                            if work(c, g) == "out":
                                out_products(m, p, 1).then_inc(t_mm, 1)
                            pe.wait_ge(s_scan, LEAD + slot * J + 2 * J + EXTRA)
                            for t in range(TPC):
                                turn(slot + 1, 1, t)

                        pairs(pe, step, ff, pair)

                    steps(pe, step_fn)
                    for j in range(J):
                        y_back(C * G - 1, j)
        upto_scan.close()

        with ExitStack() as st:
            dw = sb(st, "dw", [P, IT, H], F16)
            da_hi = sb(st, "da_hi", [P, IT, 3 * LR], F16)
            da_lo = sb(st, "da_lo", [P, IT, 3 * LR], F16)
            db = sb(st, "db", [3 * LR, H], F16)
            rawi = sb(st, "rawi", [P, 3, 2, H], I32)
            dar = sb(st, "dar", [P, IT, LR])
            dscale = sb(st, "dscale", [P, H])
            hc = sb(st, "hc", [P, 2, IT, 2, P], F16)
            yc = sb(st, "yc", [P, 2, G, J, 2, P], F16)
            ha = sb(st, "ha", [3 * LR, P], F16)
            xr = sb(st, "xr", [P, H])
            so = sb(st, "so", [P, H])
            f1 = sb(st, "f1", [P, H])
            f2 = sb(st, "f2", [P, H])
            dbr = f2[0:3 * LR, :]
            po = pb(st, "po", [P, 2, 512])
            pd = pb(st, "pd", [P, 2, 512])
            pl = pb(st, "pl", [P, 2, 512])
            pa = pb(st, "pa", [P, P])
            o_q = [sem(f"o_q{b}") for b in range(3)]
            (o_c, o_ds, o_s, o_m, o_dw, o_dah, o_dal, o_dbh, o_dbl, o_h0, o_h1, o_y0, o_y1, o_x,
             o_ha, o_hah, o_hal, o_pl,
             o_pd, o_po, o_l, o_f, o_e, o_out, o_st) = (sem("o_" + s) for s in (
                "c ds s m dw dah dal dbh dbl h0 h1 y0 y1 x ha hah hal pl pd po l f e out st").split())
            o_h, o_y = (o_h0, o_h1), (o_y0, o_y1)
            flat = "p a b -> p (a b)"
            MADE = TT // 2
            QB = 2
            with nc.Block() as block:

                @block.sync
                def _(sp):
                    units = h_s[1:, :, :, :].rearrange("(i c) p a t -> c p i a t", c=C)

                    def load(k, b, with_y):
                        tile = (k + MADE) % TT
                        c, tok = tile // TPC, bass.ds(tile % TPC * P, P)
                        if with_y:
                            for g in range(G):
                                sp.dma_start(yc[:, b, g, :, :, :].rearrange("p j a t -> p (j a) t"),
                                             y_s[c * G + g].rearrange("p (x t) -> p x t", t=T)[:, :, tok]
                                             ).then_inc(o_y[b], 16)
                        for part in range(2):
                            sp.dma_start(hc[:, b, :, part, :], units[c, :, :, part, tok]).then_inc(o_h[b], 16)

                    load(0, 0, True)
                    for w in range(IT // QB):
                        if w >= 3:
                            sp.wait_ge(o_dw, LEAD + w - 2)
                        sp.dma_start(rawi[:, w % 3, :, :], dq[w * QB:(w + 1) * QB].rearrange("i p h -> p i h")
                                     ).then_inc(o_q[w % 3], 16)
                        if w == 0:
                            sp.dma_start(dar[:, :, :], d_a).then_inc(o_c, 16)
                            for r in range(3):
                                sp.dma_start(dbr[r * LR:(r + 1) * LR, :], d_b).then_inc(o_c, 16)
                            sp.dma_start(dscale[:, :], d_scale.partition_broadcast(P)).then_inc(o_c, 16)

                    def turn(k, b, more, with_y, made):
                        if more:
                            sp.wait_ge(o_pl, LEAD + k)
                            if with_y:
                                sp.wait_ge(o_po, LEAD + k)
                            load(k + 1, 1 - b, with_y)
                        sp.wait_ge(o_st, LEAD + k * 16)
                        sp.dma_start(xr[:, :], x[(k + MADE) % TT]).then_inc(o_x, 16)
                        if made:
                            sp.dma_start(so[:, :], s_s[k - MADE]).then_inc(o_s, 16)
                        sp.wait_ge(o_out, LEAD + k + 1)
                        sp.dma_start(out[(k + MADE) % TT], xr[:, :]).then_inc(o_st, 16)

                    with sp.Fori(0, MADE // 2 - 1) as pair:
                        for b in range(2):
                            turn(pair * 2 + b, b, True, True, False)
                    turn(MADE - 2, 0, True, True, False)
                    turn(MADE - 1, 1, True, False, False)
                    with sp.Fori(MADE // 2, TT // 2 - 1) as pair:
                        for b in range(2):
                            turn(pair * 2 + b, b, True, False, True)
                    turn(TT - 2, 0, True, False, True)
                    turn(TT - 1, 1, False, False, True)
                    sp.wait_ge(o_st, LEAD + 16 * TT)

                @block.scalar
                def _(act):
                    act.wait_ge(o_c, LEAD + 80)
                    for r in range(3):
                        act.activation(da_hi[:, :, r * LR:(r + 1) * LR], dar[:, :, :], ACT.Copy).then_inc(o_dah, 1)
                    act.activation(db[:, :], dbr[:, :], ACT.Copy, scale=WS).then_inc(o_dbh, 1)
                    act.activation(dscale[:, :], dscale[:, :], ACT.Copy, scale=0.5 * Q_STEP).then_inc(o_ds, 1)
                    for w in range(IT // QB):
                        act.wait_ge(o_q[w % 3], LEAD + w // 3 * 16 + 16)
                        act.activation(dw[:, w * QB:(w + 1) * QB, :], rawi[:, w % 3, :, :], ACT.Copy,
                                       bias=-Q_ZERO).then_inc(o_dw, 1)
                    with act.Fori(0, TT) as t:
                        act.wait_ge(o_ha, LEAD + t + 1)
                        act.wait_ge(o_pl, LEAD + t)
                        act.activation(ha[:, :], pa[0:3 * LR, :], ACT.Copy).then_inc(o_hah, 1)
                        act.wait_ge(o_pl, LEAD + t + 1)
                        act.wait_ge(o_out, LEAD + t)
                        act.activation(f2[:, :], pl[:, :, :].rearrange(flat), ACT.Copy,
                                       scale=0.5 * LR_SCALE / WS).then_inc(o_l, 1)
                        act.wait_ge(o_f, LEAD + t * 2 + 2)
                        act.activation(f2[:, :], f1[:, :], ACT.Tanh).then_inc(o_e, 1)

                @block.vector
                def _(v):
                    v.wait_ge(o_dah, LEAD + 3)
                    for r in range(3):
                        v.tensor_tensor(da_lo[:, :, r * LR:(r + 1) * LR], dar[:, :, :],
                                        da_hi[:, :, r * LR:(r + 1) * LR], ALU.subtract).then_inc(o_dal, 1)
                    v.wait_ge(o_dbh, LEAD + 1)
                    v.scalar_tensor_tensor(db[2 * LR:3 * LR, :], dbr[2 * LR:3 * LR, :], WS, db[2 * LR:3 * LR, :],
                                           ALU.mult, ALU.subtract).then_inc(o_dbl, 1)
                    v.wait_ge(o_ds, LEAD + 1)

                    def turn(t, made):
                        v.wait_ge(o_hah, LEAD + t + 1)
                        v.tensor_tensor(ha[LR:2 * LR, :], pa[LR:2 * LR, :], ha[LR:2 * LR, :], ALU.subtract
                                        ).then_inc(o_hal, 1)
                        v.wait_ge(o_pd, LEAD + t + 1)
                        v.wait_ge(o_out, LEAD + t)
                        v.tensor_tensor(f1[:, :], pd[:, :, :].rearrange(flat), dscale[:, :], ALU.mult
                                        ).then_inc(o_f, 1)
                        v.wait_ge(o_l, LEAD + t + 1)
                        v.wait_ge(o_f, LEAD + t * 2 + 1)
                        v.tensor_tensor(f1[:, :], f1[:, :], f2[:, :], ALU.add).then_inc(o_f, 1)
                        v.wait_ge(o_e, LEAD + t + 1)
                        v.scalar_tensor_tensor(f1[:, :], f2[:, :], 1.0, f1[:, :], ALU.add, ALU.mult).then_inc(o_m, 1)
                        v.wait_ge(o_m, LEAD + t * 2 + 1)
                        if made:
                            v.wait_ge(o_s, LEAD + t * 16 + 16 - MADE * 16)
                            v.tensor_tensor(f1[:, :], so[:, :], f1[:, :], ALU.mult).then_inc(o_m, 1)
                        else:
                            v.wait_ge(o_po, LEAD + t + 1)
                            v.scalar_tensor_tensor(f1[:, :], po[:, :, :].rearrange(flat), 1.0 / WS, f1[:, :],
                                                   ALU.mult, ALU.mult).then_inc(o_m, 1)
                        v.wait_ge(o_m, LEAD + t * 2 + 2)
                        v.wait_ge(o_x, LEAD + t * 16 + 16)
                        v.tensor_tensor(xr[:, :], xr[:, :], f1[:, :], ALU.add).then_inc(o_out, 1)

                    with v.Fori(0, MADE) as t:
                        turn(t, False)
                    with v.Fori(MADE, TT) as t:
                        turn(t, True)

                @block.tensor
                def _(pe):
                    def w_out(t, b, pair):
                        pe.wait_ge(o_y[b], LEAD + pair * (16 * G) + 16 * G)
                        pe.wait_ge(o_out, LEAD + t)
                        for half in range(2):
                            cols = slice(half * 512, half * 512 + 512)
                            for i in range(DT):
                                for z, (part, w) in enumerate(((0, wo_hi), (1, wo_hi), (0, wo_lo))):
                                    mm = pe.matmul(po[:, half, :], yc[:, b, i // J, i % J, part, :], w[:, i, cols],
                                                   start=(i == 0 and z == 0), stop=(i == DT - 1 and z == 2))
                        mm.then_inc(o_po, 1)

                    def turn(pair, b, made, first):
                        t = pair * 2 + b
                        if first:
                            w_out(t, b, pair)
                        pe.wait_ge(o_h[b], LEAD + pair * 32 + 32)
                        if first:
                            pe.wait_ge(o_dal, LEAD + 3)
                            pe.wait_ge(o_dbl, LEAD + 1)
                        pe.wait_ge(o_hal, LEAD + t)
                        for i in range(IT):
                            for z, (a, part) in enumerate(((da_hi, 0), (da_hi, 1), (da_lo, 0))):
                                mm = pe.matmul(pa[0:3 * LR, :], a[:, i, :], hc[:, b, i, part, :],
                                               start=(i == 0 and z == 0), stop=(i == IT - 1 and z == 2))
                        mm.then_inc(o_ha, 1)
                        pe.wait_ge(o_f, LEAD + t * 2)
                        for i in range(IT):
                            if first and i % QB == 0:
                                pe.wait_ge(o_dw, LEAD + i // QB + 1)
                            for half in range(2):
                                for part in range(2):
                                    mm = pe.matmul(pd[:, half, :], hc[:, b, i, part, :],
                                                   dw[:, i, half * 512:(half + 1) * 512],
                                                   start=(i == 0 and part == 0), stop=(i == IT - 1 and part == 1))
                        mm.then_inc(o_pd, 1)
                        pe.wait_ge(o_hal, LEAD + t + 1)
                        pe.wait_ge(o_l, LEAD + t)
                        for half in range(2):
                            mm = pe.matmul(pl[:, half, :], ha[:, :], db[:, half * 512:(half + 1) * 512],
                                           start=True, stop=True)
                        mm.then_inc(o_pl, 1)
                        if not made and not first:
                            w_out(t, b, pair)

                    turn(0, 0, False, True)
                    turn(0, 1, False, False)
                    with pe.Fori(1, MADE // 2) as pair:
                        for b in range(2):
                            turn(pair, b, False, False)
                    with pe.Fori(MADE // 2, TT // 2) as pair:
                        for b in range(2):
                            turn(pair, b, True, False)


def kernel(L0_attn_hidden_states, L0_attn_W_in, L0_attn_conv_w, L0_attn_conv_b, L0_attn_W_x, L0_attn_W_dt,
           L0_attn_b_dt, L0_attn_A_log, L0_attn_D, L0_attn_W_out, L0_ffn_gate_q, L0_ffn_gate_scale,
           L0_ffn_gate_A, L0_ffn_gate_B, L0_ffn_up_q, L0_ffn_up_scale, L0_ffn_up_A, L0_ffn_up_B,
           L0_ffn_down_q, L0_ffn_down_scale, L0_ffn_down_A, L0_ffn_down_B):
    import numpy as np
    import concourse.bacc as bacc
    from concourse.bass_utils import run_bass_kernel_spmd as run

    def arr(a):
        return np.ascontiguousarray(np.asarray(a))

    def rows(a, n):
        a = np.asarray(a)
        return np.concatenate([a, np.zeros((n - a.shape[0],) + a.shape[1:], a.dtype)])

    def qtiles(q):
        return rows(q, IPAD).reshape(IT, P, HK, P).transpose(0, 3, 2, 1).reshape(IT, P, HK * P)

    def cols(a):
        return np.asarray(a).reshape(DT, P).T

    gu = np.concatenate([qtiles(L0_ffn_gate_q), qtiles(L0_ffn_up_q)], axis=2)
    ins = dict(
        x=np.asarray(L0_attn_hidden_states).reshape(TT, P, H),
        win=rows(np.asarray(L0_attn_W_in).reshape(2 * DT, P, HK, P).transpose(0, 3, 2, 1).reshape(2 * DT, P, HK * P),
                 2 * DT + 1),
        convw=np.asarray(L0_attn_conv_w).reshape(DT, P, K).transpose(1, 0, 2),
        convb=cols(L0_attn_conv_b),
        wx=np.asarray(L0_attn_W_x).T.reshape(DT, P, S3).transpose(1, 0, 2),
        wdt=rows(np.asarray(L0_attn_W_dt).reshape(DT, P, R).transpose(0, 2, 1), DT + 1),
        bdt=cols(L0_attn_b_dt),
        alog=np.asarray(L0_attn_A_log).reshape(DT, P, N).transpose(1, 0, 2),
        dskip=cols(L0_attn_D),
        wout=np.asarray(L0_attn_W_out).T.reshape(DT, P, H),
        gu_q=rows(gu, IT + 2),
        g_scale=rows(L0_ffn_gate_scale, IPAD).reshape(IT, P).T,
        u_scale=rows(L0_ffn_up_scale, IPAD).reshape(IT, P).T,
        lr_a=np.stack([np.asarray(a).reshape(HK, P, LR).transpose(1, 0, 2) for a in (L0_ffn_gate_A, L0_ffn_up_A)]),
        g_b=rows(np.asarray(L0_ffn_gate_B).T, IPAD).T,
        u_b=rows(np.asarray(L0_ffn_up_B).T, IPAD).T,
        dq=rows(np.asarray(L0_ffn_down_q).T, IPAD).reshape(IT, P, H),
        d_scale=np.asarray(L0_ffn_down_scale),
        d_a=rows(L0_ffn_down_A, IPAD).reshape(IT, P, LR).transpose(1, 0, 2),
        d_b=np.asarray(L0_ffn_down_B),
        ident_in=np.eye(P, dtype=np.float32),
    )
    nc = bacc.Bacc("TRN2", target_bir_lowering=False, num_devices=1)
    arrays, args = {}, []
    for name, a in ins.items():
        arrays["in_" + name] = arr(a)
        args.append(nc.dram_tensor("in_" + name, a.shape, mybir.dt.from_np(a.dtype), kind="ExternalInput").ap())
    args.append(nc.dram_tensor("out_0", (TT, P, H), F32, kind="ExternalOutput").ap())
    for name, shape, dt in (("u_s", (G, C, P, J, T), F32), ("gs_s", (G, C, P, J, T), F32),
                            ("dt_s", (G, C, P, J, T), F32), ("du_s", (G, C, P, J, T), F32),
                            ("bt_s", (N, L), F32), ("h_s", (1 + IT * UNITS, P, 2, T), F16),
                            ("y_s", (C * G, P, J * 2 * T), F16), ("s_s", (TT // 2, P, H), F32)):
        args.append(nc.dram_tensor(name, shape, dt, kind="Internal").ap())
    mixer_kernel(nc, *args)
    r = run(nc, [arrays], core_ids=[0])
    return r.results[0]["out_0"].reshape(1, L, H)
```
